# Optimizing a Trainium2 kernel written in Bass

```python
import numpy as np
import jax
import jax.numpy as jnp

def _softmax(x, axis=-1):
    return jax.nn.softmax(x, axis=axis)

def _gelu(x):
    return jax.nn.gelu(x, approximate=True)

def _silu(x):
    return jax.nn.silu(x)

def _sigmoid(x):
    return jax.nn.sigmoid(x)

def _layernorm(x, axis=-1, eps=1e-05):
    m = jnp.mean(x, axis=axis, keepdims=True)
    v = jnp.var(x, axis=axis, keepdims=True)
    return (x - m) / jnp.sqrt(v + eps)

def _scatter_add(tgt, idx, src, axis=0):
    return tgt.at[idx].add(src)

def _segment_sum(src, seg, n):
    return jax.ops.segment_sum(src, seg, n)
kernel_name = 'mk_recurrent_d2_jaxref_r8_54099b'

def setup_inputs(seed: int=0):
    np.random.seed(seed)
    _w = jnp.asarray

    def _L0_attn_setup():
        import jax, jax.numpy as jnp
        import numpy as np
        B, S, D = (2, 256, 128)
        H = 16
        HD = D // H
        SCALE = HD ** (-0.5)

        def _rope_tables(seq_len, dim, dtype=jnp.float32):
            inv_freq = 1.0 / 10000.0 ** (jnp.arange(0, dim, 2, dtype=jnp.float32) / dim)
            t = jnp.arange(seq_len, dtype=jnp.float32)
            freqs = t[:, None] * inv_freq[None, :]
            return (jnp.cos(freqs).astype(dtype), jnp.sin(freqs).astype(dtype))

        def _apply_rope(x, cos, sin):
            half = x.shape[-1] // 2
            x1, x2 = (x[..., :half], x[..., half:])
            c = cos[None, None, :, :]
            s = sin[None, None, :, :]
            rx1 = x1 * c - x2 * s
            rx2 = x1 * s + x2 * c
            return jnp.concatenate([rx1, rx2], axis=-1)
        key = jax.random.key(seed)
        k1, k2, k3 = jax.random.split(key, 3)
        x = jax.random.normal(k1, (B, S, D), dtype=jnp.float32)
        w_qkv = jax.random.normal(k2, (3 * D, D), dtype=jnp.float32) * D ** (-0.5)
        w_out = jax.random.normal(k3, (D, D), dtype=jnp.float32) * D ** (-0.5)
        b_out = jnp.zeros((D,), dtype=jnp.float32)
        return {'x': x, 'w_qkv': w_qkv, 'w_out': w_out, 'b_out': b_out}
    _L0_attn_in = _L0_attn_setup()

    def _L0_ffn_setup():
        import jax, jax.numpy as jnp
        import numpy as np
        DIM = 128
        DEPTH = 2
        HEADS = 8
        DIM_HEAD = 64
        WINDOW = 64
        INNER = HEADS * DIM_HEAD
        HID = int(DIM * 4 * 2 / 3)
        B, N = (2, 1024)
        QK_SCALE = 8.0

        def shift_token(t):
            t1, t2 = jnp.split(t, 2, axis=-1)
            t2 = jnp.pad(t2, ((0, 0), (1, 0), (0, 0)))[:, :-1]
            return jnp.concatenate([t1, t2], axis=-1)

        def l2norm(t):
            return t / jnp.clip(jnp.linalg.norm(t, axis=-1, keepdims=True), 1e-12)

        def rotate_half(x):
            x1, x2 = jnp.split(x, 2, axis=-1)
            return jnp.concatenate([-x2, x1], axis=-1)

        def rotary_xpos(q, k):
            n = q.shape[-2]
            half_idx = jnp.arange(0, DIM_HEAD, 2, dtype=jnp.float32)
            inv_freq = 1.0 / 10000.0 ** (half_idx / DIM_HEAD)
            t = jnp.arange(n, dtype=jnp.float32)
            freqs = t[:, None] * inv_freq[None, :]
            freqs = jnp.concatenate([freqs, freqs], axis=-1)
            base = (half_idx + 0.4 * DIM_HEAD) / (1.4 * DIM_HEAD)
            power = (t - n // 2) / float(WINDOW // 2)
            scale = base[None, :] ** power[:, None]
            scale = jnp.concatenate([scale, scale], axis=-1)
            cos, sin = (jnp.cos(freqs), jnp.sin(freqs))
            q = q * cos * scale + rotate_half(q) * sin * scale
            k = k * cos / scale + rotate_half(k) * sin / scale
            return (q, k)

        def local_attention(q, k, v):
            b, h, n, d = q.shape
            w = n // WINDOW
            bq = q.reshape(b, h, w, WINDOW, d) * QK_SCALE
            bk = k.reshape(b, h, w, WINDOW, d)
            bv = v.reshape(b, h, w, WINDOW, d)

            def look_around(t):
                p = jnp.pad(t, ((0, 0), (0, 0), (1, 0), (0, 0), (0, 0)))
                return jnp.concatenate([p[:, :, :w], p[:, :, 1:]], axis=3)
            bk, bv = (look_around(bk), look_around(bv))
            bt = jnp.arange(n).reshape(w, WINDOW)
            btp = jnp.pad(bt, ((1, 0), (0, 0)), constant_values=-1)
            btk = jnp.concatenate([btp[:w], btp[1:]], axis=1)
            sim = jnp.einsum('bhwid,bhwjd->bhwij', bq, bk)
            i = bt[:, :, None]
            j = btk[:, None, :]
            mask = (i < j) | (i > j + WINDOW) | (j == -1)
            sim = jnp.where(mask, -jnp.finfo(sim.dtype).max, sim)
            attn = jax.nn.softmax(sim, axis=-1)
            out = jnp.einsum('bhwij,bhwjd->bhwid', attn, bv)
            return out.reshape(b, h, n, d)

        def _layer(x, wqkv, qs, ksc, wo, lg, lb, w1, b1, w2, b2):
            b, n, _ = x.shape
            h = shift_token(x)
            qkv = h @ wqkv
            q, k, v = jnp.split(qkv, 3, axis=-1)
            to_heads = lambda t: t.reshape(b, n, HEADS, DIM_HEAD).transpose(0, 2, 1, 3)
            q, k, v = (to_heads(q), to_heads(k), to_heads(v))
            q = l2norm(q) * qs
            k = l2norm(k) * ksc
            q, k = rotary_xpos(q, k)
            o = local_attention(q, k, v)
            o = o.transpose(0, 2, 1, 3).reshape(b, n, INNER)
            x = x + o @ wo
            h = shift_token(x)
            mu = h.mean(-1, keepdims=True)
            var = h.var(-1, keepdims=True)
            h = (h - mu) / jnp.sqrt(var + 1e-05) * lg + lb
            h = h @ w1 + b1
            a, g = jnp.split(h, 2, axis=-1)
            h = a * jax.nn.gelu(g, approximate=False)
            x = x + h @ w2 + b2
            return x
        key = jax.random.key(seed)
        ks = jax.random.split(key, 6)
        return {'x': jax.random.normal(ks[0], (B, N, DIM), jnp.float32), 'wqkv': jax.random.normal(ks[1], (DEPTH, DIM, 3 * INNER), jnp.float32) * 0.02, 'q_scale': jnp.ones((DEPTH, DIM_HEAD), jnp.float32), 'k_scale': jnp.ones((DEPTH, DIM_HEAD), jnp.float32), 'wo': jax.random.normal(ks[2], (DEPTH, INNER, DIM), jnp.float32) * 0.02, 'ln_g': jnp.ones((DEPTH, DIM), jnp.float32), 'ln_b': jnp.zeros((DEPTH, DIM), jnp.float32), 'w1': jax.random.normal(ks[3], (DEPTH, DIM, 2 * HID), jnp.float32) * 0.02, 'b1': jnp.zeros((DEPTH, 2 * HID), jnp.float32), 'w2': jax.random.normal(ks[4], (DEPTH, HID, DIM), jnp.float32) * 0.02, 'b2': jnp.zeros((DEPTH, DIM), jnp.float32)}
    _L0_ffn_in = _L0_ffn_setup()

    def _L1_attn_setup():
        import jax, jax.numpy as jnp
        import numpy as np
        B, T = (4, 256)
        D_MODEL = 128
        N_HEADS = 8
        HEAD_DIM = 32
        KV_LRANK = 64

        def _orthogonalize_per_head(w):
            chunks = w.reshape(N_HEADS, HEAD_DIM, D_MODEL)

            def ns(m):
                A = m @ m.T
                Bm = 1.5 * jnp.eye(HEAD_DIM, dtype=m.dtype) - 0.5 * A
                return Bm @ m
            return jax.vmap(ns)(chunks).reshape(w.shape)
        key = jax.random.key(seed)
        ks = jax.random.split(key, 6)

        def lin(k, out_dim, in_dim):
            bound = 1.0 / np.sqrt(in_dim)
            return jax.random.uniform(k, (out_dim, in_dim), jnp.float32, -bound, bound)
        Wq = _orthogonalize_per_head(lin(ks[0], N_HEADS * HEAD_DIM, D_MODEL))
        return {'x': jax.random.normal(ks[1], (B, T, D_MODEL), jnp.float32), 'Wq': Wq, 'Wkv_down': lin(ks[2], KV_LRANK, D_MODEL), 'Wk_up': lin(ks[3], N_HEADS * HEAD_DIM, KV_LRANK), 'Wv_up': lin(ks[4], N_HEADS * HEAD_DIM, KV_LRANK), 'Wo': lin(ks[5], D_MODEL, N_HEADS * HEAD_DIM)}
    _L1_attn_in = _L1_attn_setup()

    def _L1_ffn_setup():
        import jax, jax.numpy as jnp
        import numpy as np
        HIDDEN = 128
        FF = 512
        N_EXPERTS = 8
        CAP_FACTOR = 1.0
        B, S = (4, 256)
        STD = 0.02

        def _gelu(x):
            return x * 0.5 * (1.0 + jax.lax.erf(x / 1.41421))
        key = jax.random.key(seed)
        ks = jax.random.split(key, 6)
        x = jax.random.normal(ks[0], (B, S, HIDDEN), dtype=jnp.float32)
        W_sw = jax.random.normal(ks[1], (HIDDEN, N_EXPERTS), dtype=jnp.float32) * STD
        b_sw = jnp.zeros((N_EXPERTS,), dtype=jnp.float32)
        W1 = jax.random.normal(ks[2], (N_EXPERTS, HIDDEN, FF), dtype=jnp.float32) * STD
        b1 = jnp.zeros((N_EXPERTS, FF), dtype=jnp.float32)
        W2 = jax.random.normal(ks[3], (N_EXPERTS, FF, HIDDEN), dtype=jnp.float32) * STD
        b2 = jnp.zeros((N_EXPERTS, HIDDEN), dtype=jnp.float32)
        return {'x': x, 'W_sw': W_sw, 'b_sw': b_sw, 'W1': W1, 'b1': b1, 'W2': W2, 'b2': b2}
    _L1_ffn_in = _L1_ffn_setup()
    _d = {'L0_attn_x': _L0_attn_in['x'], 'L0_attn_w_qkv': _L0_attn_in['w_qkv'], 'L0_attn_w_out': _L0_attn_in['w_out'], 'L0_attn_b_out': _L0_attn_in['b_out'], 'L0_ffn_wqkv': _L0_ffn_in['wqkv'], 'L0_ffn_q_scale': _L0_ffn_in['q_scale'], 'L0_ffn_k_scale': _L0_ffn_in['k_scale'], 'L0_ffn_wo': _L0_ffn_in['wo'], 'L0_ffn_ln_g': _L0_ffn_in['ln_g'], 'L0_ffn_ln_b': _L0_ffn_in['ln_b'], 'L0_ffn_w1': _L0_ffn_in['w1'], 'L0_ffn_b1': _L0_ffn_in['b1'], 'L0_ffn_w2': _L0_ffn_in['w2'], 'L0_ffn_b2': _L0_ffn_in['b2'], 'L1_attn_Wq': _L1_attn_in['Wq'], 'L1_attn_Wkv_down': _L1_attn_in['Wkv_down'], 'L1_attn_Wk_up': _L1_attn_in['Wk_up'], 'L1_attn_Wv_up': _L1_attn_in['Wv_up'], 'L1_attn_Wo': _L1_attn_in['Wo'], 'L1_ffn_W_sw': _L1_ffn_in['W_sw'], 'L1_ffn_b_sw': _L1_ffn_in['b_sw'], 'L1_ffn_W1': _L1_ffn_in['W1'], 'L1_ffn_b1': _L1_ffn_in['b1'], 'L1_ffn_W2': _L1_ffn_in['W2'], 'L1_ffn_b2': _L1_ffn_in['b2']}
    _x0 = _d['L0_attn_x']
    _d['L0_attn_x'] = jax.random.normal(jax.random.fold_in(jax.random.key(seed), 1), (4, 1024, 128), dtype=_x0.dtype)
    del _x0
    return _d

def reference(L0_attn_x, L0_attn_w_qkv, L0_attn_w_out, L0_attn_b_out, L0_ffn_wqkv, L0_ffn_q_scale, L0_ffn_k_scale, L0_ffn_wo, L0_ffn_ln_g, L0_ffn_ln_b, L0_ffn_w1, L0_ffn_b1, L0_ffn_w2, L0_ffn_b2, L1_attn_Wq, L1_attn_Wkv_down, L1_attn_Wk_up, L1_attn_Wv_up, L1_attn_Wo, L1_ffn_W_sw, L1_ffn_b_sw, L1_ffn_W1, L1_ffn_b1, L1_ffn_W2, L1_ffn_b2):

    def _L0_attn_ref(x, w_qkv, w_out, b_out):
        import jax, jax.numpy as jnp
        import numpy as np
        B, S, D = (2, 256, 128)
        H = 16
        HD = D // H
        SCALE = HD ** (-0.5)

        def _rope_tables(seq_len, dim, dtype=jnp.float32):
            inv_freq = 1.0 / 10000.0 ** (jnp.arange(0, dim, 2, dtype=jnp.float32) / dim)
            t = jnp.arange(seq_len, dtype=jnp.float32)
            freqs = t[:, None] * inv_freq[None, :]
            return (jnp.cos(freqs).astype(dtype), jnp.sin(freqs).astype(dtype))

        def _apply_rope(x, cos, sin):
            half = x.shape[-1] // 2
            x1, x2 = (x[..., :half], x[..., half:])
            c = cos[None, None, :, :]
            s = sin[None, None, :, :]
            rx1 = x1 * c - x2 * s
            rx2 = x1 * s + x2 * c
            return jnp.concatenate([rx1, rx2], axis=-1)
        b, s, d = x.shape
        qkv = jnp.einsum('bsd,ed->bse', x, w_qkv)
        qkv = qkv.reshape(b, s, 3, H, HD).transpose(2, 0, 3, 1, 4)
        q, k, v = (qkv[0], qkv[1], qkv[2])
        cos, sin = _rope_tables(s, HD, x.dtype)
        q = _apply_rope(q, cos, sin)
        k = _apply_rope(k, cos, sin)
        scores = jnp.einsum('bhsd,bhtd->bhst', q, k) * SCALE
        attn = jax.nn.softmax(scores, axis=-1)
        out = jnp.einsum('bhst,bhtd->bhsd', attn, v)
        out = out.transpose(0, 2, 1, 3).reshape(b, s, d)
        return jnp.einsum('bsd,ed->bse', out, w_out) + b_out

    def _L0_ffn_ref(x, wqkv, q_scale, k_scale, wo, ln_g, ln_b, w1, b1, w2, b2):
        import jax, jax.numpy as jnp
        import numpy as np
        DIM = 128
        DEPTH = 2
        HEADS = 8
        DIM_HEAD = 64
        WINDOW = 64
        INNER = HEADS * DIM_HEAD
        HID = int(DIM * 4 * 2 / 3)
        B, N = (2, 1024)
        QK_SCALE = 8.0

        def shift_token(t):
            t1, t2 = jnp.split(t, 2, axis=-1)
            t2 = jnp.pad(t2, ((0, 0), (1, 0), (0, 0)))[:, :-1]
            return jnp.concatenate([t1, t2], axis=-1)

        def l2norm(t):
            return t / jnp.clip(jnp.linalg.norm(t, axis=-1, keepdims=True), 1e-12)

        def rotate_half(x):
            x1, x2 = jnp.split(x, 2, axis=-1)
            return jnp.concatenate([-x2, x1], axis=-1)

        def rotary_xpos(q, k):
            n = q.shape[-2]
            half_idx = jnp.arange(0, DIM_HEAD, 2, dtype=jnp.float32)
            inv_freq = 1.0 / 10000.0 ** (half_idx / DIM_HEAD)
            t = jnp.arange(n, dtype=jnp.float32)
            freqs = t[:, None] * inv_freq[None, :]
            freqs = jnp.concatenate([freqs, freqs], axis=-1)
            base = (half_idx + 0.4 * DIM_HEAD) / (1.4 * DIM_HEAD)
            power = (t - n // 2) / float(WINDOW // 2)
            scale = base[None, :] ** power[:, None]
            scale = jnp.concatenate([scale, scale], axis=-1)
            cos, sin = (jnp.cos(freqs), jnp.sin(freqs))
            q = q * cos * scale + rotate_half(q) * sin * scale
            k = k * cos / scale + rotate_half(k) * sin / scale
            return (q, k)

        def local_attention(q, k, v):
            b, h, n, d = q.shape
            w = n // WINDOW
            bq = q.reshape(b, h, w, WINDOW, d) * QK_SCALE
            bk = k.reshape(b, h, w, WINDOW, d)
            bv = v.reshape(b, h, w, WINDOW, d)

            def look_around(t):
                p = jnp.pad(t, ((0, 0), (0, 0), (1, 0), (0, 0), (0, 0)))
                return jnp.concatenate([p[:, :, :w], p[:, :, 1:]], axis=3)
            bk, bv = (look_around(bk), look_around(bv))
            bt = jnp.arange(n).reshape(w, WINDOW)
            btp = jnp.pad(bt, ((1, 0), (0, 0)), constant_values=-1)
            btk = jnp.concatenate([btp[:w], btp[1:]], axis=1)
            sim = jnp.einsum('bhwid,bhwjd->bhwij', bq, bk)
            i = bt[:, :, None]
            j = btk[:, None, :]
            mask = (i < j) | (i > j + WINDOW) | (j == -1)
            sim = jnp.where(mask, -jnp.finfo(sim.dtype).max, sim)
            attn = jax.nn.softmax(sim, axis=-1)
            out = jnp.einsum('bhwij,bhwjd->bhwid', attn, bv)
            return out.reshape(b, h, n, d)

        def _layer(x, wqkv, qs, ksc, wo, lg, lb, w1, b1, w2, b2):
            b, n, _ = x.shape
            h = shift_token(x)
            qkv = h @ wqkv
            q, k, v = jnp.split(qkv, 3, axis=-1)
            to_heads = lambda t: t.reshape(b, n, HEADS, DIM_HEAD).transpose(0, 2, 1, 3)
            q, k, v = (to_heads(q), to_heads(k), to_heads(v))
            q = l2norm(q) * qs
            k = l2norm(k) * ksc
            q, k = rotary_xpos(q, k)
            o = local_attention(q, k, v)
            o = o.transpose(0, 2, 1, 3).reshape(b, n, INNER)
            x = x + o @ wo
            h = shift_token(x)
            mu = h.mean(-1, keepdims=True)
            var = h.var(-1, keepdims=True)
            h = (h - mu) / jnp.sqrt(var + 1e-05) * lg + lb
            h = h @ w1 + b1
            a, g = jnp.split(h, 2, axis=-1)
            h = a * jax.nn.gelu(g, approximate=False)
            x = x + h @ w2 + b2
            return x
        for l in range(DEPTH):
            x = _layer(x, wqkv[l], q_scale[l], k_scale[l], wo[l], ln_g[l], ln_b[l], w1[l], b1[l], w2[l], b2[l])
        return x

    def _L1_attn_ref(x, Wq, Wkv_down, Wk_up, Wv_up, Wo):
        import jax, jax.numpy as jnp
        import numpy as np
        B, T = (4, 256)
        D_MODEL = 128
        N_HEADS = 8
        HEAD_DIM = 32
        KV_LRANK = 64

        def _orthogonalize_per_head(w):
            chunks = w.reshape(N_HEADS, HEAD_DIM, D_MODEL)

            def ns(m):
                A = m @ m.T
                Bm = 1.5 * jnp.eye(HEAD_DIM, dtype=m.dtype) - 0.5 * A
                return Bm @ m
            return jax.vmap(ns)(chunks).reshape(w.shape)
        b, t, _ = x.shape
        q = (x @ Wq.T).reshape(b, t, N_HEADS, HEAD_DIM)
        kv_latent = x @ Wkv_down.T
        k = (kv_latent @ Wk_up.T).reshape(b, t, N_HEADS, HEAD_DIM)
        v = (kv_latent @ Wv_up.T).reshape(b, t, N_HEADS, HEAD_DIM)
        scale = HEAD_DIM ** (-0.5)
        scores = jnp.einsum('bqhd,bkhd->bhqk', q, k) * scale
        attn = jax.nn.softmax(scores, axis=-1)
        out = jnp.einsum('bhqk,bkhd->bqhd', attn, v)
        out = out.reshape(b, t, N_HEADS * HEAD_DIM)
        return out @ Wo.T

    def _L1_ffn_ref(x, W_sw, b_sw, W1, b1, W2, b2):
        import jax, jax.numpy as jnp
        import numpy as np
        HIDDEN = 128
        FF = 512
        N_EXPERTS = 8
        CAP_FACTOR = 1.0
        B, S = (4, 256)
        STD = 0.02

        def _gelu(x):
            return x * 0.5 * (1.0 + jax.lax.erf(x / 1.41421))
        Bb, Ss, D = x.shape
        T = Bb * Ss
        E = W1.shape[0]
        capacity = int(CAP_FACTOR * T / E)
        xf = x.reshape(T, D)
        logits = xf @ W_sw + b_sw
        probs = jax.nn.softmax(logits, axis=-1)
        pmax = jnp.max(probs, axis=-1)
        routes = jnp.argmax(probs, axis=-1)
        factor = pmax / jax.lax.stop_gradient(pmax)
        xs = xf * factor[:, None]
        onehot = jax.nn.one_hot(routes, E, dtype=jnp.int32)
        pos = jnp.cumsum(onehot, axis=0) - 1
        pos_tok = jnp.take_along_axis(pos, routes[:, None], axis=1)[:, 0]
        keep = pos_tok < capacity
        pos_safe = jnp.where(keep, pos_tok, capacity)
        buf = jnp.zeros((E, capacity + 1, D), dtype=xs.dtype)
        buf = buf.at[routes, pos_safe].set(xs)
        buf = buf[:, :capacity]
        h = _gelu(jnp.einsum('ecd,edf->ecf', buf, W1) + b1[:, None, :])
        expert_out = jnp.einsum('ecf,efd->ecd', h, W2) + b2[:, None, :]
        gathered = expert_out[routes, jnp.minimum(pos_tok, capacity - 1)]
        final = jnp.where(keep[:, None], gathered, xs)
        return final.reshape(Bb, Ss, D)
    x = L0_attn_x
    xn = _layernorm(x, axis=-1)
    s = _L0_attn_ref(xn, L0_attn_w_qkv, L0_attn_w_out, L0_attn_b_out)
    g = _silu(_L0_ffn_ref(xn, L0_ffn_wqkv, L0_ffn_q_scale, L0_ffn_k_scale, L0_ffn_wo, L0_ffn_ln_g, L0_ffn_ln_b, L0_ffn_w1, L0_ffn_b1, L0_ffn_w2, L0_ffn_b2))
    x = x + s * g
    xn = _layernorm(x, axis=-1)
    s = _L1_attn_ref(xn, L1_attn_Wq, L1_attn_Wkv_down, L1_attn_Wk_up, L1_attn_Wv_up, L1_attn_Wo)
    g = _silu(_L1_ffn_ref(xn, L1_ffn_W_sw, L1_ffn_b_sw, L1_ffn_W1, L1_ffn_b1, L1_ffn_W2, L1_ffn_b2))
    x = x + s * g
    return x

_drawn_inputs = setup_inputs


def setup_inputs(seed=0):
    import zlib

    import numpy as np

    out = dict(_drawn_inputs(seed))
    spreads = {'L0_attn_b_out': (0.0, 0.1),
     'L0_ffn_q_scale': (1.0, 0.6),
     'L0_ffn_k_scale': (1.0, 0.6),
     'L0_ffn_ln_g': (1.0, 0.6),
     'L0_ffn_ln_b': (0.0, 0.8),
     'L0_ffn_b1': (0.0, 0.8),
     'L0_ffn_b2': (0.0, 0.414),
     'L1_ffn_b_sw': (0.0, 0.8),
     'L1_ffn_b1': (0.0, 0.8),
     'L1_ffn_b2': (0.0, 0.8)}
    factors = {'L0_ffn_wqkv': 8.0,
     'L0_ffn_wo': 8.0,
     'L0_ffn_w1': 8.0,
     'L0_ffn_w2': 8.0,
     'L1_attn_Wq': 8.0,
     'L1_attn_Wkv_down': 8.0,
     'L1_attn_Wk_up': 8.0,
     'L1_attn_Wv_up': 8.0,
     'L1_attn_Wo': 8.0,
     'L1_ffn_W_sw': 8.0,
     'L1_ffn_W1': 8.0,
     'L1_ffn_W2': 8.0}
    for name, (base, spread) in spreads.items():
        noise = np.random.default_rng([zlib.crc32(name.encode()), seed]).standard_normal(out[name].shape)
        drawn = base * np.exp(spread * noise) if base else spread * noise
        out[name] = jnp.asarray(drawn.astype(out[name].dtype))
    for name, factor in factors.items():
        out[name] = (out[name] * factor).astype(out[name].dtype)
    return out
```

```python
from contextlib import ExitStack

import numpy as np
import concourse.bass as bass
from concourse import mybir

F32 = mybir.dt.float32
BF16 = mybir.dt.bfloat16
U32 = mybir.dt.uint32
ALU = mybir.AluOpType
ACT = mybir.ActivationFunctionType
AX = mybir.AxisListType

P = 128
B, N, D = 4, 1024, 128
TB = N // P
TILES = B * TB
CT = 4
CW = CT * P
EPS = 1e-5
UNITS = 16
UR = D // 4


class Arena:

    def __init__(self, tensor, words):
        self.tensor, self.words, self.at = tensor, words, 0

    def take(self, words):
        piece = self.tensor[:, self.at:self.at + words]
        self.at += words + words % 2
        assert self.at <= self.words, f"the SBUF arena is full: {self.at}"
        return piece

    def f32(self, *shape):
        return split(self.take(int(np.prod(shape))), shape)

    def bf16(self, *shape):
        n = int(np.prod(shape))
        return split(self.take((n + 1) // 2).bitcast(BF16)[:, 0:n], shape)


class Banks:

    def __init__(self, tensor):
        self.tensor = tensor

    def __getitem__(self, n):
        return self.tensor[:, CW * n:CW * (n + 1)]

    def run(self, n, count):
        return self.tensor[:, CW * n:CW * (n + count)]


def split(piece, shape):
    if len(shape) == 1:
        return piece
    names = "abcd"[:len(shape)]
    return piece.rearrange(f"p ({' '.join(names)}) -> p {' '.join(names)}", **dict(zip(names[1:], shape[1:])))


class Chain:

    def __init__(self, eng, sem):
        self.eng, self.sem, self.base, self.n = eng, sem, 0, 0

    def step(self, ins):
        self.n += 1
        ins.then_inc(self.sem, 1)
        self.eng.wait_ge(self.sem, self.base + self.n)

    def loop(self, turn, per_turn, before):
        self.base, self.n = before + turn * per_turn, 0



def attention_phase(nc, sem, arena, bank, identb, identf, name, heads, hd, qk_parts, v_rows, out_rows):
    M = P // heads
    sets = 4 // heads
    if sets == 1:
        q_blocks, k_blocks = [[0, 1, 2, 0, 1, 0]], [[0, 0, 0, 1, 1, 2]]
    else:
        q_blocks, k_blocks = [[0, 1, 0], [1, 2, 0]], [[0, 0, 1], [1, 0, 2]]
    KP = 96
    MR = 3
    NL = 2 * sum(len(b) for b in q_blocks) + 1
    scale = float(hd) ** -0.5
    NT = heads * TB
    JOBS = 2 * NT + 1 + 2
    FIRST = 2 * NT + 1
    GROUPS = 2 * TB
    STEPS = GROUPS * heads
    BEGIN, END = heads + 1, STEPS - 5
    RING = 2 * heads

    mark = arena.at
    Q = [arena.bf16(sets, heads, N) for _ in range(2)]
    K = [arena.bf16(sets, heads, N) for _ in range(2)]
    V = [arena.f32(TB, P) for _ in range(2)]
    probs = arena.f32(RING, CW)
    halfmax = arena.f32(NT, 2)
    negmax = arena.f32(NT)
    rest = arena.f32(2, NT)
    maxall = arena.bf16(P)
    maxparts = maxall[:, 0:MR * NT].rearrange("p (m n) -> p m n", m=MR)
    maxrows = arena.bf16(P)
    accs = arena.f32(N)
    rden = arena.f32(2, CT * heads)

    s_cleared = sem(name + "_cleared")
    s_load = [sem(f"{name}_load{i}") for i in range(2)]
    s_rows = [sem(f"{name}_rows{i}") for i in range(2)]
    s_job = sem(name + "_job")
    s_jobdone = sem(name + "_jobdone")
    s_parts = sem(name + "_parts")
    s_st = sem(name + "_st")
    s_exp = sem(name + "_exp")
    s_pv = sem(name + "_pv")
    s_acc = sem(name + "_acc")
    s_chain = sem(name + "_chain")

    def sbank(n):
        return bank[n % 3]

    def stbank(n):
        return bank[3 + n % 3]

    acc = [bank[6], bank[7]]

    def turn_free(eng, done, base, n, before):
        if n >= 3:
            eng.wait_ge(done, base + (n - 2))
        elif before:
            eng.wait_ge(done, base + (1 - before + max(j for j in range(before) if j % 3 == n)))
    LINKS = 6
    OLINKS = 1

    def jobs_before(u):
        return u * JOBS + FIRST

    def jobs_by(step):
        return min(max(step + 1 - BEGIN, 0), END - BEGIN) * 2 * NT // (END - BEGIN)

    with nc.Block() as block:

        @block.gpsimd
        def _(pool):
            nc.gpsimd.memset(maxall, 0.0).then_inc(s_cleared, 1)
            n = 1
            for s in range(2):
                for rows, value in ((Q[s], 0.0), (K[s][0:KP], 0.0), (K[s][KP:P], 1.0)):
                    nc.gpsimd.memset(rows, value).then_inc(s_cleared, 1)
                    n += 1
                    pool.wait_ge(s_cleared, n)

        @block.sync
        def _(sp):
            def load(u, s):
                for which, (stack, blocks) in enumerate(((Q[s], q_blocks), (K[s], k_blocks))):
                    for st in range(sets):
                        for i, part in enumerate(blocks[st]):
                            src = qk_parts[bass.ds(u, 1), 3 * which + part, :, :].rearrange(
                                "a (h d) t -> (a d) h t", d=hd)
                            sp.dma_start(stack[hd * i:hd * (i + 1), st, :, :], src).then_inc(s_load[s], 16)

            def load_values(u, s):
                sp.dma_start(V[s], v_rows[bass.ds(u, 1), :, :, :].rearrange("a p c m -> (a p) c m"))\
                    .then_inc(s_load[s], 16)

            def rows(u, s):
                sp.wait_ge(s_jobdone, jobs_before(u) - (0 if isinstance(u, int) and u == 0 else 2))
                for m in range(MR):
                    sp.dma_start(Q[s][KP + m:KP + m + 1, sets - 1, :, :].rearrange("p h (t q) -> p (h t) q", q=P),
                                 maxrows[NT * m:NT * (m + 1), :]).then_inc(s_rows[s], 16)

            def unit(u, s):
                sp.wait_ge(s_exp, u * STEPS)
                load(u + 1, 1 - s)
                sp.wait_ge(s_pv, u * GROUPS)
                load_values(u + 1, 1 - s)
                rows(u + 1, 1 - s)

            sp.wait_ge(s_cleared, 7)
            load(0, 0)
            load_values(0, 0)
            rows(0, 0)
            with sp.Fori(0, UNITS // 2 - 1) as i:
                unit(2 * i, 0)
                unit(2 * i + 1, 1)
            unit(UNITS - 2, 0)

        @block.tensor
        def _(pe):
            def loaded(u, s):
                pe.wait_ge(s_load[s], 16 * NL * ((u - s) // 2 + 1) if isinstance(u, int) else (u - s) * (8 * NL) + 16 * NL)

            def max_scores(s, base, before, first, last):
                for k in range(first, last):
                    h, t, half = k // (2 * TB), k // 2 % TB, k % 2
                    turn_free(pe, s_jobdone, base, k, before)
                    nc.tensor.matmul(sbank(k), Q[s][0:KP, 0, h, P * t:P * (t + 1)],
                                     K[s][0:KP, 0, h, CW * half:CW * (half + 1)],
                                     start=True, stop=True).then_inc(s_job, 1)

            def max_transpose(u, base, n):
                pe.wait_ge(s_parts, u + 1)
                turn_free(pe, s_jobdone, base, n, 0)
                nc.tensor.transpose(sbank(n)[:, 0:P // 2].bitcast(BF16), maxall, identb).then_inc(s_job, 1)

            def shifted_scores(u, s, step):
                c, half, h = step // (2 * heads), step // heads % 2, step % heads
                turn_free(pe, s_exp, STEPS * u, step, 0 if isinstance(u, int) and u == 0 else STEPS)
                for st in range(sets):
                    rows = KP + MR if st == sets - 1 else KP
                    last = nc.tensor.matmul(stbank(step), K[s][0:rows, st, h, P * c:P * (c + 1)],
                                            Q[s][0:rows, st, h, CW * half:CW * (half + 1)],
                                            start=(st == 0), stop=(st == sets - 1))
                last.then_inc(s_st, 1)

            def values(u, s, g, before):
                c, half = divmod(g, 2)
                pe.wait_ge(s_exp, STEPS * u + heads * (g + 1))
                if c == 0 and before > FIRST:
                    pe.wait_ge(s_acc, 2 * u + half - 1)
                for h in range(heads):
                    last = nc.tensor.matmul(acc[half][M * h:M * (h + 1), :], V[s][:, c, M * h:M * (h + 1)],
                                            probs[:, (heads * g + h) % RING, :],
                                            start=(c == 0), stop=(c == TB - 1), tile_position=(0, M * h))
                last.then_inc(s_pv, 1)

            def outputs(u, base, n, before):
                for g in range(2):
                    pe.wait_ge(s_acc, 2 * u + g + 1)
                    turn_free(pe, s_jobdone, base, n + g, before)
                    for t in range(CT):
                        last = nc.tensor.transpose(sbank(n + g)[:, P * t:P * (t + 1)],
                                                   accs[:, CW * g + P * t:CW * g + P * (t + 1)], identf)
                    last.then_inc(s_job, 1)

            def unit(u, s, following, before):
                base = jobs_before(u)
                pe.wait_ge(s_rows[s], 16 * MR * (u // 2 + 1) if isinstance(u, int) else (u - s) * (8 * MR) + 16 * MR)
                for step in range(STEPS):
                    shifted_scores(u, s, step)
                    if following:
                        if step == BEGIN:
                            loaded(u + 1, 1 - s)
                        max_scores(1 - s, base, before, jobs_by(step - 1), jobs_by(step))
                    if step >= heads and step % heads == heads - 1:
                        values(u, s, step // heads - 1, before)
                if following:
                    max_transpose(u + 1, base, 2 * NT)
                values(u, s, GROUPS - 1, before)
                outputs(u, base, 2 * NT + 1 if following else 0, before)

            loaded(0, 0)
            max_scores(0, 0, 0, 0, 2 * NT)
            max_transpose(0, 0, 2 * NT)
            unit(0, 0, True, FIRST)
            with pe.Fori(0, UNITS // 2 - 1) as i:
                unit(2 * i + 1, 1, True, JOBS)
                unit(2 * i + 2, 0, True, JOBS)
            unit(UNITS - 1, 1, False, JOBS)

        @block.scalar
        def _(act):
            def unit(u, s, first):
                for n in range(STEPS):
                    act.wait_ge(s_st, STEPS * u + n + 1)
                    if n >= RING or not first:
                        act.wait_ge(s_pv, GROUPS * u + n // heads - 1)
                    nc.scalar.activation(probs[:, n % RING, :], stbank(n), ACT.Exp, scale=scale).then_inc(s_exp, 1)
                if not first:
                    act.wait_ge(s_job, jobs_before(u))
                for half in range(2):
                    act.wait_ge(s_pv, GROUPS * (u + 1) - 1 + half)
                    nc.scalar.activation(accs[:, CW * half:CW * (half + 1)], acc[half], ACT.Copy).then_inc(s_acc, 1)

            unit(0, 0, True)
            with act.Fori(0, UNITS // 2 - 1) as i:
                unit(2 * i + 1, 1, False)
                unit(2 * i + 2, 0, False)
            unit(UNITS - 1, 1, False)

        @block.vector
        def _(dve):
            chain = Chain(dve, s_chain)
            dve.wait_ge(s_cleared, 1)

            def job(base, n):
                dve.wait_ge(s_job, base + n + 1)

            def maxima(base):
                for k in range(NT):
                    for half in range(2):
                        n = 2 * k + half
                        job(base, n)
                        nc.vector.tensor_reduce(halfmax[:, k, half:half + 1], sbank(n), AX.X, ALU.max)\
                            .then_inc(s_jobdone, 1)
                dve.wait_ge(s_jobdone, base + 2 * NT)
                chain.step(nc.vector.tensor_tensor(negmax, halfmax[:, :, 0], halfmax[:, :, 1], ALU.max))
                chain.step(nc.vector.tensor_scalar(negmax, negmax, -1.0, None, ALU.mult))
                chain.step(nc.vector.tensor_copy(maxparts[:, 0, :], negmax))
                chain.step(nc.vector.tensor_tensor(rest[:, 0, :], negmax, maxparts[:, 0, :], ALU.subtract))
                chain.step(nc.vector.tensor_copy(maxparts[:, 1, :], rest[:, 0, :]))
                chain.step(nc.vector.tensor_tensor(rest[:, 1, :], rest[:, 0, :], maxparts[:, 1, :], ALU.subtract))
                nc.vector.tensor_copy(maxparts[:, 2, :], rest[:, 1, :]).then_inc(s_parts, 1)

            def after_maxima(u, s, base, n):
                job(base, n)
                if not isinstance(u, int) or u:
                    o = 1 - s
                    dve.wait_ge(s_rows[o], 16 * MR * ((u - 1) // 2 + 1) if isinstance(u, int)
                                else (u - 1 - o) * (8 * MR) + 16 * MR)
                nc.vector.tensor_copy(maxrows, sbank(n)[:, 0:P // 2].bitcast(BF16))\
                    .then_inc(s_jobdone, 1)

            def outputs(u, base, n):
                for g in range(2):
                    job(base, n + g)
                    out = sbank(n + g).rearrange("p (t h m) -> p t h m", t=CT, h=heads)
                    rd = rden[:, g, :].rearrange("p (t h) -> p t h", t=CT)
                    chain.step(nc.vector.reciprocal(rd, out[:, :, :, hd]))
                    dst = out_rows[:, bass.ds(u, 1), CT * g:CT * (g + 1), :]
                    nc.vector.tensor_tensor(
                        dst.rearrange("p a t (h d) -> p (a t) h d", d=hd), out[:, :, :, 0:hd],
                        rd.unsqueeze(3).broadcast_to([P, CT, heads, hd]), ALU.mult).then_inc(s_jobdone, 1)

            def unit(u, s, following):
                base = jobs_before(u)
                if following:
                    maxima(base)
                    after_maxima(u + 1, 1 - s, base, 2 * NT)
                outputs(u, base, 2 * NT + 1 if following else 0)

            maxima(0)
            after_maxima(0, 0, 0, 2 * NT)
            per = 2 * OLINKS + LINKS
            with dve.Fori(0, UNITS // 2 - 1) as i:
                chain.loop(2 * i, per, LINKS)
                unit(2 * i, 0, True)
                chain.loop(2 * i + 1, per, LINKS)
                unit(2 * i + 1, 1, True)
            chain.loop(UNITS - 2, per, LINKS)
            unit(UNITS - 2, 0, True)
            unit(UNITS - 1, 1, False)
    arena.at = mark



LN_STEPS = 7


def layernorm(nc, dve, chain, x, out, w, std_wait, std_signal, out_sem, eps=EPS):
    for t in range(CT):
        ins = nc.vector.bn_stats(w.stats[:, t, :], x[:, t, :])
        if t < CT - 1:
            ins.then_inc(w.stat_sem, 1)
    chain.step(ins)
    chain.eng.wait_ge(w.stat_sem, w.stat_count())
    even, odd = w.stats[:, :, 1:3], w.stats[:, :, 4:6]
    chain.step(nc.vector.tensor_tensor(w.both, even, odd, ALU.add))
    chain.step(nc.vector.tensor_tensor(w.diff, w.stats[:, :, 1], w.stats[:, :, 4], ALU.subtract))
    chain.step(nc.vector.tensor_tensor(w.diff2, w.diff, w.diff, ALU.mult))
    chain.step(nc.vector.tensor_scalar(w.var, w.both[:, :, 1], 1.0 / D, eps, ALU.mult, ALU.add))
    nc.vector.scalar_tensor_tensor(w.vareps, w.diff2, 0.25, w.var, ALU.mult, ALU.add).then_inc(std_signal, 1)
    chain.step(nc.vector.tensor_scalar(w.mean, w.both[:, :, 0], 0.5, None, ALU.mult))
    std_wait()
    if w.invert is not None:
        chain.step(w.invert())
    for t in range(CT):
        ins = nc.vector.tensor_scalar(out[:, t, :], x[:, t, :], w.mean[:, t:t + 1], w.rstd[:, t:t + 1],
                                      ALU.subtract, ALU.mult)
        ins.then_inc(out_sem, 1)


class NormBuffers:
    def __init__(self, nc, arena, stat_sem):
        self.stats, self.both = arena.f32(CT, 6), arena.f32(CT, 2)
        self.diff, self.diff2, self.var = arena.f32(CT), arena.f32(CT), arena.f32(CT)
        self.vareps, self.mean, self.std, self.rstd = arena.f32(CT), arena.f32(CT), arena.f32(CT), arena.f32(CT)
        self.stat_sem = stat_sem
        self.invert = lambda: nc.vector.reciprocal(self.rstd, self.std)



def enter_phase(nc, sem, arena, bank, identf, x, weights, ropes, xn_out, qk_parts, v_rows):
    mark = arena.at
    w_all = arena.f32(5, D)
    cos, sin = arena.f32(N), arena.f32(N)
    xs = [arena.f32(CT, D) for _ in range(2)]
    xn = [arena.f32(CT, D) for _ in range(2)]
    xt = [arena.f32(CW) for _ in range(2)]
    t1, t2, rot = arena.f32(2, CW), arena.f32(2, CW), arena.f32(2, CW)
    rest = arena.f32(2, CW)
    parts = [arena.bf16(2, 3, CW) for _ in range(2)]
    vrow = [arena.f32(CT, 16, 32) for _ in range(2)]
    zero = arena.f32(D)
    s_stat = sem("e_stat")
    w = NormBuffers(nc, arena, s_stat)

    s_const = sem("e_const")
    s_x = [sem(f"e_x{i}") for i in range(2)]
    s_zero = sem("e_zero")
    s_var, s_std = sem("e_var"), sem("e_std")
    s_xn = sem("e_xn")
    s_xnout = [sem(f"e_xnout{i}") for i in range(2)]
    s_t = sem("e_t")
    s_xt = sem("e_xt")
    s_qk = sem("e_qk")
    s_v = sem("e_v")
    s_vrow = sem("e_vrow")
    s_t12 = sem("e_t12")
    s_rot = sem("e_rot")
    s_p1, s_r1, s_p2, s_p3 = sem("e_p1"), sem("e_r1"), sem("e_p2"), sem("e_p3")
    s_out = [sem(f"e_out{i}") for i in range(2)]
    s_fill = sem("e_fill")
    s_chain = sem("e_chain")
    OUTS = 8
    CHUNKS = 2 * B

    with nc.Block() as block:

        @block.sync
        def _(sp):
            def load(b):
                for s in range(2):
                    sp.dma_start(xs[s], x[bass.ds(b, 1), CW * s:CW * (s + 1), :].rearrange(
                        "a (t p) d -> p (a t) d", p=P)).then_inc(s_x[s], 16)

            def store(b, s):
                n = 2 * b + s
                sp.wait_ge(s_xn, CT * (n + 1))
                sp.dma_start(xn_out[bass.ds(b * (N + 1) + 1 + CW * s, CW), :].rearrange("(t p) d -> p t d", p=P),
                             xn[s]).then_inc(s_xnout[s], 16)
                sp.wait_ge(s_vrow, n + 1)
                for g in range(4):
                    sp.dma_start(v_rows[bass.ds(4 * b + g, 1), :, CT * s:CT * (s + 1), :].rearrange(
                        "a p t m -> (a p) t m"),
                        vrow[s][:, :, 4 * g:4 * g + 4, :].rearrange("p t h m -> p t (h m)")).then_inc(s_out[s], 16)
                sp.wait_ge(s_p3, n + 1)
                sp.wait_ge(s_p2, n + 1)
                for g in range(4):
                    sp.dma_start(qk_parts[bass.ds(4 * b + g, 1), :, :, CW * s:CW * (s + 1)].rearrange(
                        "a n r t -> (a r) n t"),
                        parts[s][UR * g:UR * (g + 1), :, :, :].rearrange("r w n t -> r (w n) t"))\
                        .then_inc(s_out[s], 16)

            for i in range(5):
                sp.dma_start(w_all[:, i, :], weights[i]).then_inc(s_const, 16)
            sp.dma_start(cos, ropes[0]).then_inc(s_const, 16)
            sp.dma_start(sin, ropes[1]).then_inc(s_const, 16)
            load(0)
            sp.wait_ge(s_zero, 1)
            sp.dma_start(xn_out[0:3 * (N + 1) + 1:N + 1, :], zero[0:B, :]).then_inc(s_fill, 16)
            with sp.Fori(0, B - 1) as b:
                store(b, 0)
                sp.wait_ge(s_xn, CT * 2 * (b + 1))
                load(b + 1)
                store(b, 1)
            store(B - 1, 0)
            store(B - 1, 1)
            for s in range(2):
                sp.wait_ge(s_xnout[s], 16 * B)
                sp.wait_ge(s_out[s], 16 * OUTS * B)
            sp.wait_ge(s_fill, 16)

        @block.gpsimd
        def _(pool):
            nc.gpsimd.memset(zero, 0.0).then_inc(s_zero, 1)
            for s in range(2):
                pool.wait_ge(s_zero, 2 * s + 1)
                nc.gpsimd.memset(vrow[s], 0.0).then_inc(s_zero, 1)
                pool.wait_ge(s_zero, 2 * s + 2)
                nc.gpsimd.memset(vrow[s][:, :, :, 8:9], 1.0).then_inc(s_zero, 1)
            with pool.Fori(0, CHUNKS) as n:
                pool.wait_ge(s_t12, 3 * (n + 1))
                pool.wait_ge(s_p1, n)
                pool.wait_ge(s_r1, n)
                nc.gpsimd.tensor_tensor(rot, t1, t2, ALU.add).then_inc(s_rot, 1)

        @block.tensor
        def _(pe):
            pe.wait_ge(s_const, 16 * 7)
            with pe.Fori(0, B) as b:
                for s in range(2):
                    n = 2 * b + s
                    pe.wait_ge(s_xn, CT * (n + 1))
                    for t in range(CT):
                        last = nc.tensor.transpose(bank[0][:, P * t:P * (t + 1)], xn[s][:, t, :], identf)
                    last.then_inc(s_t, 1)
                    pe.wait_ge(s_xt, n + 1)
                    pe.wait_ge(s_t12, 3 * n)
                    for i in range(4):
                        last = nc.tensor.matmul(bank[2 + i], w_all[:, i, :], xt[s], start=True, stop=True)
                    last.then_inc(s_qk, 1)
                    pe.wait_ge(s_vrow, n)
                    for t in range(CT):
                        last = nc.tensor.matmul(bank[1][:, P * t:P * (t + 1)], xt[s][:, P * t:P * (t + 1)],
                                                w_all[:, 4, :], start=True, stop=True)
                    last.then_inc(s_v, 1)

        @block.scalar
        def _(act):
            def root(n):
                act.wait_ge(s_var, n + 1)
                nc.scalar.activation(w.std, w.vareps, ACT.Sqrt).then_inc(s_std, 1)

            def post(b, s):
                n = 2 * b + s
                act.wait_ge(s_t, n + 1)
                nc.scalar.activation(xt[s], bank[0], ACT.Copy).then_inc(s_xt, 1)
                act.wait_ge(s_v, n + 1)
                act.wait_ge(s_out[s], 16 * OUTS * b)
                nc.scalar.activation(vrow[s][:, :, :, 0:8],
                                     bank[1].rearrange("p (t h d) -> p t h d", t=CT, h=16), ACT.Copy).then_inc(s_vrow, 1)
                act.wait_ge(s_rot, n + 1)
                nc.scalar.activation(parts[s][:, :, 0, :], rot, ACT.Copy).then_inc(s_p1, 1)
                act.wait_ge(s_r1, n + 1)
                nc.scalar.activation(parts[s][:, :, 1, :], rest, ACT.Copy).then_inc(s_p2, 1)

            act.wait_ge(s_zero, 5)
            root(0)
            with act.Fori(0, B - 1) as b:
                root(2 * b + 1)
                post(b, 0)
                root(2 * b + 2)
                post(b, 1)
            root(2 * B - 1)
            post(B - 1, 0)
            post(B - 1, 1)

        @block.vector
        def _(dve):
            chain = Chain(dve, s_chain)

            def norm(b, s):
                n = 2 * b + s
                dve.wait_ge(s_x[s], 16 * (b + 1))
                dve.wait_ge(s_t, n)
                dve.wait_ge(s_xnout[s], 16 * b)
                w.stat_count = lambda: (CT - 1) * (n + 1)
                chain.base, chain.n = n * LN_STEPS, 0
                layernorm(nc, dve, chain, xs[s], xn[s], w, lambda: dve.wait_ge(s_std, n + 1), s_var, s_xn)

            def rotate(b, s):
                n = 2 * b + s
                dve.wait_ge(s_qk, n + 1)
                dve.wait_ge(s_rot, n)
                place = slice(CW * s, CW * (s + 1))
                both = bank.run(2, 2).rearrange("p (w t) -> p w t", w=2)
                partner = bank.run(4, 2).rearrange("p (w t) -> p w t", w=2)
                nc.vector.tensor_tensor(t1, both, cos[:, place].unsqueeze(1).broadcast_to([P, 2, CW]), ALU.mult)\
                    .then_inc(s_t12, 1)
                nc.vector.tensor_tensor(t2, partner, sin[:, place].unsqueeze(1).broadcast_to([P, 2, CW]), ALU.mult)\
                    .then_inc(s_t12, 2)
                dve.wait_ge(s_p1, n + 1)
                dve.wait_ge(s_p2, n)
                dve.wait_ge(s_p3, n)
                nc.vector.tensor_tensor(rest, rot, parts[s][:, :, 0, :], ALU.subtract).then_inc(s_r1, 1)
                dve.wait_ge(s_r1, n + 1)
                dve.wait_ge(s_p2, n + 1)
                nc.vector.tensor_tensor(parts[s][:, :, 2, :], rest, parts[s][:, :, 1, :], ALU.subtract).then_inc(s_p3, 1)

            dve.wait_ge(s_const, 16 * 7)
            norm(0, 0)
            with dve.Fori(0, B - 1) as b:
                norm(b, 1)
                rotate(b, 0)
                norm(b + 1, 0)
                rotate(b, 1)
            norm(B - 1, 1)
            rotate(B - 1, 0)
            rotate(B - 1, 1)
    arena.at = mark



HEADS, DH = 8, 64
INNER = HEADS * DH
WINDOW = 64
SPAN = P + WINDOW
HID = 341
NEG = -1e30


def local_attention(nc, sem, arena, bank, identf, layer, stream, mid, wqkv, q_scales, wo, tables, masks):
    mark = arena.at
    PAIRS = HEADS // 2
    G = 4
    wq = arena.f32(3, INNER)
    wo_sb = arena.f32(PAIRS, D)
    scales = arena.f32(2, 2, DH)
    tabs = arena.f32(2, TB, 2, DH)
    mask_all = arena.f32(CT, SPAN)
    mask = [arena.f32(SPAN) for _ in range(2)]
    hs = [arena.f32(D) for _ in range(2)]
    xs = [arena.f32(D) for _ in range(2)]
    ht = arena.f32(P)
    sq = arena.f32(2 * HEADS, DH)
    ss, clipped, rnorm = arena.f32(2 * HEADS), arena.f32(2 * HEADS), arena.f32(2 * HEADS)
    power = arena.f32(2 * HEADS)
    t1, t2, rot = arena.f32(2, HEADS, DH), arena.f32(2, HEADS, DH), arena.f32(2, HEADS, DH)
    qk = arena.f32(2, INNER)
    qa, qb = arena.f32(PAIRS, P), arena.f32(PAIRS, P)
    kt = [arena.f32(PAIRS, SPAN) for _ in range(2)]
    v = [arena.f32(INNER) for _ in range(2)]
    sm = arena.f32(HEADS, SPAN)
    top, negtop, den, rden = arena.f32(HEADS), arena.f32(HEADS), arena.f32(HEADS), arena.f32(HEADS)
    p = arena.f32(HEADS, 2 * P)
    pt = arena.f32(HEADS, 2 * P)
    ot = arena.f32(PAIRS, P)
    outs = [arena.f32(D) for _ in range(2)]

    s = {n: sem("l_" + n) for n in (
        "w tab clear ht0 ht qkv sq ss clip rn t1 rot qk qt qa kt tail v s top neg e den norm pt pta ptv o ot y "
        "out mask").split()}
    s_h = [sem(f"l_h{i}") for i in range(2)]
    s_o = [sem(f"l_o{i}") for i in range(2)]
    PAIRT = TILES // 2
    NLOAD = 3

    with nc.Block() as block:

        @block.sync
        def _(sp):
            def load(i, z):
                row = (2 * i + z) * P + i // (TB // 2)
                sp.dma_start(hs[z][:, 0:D // 2], stream[bass.ds(layer, 1), bass.ds(row + 1, P), 0:D // 2].rearrange(
                    "a r d -> (a r) d")).then_inc(s_h[z], 16)
                sp.dma_start(hs[z][:, D // 2:D], stream[bass.ds(layer, 1), bass.ds(row, P), D // 2:D].rearrange(
                    "a r d -> (a r) d")).then_inc(s_h[z], 16)
                sp.dma_start(xs[z], stream[bass.ds(layer, 1), bass.ds(row + 1, P), :].rearrange(
                    "a r d -> (a r) d")).then_inc(s_h[z], 16)

            def store(i, z):
                row = (2 * i + z) * P + i // (TB // 2) + 1
                sp.wait_ge(s["out"], 2 * i + z + 1)
                sp.dma_start(mid[bass.ds(row, P), :], outs[z]).then_inc(s_o[z], 16)

            sp.dma_start(wq, wqkv[bass.ds(layer, 1), :, :].rearrange("a p (w n) -> (a p) w n", w=3)).then_inc(s["w"], 16)
            sp.dma_start(wo_sb, wo[bass.ds(layer, 1), :, :].rearrange("a (c p) n -> (a p) c n", p=P)).then_inc(s["w"], 16)
            sp.dma_start(scales, q_scales[bass.ds(layer, 1), :, :, :, :].rearrange("a p x w d -> (a p) x w d"))\
                .then_inc(s["w"], 16)
            sp.dma_start(tabs, tables).then_inc(s["w"], 16)
            sp.dma_start(mask_all, masks).then_inc(s["w"], 16)
            load(0, 0)
            load(0, 1)
            sp.wait_ge(s["w"], 80)
            with sp.Fori(0, PAIRT - 1) as i:
                for z in range(2):
                    sp.wait_ge(s["out"], 2 * i + z + 1)
                    load(i + 1, z)
                    store(i, z)
            store(PAIRT - 1, 0)
            store(PAIRT - 1, 1)
            for z in range(2):
                sp.wait_ge(s_o[z], 16 * PAIRT)

        @block.gpsimd
        def _(pool):
            n = 0
            for piece, value in ((qa, 0.0), (qb, 0.0), (p, 0.0), (kt[1], 0.0), (v[1], 0.0), (power, -0.5)):
                nc.gpsimd.memset(piece, value).then_inc(s["clear"], 1)
                n += 1
                pool.wait_ge(s["clear"], n)
            pool.wait_ge(s["w"], 80)

            def tile(i, z):
                n = 2 * i + z
                if z == 0:
                    pool.wait_ge(s["top"], HEADS * n)
                    nc.gpsimd.tensor_copy(
                        mask[0], mask_all.rearrange("p a n -> p (a n)")[:, bass.ds(i % (TB // 2) * SPAN, SPAN)])\
                        .then_inc(s["mask"], 1)
                pool.wait_ge(s["clip"], n + 1)
                nc.gpsimd.tensor_tensor(rnorm, clipped, power, ALU.pow).then_inc(s["rn"], 1)
                pool.wait_ge(s["t1"], 3 * (n + 1))
                nc.gpsimd.tensor_tensor(rot, t1, t2, ALU.add).then_inc(s["rot"], 1)
                pool.wait_ge(s["rot"], n + 1)
                pool.wait_ge(s["rn"], n + 1)
                pool.wait_ge(s["qt"], n)
                nc.gpsimd.tensor_tensor(
                    qk.rearrange("p w (h d) -> p (w h) d", d=DH), rot.rearrange("p w h d -> p (w h) d"),
                    rnorm.unsqueeze(2).broadcast_to([P, 2 * HEADS, DH]), ALU.mult).then_inc(s["qk"], 1)

            with pool.Fori(0, PAIRT) as i:
                tile(i, 0)
                tile(i, 1)

        @block.tensor
        def _(pe):
            def project(i, z):
                n = 2 * i + z
                pe.wait_ge(s_h[z], 16 * NLOAD * (i + 1))
                pe.wait_ge(s["v"], n)
                nc.tensor.transpose(bank[2][:, 0:P], hs[z], identf).then_inc(s["ht0"], 1)
                pe.wait_ge(s["ht"], n + 1)
                pe.wait_ge(s["t1"], 3 * n)
                pe.wait_ge(s["sq"], n)
                for w in range(2):
                    last = nc.tensor.matmul(bank[w], ht, wq[:, w, :], start=True, stop=True)
                last.then_inc(s["qkv"], 1)
                nc.tensor.matmul(bank[2], ht, wq[:, 2, :], start=True, stop=True).then_inc(s["qkv"], 1)

            def turn(n):
                pe.wait_ge(s["qk"], n + 1)
                pe.wait_ge(s["pta"], 2 * n)
                pe.wait_ge(s["ptv"], 2 * n)
                for w in range(2):
                    for c in range(PAIRS):
                        last = nc.tensor.transpose(bank[3 + w][:, P * c:P * (c + 1)], qk[:, w, P * c:P * (c + 1)], identf)
                last.then_inc(s["qt"], 1)

            def scores(n, z, g):
                if g == 0:
                    pe.wait_ge(s["qa"], 2 * (n + 1))
                    pe.wait_ge(s["kt"], n + 1)
                    pe.wait_ge(s["tail"], n + 1)
                pe.wait_ge(s["top"], HEADS * n + G * g)
                for j in range(G):
                    h = G * g + j
                    last = nc.tensor.matmul(bank[5 + j // 2][:, SPAN * (j % 2):SPAN * (j % 2 + 1)],
                                            (qa, qb)[h % 2][:, h // 2, :], kt[z][:, h // 2, :], start=True, stop=True)
                last.then_inc(s["s"], 1)

            def probs_turn(n, g):
                pe.wait_ge(s["norm"], 2 * n + g + 1)
                if g == 0:
                    pe.wait_ge(s["qa"], 2 * (n + 1))
                    pe.wait_ge(s["kt"], n + 1)
                else:
                    pe.wait_ge(s["pta"], 2 * n + 1)
                    pe.wait_ge(s["ptv"], 2 * n + 1)
                for j in range(G):
                    for c in range(2):
                        last = nc.tensor.transpose(bank[3 + j // 2][:, 2 * P * (j % 2) + P * c:2 * P * (j % 2) + P * (c + 1)],
                                                   p[:, G * g + j, P * c:P * (c + 1)], identf)
                last.then_inc(s["pt"], 1)

            def values(n, z, g):
                pe.wait_ge(s["pta"], 2 * n + g + 1)
                pe.wait_ge(s["ptv"], 2 * n + g + 1)
                if g == 0:
                    pe.wait_ge(s["v"], n + 1)
                    pe.wait_ge(s["out"], n)
                for pair in range(2):
                    for c in range(2):
                        for j in range(2):
                            h = G * g + 2 * pair + j
                            last = nc.tensor.matmul(
                                bank[7][DH * j:DH * (j + 1), P * (h // 2):P * (h // 2 + 1)],
                                v[1 - z if c == 0 else z][:, DH * h:DH * (h + 1)], pt[:, h, P * c:P * (c + 1)],
                                start=(c == 0), stop=(c == 1), tile_position=(0, DH * j))
                last.then_inc(s["o"], 1)

            def project_out(n):
                pe.wait_ge(s["ot"], n + 1)
                for c in range(PAIRS):
                    last = nc.tensor.matmul(bank[7][:, 0:D], ot[:, c, :], wo_sb[:, c, :],
                                            start=(c == 0), stop=(c == PAIRS - 1))
                last.then_inc(s["y"], 1)

            def tile(i, z, following):
                n = 2 * i + z
                scores(n, z, 0)
                if following:
                    project(i + z, 1 - z)
                scores(n, z, 1)
                probs_turn(n, 0)
                values(n, z, 0)
                probs_turn(n, 1)
                values(n, z, 1)
                if following:
                    turn(n + 1)
                project_out(n)

            pe.wait_ge(s["w"], 80)
            pe.wait_ge(s["clear"], 6)
            project(0, 0)
            turn(0)
            with pe.Fori(0, PAIRT - 1) as i:
                tile(i, 0, True)
                tile(i, 1, True)
            tile(PAIRT - 1, 0, True)
            tile(PAIRT - 1, 1, False)

        @block.scalar
        def _(act):
            def prepare(n, z):
                act.wait_ge(s["ht0"], n + 1)
                act.wait_ge(s["qkv"], 2 * n)
                nc.scalar.activation(ht, bank[2][:, 0:P], ACT.Copy).then_inc(s["ht"], 1)
                act.wait_ge(s["qkv"], 2 * n + 1)
                act.wait_ge(s["ss"], n)
                nc.scalar.activation(sq, bank.run(0, 2).rearrange("p (h d) -> p h d", d=DH), ACT.Square)\
                    .then_inc(s["sq"], 1)

            def values_copy(n, z):
                act.wait_ge(s["qkv"], 2 * n + 2)
                act.wait_ge(s["o"], 2 * n)
                nc.scalar.activation(v[z], bank[2], ACT.Copy).then_inc(s["v"], 1)

            def keys(n, z):
                act.wait_ge(s["qt"], n + 1)
                act.wait_ge(s["tail"], n)
                nc.scalar.activation(kt[z][:, :, WINDOW:SPAN], bank[4].rearrange("p (c t) -> p c t", c=PAIRS), ACT.Copy)\
                    .then_inc(s["kt"], 1)

            def exps(n, g):
                act.wait_ge(s["neg"], 2 * n + g + 1)
                act.wait_ge(s["pt"], 2 * n)
                for j in range(G):
                    h = G * g + j
                    nc.scalar.activation(p[:, h, WINDOW:2 * P], sm[:, h, :], ACT.Exp, bias=negtop[:, h:h + 1],
                                         scale=8.0, accum_out=den[:, h:h + 1]).then_inc(s["e"], 1)

            def probs_copy(n, g):
                act.wait_ge(s["pt"], 2 * n + g + 1)
                act.wait_ge(s["o"], 2 * n)
                nc.scalar.activation(pt[:, G * g:G * g + 2, :], bank[3].rearrange("p (h t) -> p h t", h=2), ACT.Copy)\
                    .then_inc(s["pta"], 1)

            def out_copy(n):
                act.wait_ge(s["o"], 2 * n + 2)
                act.wait_ge(s["y"], n)
                nc.scalar.activation(ot, bank[7].rearrange("p (c t) -> p c t", c=PAIRS), ACT.Copy).then_inc(s["ot"], 1)

            def tile(i, z, following):
                n = 2 * i + z
                exps(n, 0)
                if following:
                    prepare(n + 1, 1 - z)
                exps(n, 1)
                probs_copy(n, 0)
                probs_copy(n, 1)
                if following:
                    values_copy(n + 1, 1 - z)
                    keys(n + 1, 1 - z)
                out_copy(n)

            act.wait_ge(s["clear"], 6)
            prepare(0, 0)
            values_copy(0, 0)
            keys(0, 0)
            with act.Fori(0, PAIRT - 1) as i:
                tile(i, 0, True)
                tile(i, 1, True)
            tile(PAIRT - 1, 0, True)
            tile(PAIRT - 1, 1, False)

        @block.vector
        def _(dve):
            def norms(n, z, i):
                dve.wait_ge(s["sq"], n + 1)
                dve.wait_ge(s["rn"], n)
                nc.vector.tensor_reduce(ss, sq, AX.X, ALU.add).then_inc(s["ss"], 1)
                dve.wait_ge(s["ss"], n + 1)
                nc.vector.tensor_scalar(clipped, ss, 1e-24, None, ALU.max).then_inc(s["clip"], 1)
                dve.wait_ge(s["rot"], n)
                t = (i % (TB // 2)) * 2 + z
                both = bank.run(0, 2).rearrange("p (w h d) -> p w h d", w=2, h=HEADS)
                flat = tabs.rearrange("p x t w d -> p (x t w d)")
                H = DH // 2

                def table(x, lo, hi, w):
                    one = flat[:, bass.ds(t * (2 * DH) + x * TB * 2 * DH, 2 * DH)].rearrange("p (w d) -> p w d", w=2)
                    return one[:, :, lo:hi].unsqueeze(2).broadcast_to([P, 2, HEADS, hi - lo])

                nc.vector.tensor_tensor(t1, both, table(0, 0, DH, 2), ALU.mult).then_inc(s["t1"], 1)
                nc.vector.tensor_tensor(t2[:, :, :, 0:H], both[:, :, :, H:DH], table(1, 0, H, 2), ALU.mult)\
                    .then_inc(s["t1"], 1)
                nc.vector.tensor_tensor(t2[:, :, :, H:DH], both[:, :, :, 0:H], table(1, H, DH, 2), ALU.mult)\
                    .then_inc(s["t1"], 1)

            def queries(n, z):
                dve.wait_ge(s["qt"], n + 1)
                dve.wait_ge(s["s"], 2 * n)
                nc.vector.tensor_copy(qa[0:DH], bank[3][0:DH].rearrange("p (c t) -> p c t", c=PAIRS)).then_inc(s["qa"], 1)
                nc.vector.tensor_copy(qb[DH:P], bank[3][DH:P].rearrange("p (c t) -> p c t", c=PAIRS)).then_inc(s["qa"], 1)
                dve.wait_ge(s["kt"], n)
                nc.vector.tensor_copy(kt[z][:, :, 0:WINDOW], kt[1 - z][:, :, P:SPAN]).then_inc(s["tail"], 1)

            def maxima(n, z, g, i):
                dve.wait_ge(s["s"], 2 * n + g + 1)
                dve.wait_ge(s["tab"], 3)
                if g == 0 and z == 0:
                    dve.wait_ge(s["mask"], i + 1)
                dve.wait_ge(s["e"], HEADS * n)
                part = slice(G * g, G * (g + 1))
                for b in range(2):
                    nc.vector.tensor_tensor(
                        sm[:, G * g + 2 * b:G * g + 2 * b + 2, :],
                        bank[5 + b][:, 0:2 * SPAN].rearrange("p (h t) -> p h t", h=2),
                        mask[z].unsqueeze(1).broadcast_to([P, 2, SPAN]), ALU.add).then_inc(s["top"], 2)
                dve.wait_ge(s["top"], HEADS * n + G * (g + 1))
                nc.vector.tensor_reduce(top[:, part], sm[:, part, :], AX.X, ALU.max).then_inc(s["den"], 1)
                dve.wait_ge(s["den"], 4 * n + 1 + g)
                nc.vector.tensor_scalar(negtop[:, part], top[:, part], -8.0, None, ALU.mult).then_inc(s["neg"], 1)

            def normalize(n, g):
                dve.wait_ge(s["e"], HEADS * n + G * (g + 1))
                part = slice(G * g, G * (g + 1))
                nc.vector.reciprocal(rden[:, part], den[:, part]).then_inc(s["den"], 1)
                dve.wait_ge(s["den"], 4 * n + g + 3)
                nc.vector.tensor_tensor(p[:, part, WINDOW:2 * P], p[:, part, WINDOW:2 * P],
                                        rden[:, part].unsqueeze(2).broadcast_to([P, G, SPAN]), ALU.mult)\
                    .then_inc(s["norm"], 1)

            def probs_copy(n, g):
                dve.wait_ge(s["pt"], 2 * n + g + 1)
                dve.wait_ge(s["o"], 2 * n)
                nc.vector.tensor_copy(pt[:, G * g + 2:G * g + 4, :], bank[4].rearrange("p (h t) -> p h t", h=2))\
                    .then_inc(s["ptv"], 1)

            def finish(n, z, i):
                dve.wait_ge(s["y"], n + 1)
                dve.wait_ge(s_o[z], 16 * (i))
                nc.vector.tensor_tensor(outs[z], bank[7][:, 0:D], xs[z], ALU.add).then_inc(s["out"], 1)

            def tile(i, z, following):
                n = 2 * i + z
                maxima(n, z, 0, i)
                if following:
                    norms(n + 1, 1 - z, i + z)
                maxima(n, z, 1, i)
                normalize(n, 0)
                normalize(n, 1)
                probs_copy(n, 0)
                probs_copy(n, 1)
                if following:
                    queries(n + 1, 1 - z)
                finish(n, z, i)

            dve.wait_ge(s["w"], 80)
            dve.wait_ge(s["clear"], 6)
            for x in range(2):
                nc.vector.tensor_tensor(tabs[:, x], tabs[:, x],
                                        scales[:, x].unsqueeze(1).broadcast_to([P, TB, 2, DH]), ALU.mult)\
                    .then_inc(s["tab"], 1)
            nc.vector.tensor_copy(mask[1], mask_all[:, 1, :]).then_inc(s["tab"], 1)
            dve.wait_ge(s["tab"], 3)
            norms(0, 0, 0)
            queries(0, 0)
            with dve.Fori(0, PAIRT - 1) as i:
                tile(i, 0, True)
                tile(i, 1, True)
            tile(PAIRT - 1, 0, True)
            tile(PAIRT - 1, 1, False)
    arena.at = mark


BLOCKS = 3
HB = -(-HID // BLOCKS)


def feed_forward(nc, sem, arena, bank, identf, layer, mid, stream, ln, w1, b1, w2, b2):
    mark = arena.at
    size = [HB, HB, HID - 2 * HB]
    w1_sb = arena.f32(2, HID)
    w2_sb = arena.f32(BLOCKS, D)
    b1_sb = arena.f32(2, BLOCKS)
    b2_sb = arena.f32(D)
    ln_sb = arena.f32(2)
    hs = [arena.f32(CT, D) for _ in range(2)]
    xs = [arena.f32(CT, D) for _ in range(2)]
    hn = arena.f32(CT, D)
    ht = [arena.f32(CW) for _ in range(2)]
    gate = arena.f32(BLOCKS, CW)
    u = arena.f32(BLOCKS, CW)
    xb = [arena.f32(CT, D) for _ in range(2)]
    outs = [arena.f32(CT, D) for _ in range(2)]
    power = arena.f32(CT)
    s = {n: sem("f_" + n) for n in "w power stat chain var std hn t ht a gate u y xb out".split()}
    s_h = [sem(f"f_h{i}") for i in range(2)]
    s_o = [sem(f"f_o{i}") for i in range(2)]
    w = NormBuffers(nc, arena, s["stat"])
    w.invert = None
    CHUNKS = 2 * B
    LOADS = 7

    with nc.Block() as block:

        @block.sync
        def _(sp):
            def load(b, z):
                row = b * (N + 1) + CW * z
                for dst, r, lo, hi in ((hs[z], row + 1, 0, D // 2), (hs[z], row, D // 2, D), (xs[z], row + 1, 0, D)):
                    sp.dma_start(dst[:, :, lo:hi], mid[bass.ds(r, CW), lo:hi].rearrange("(t p) d -> p t d", p=P))\
                        .then_inc(s_h[z], 16)

            def store(b, z):
                sp.wait_ge(s["out"], 2 * b + z + 1)
                sp.dma_start(stream[bass.ds(layer + 1, 1), bass.ds(b * (N + 1) + CW * z + 1, CW), :].rearrange(
                    "a (t p) d -> p (a t) d", p=P), outs[z]).then_inc(s_o[z], 16)

            load(0, 0)
            load(0, 1)
            with sp.Fori(0, B - 1) as b:
                for z in range(2):
                    store(b, z)
                    sp.wait_ge(s["xb"], 2 * b + z + 1)
                    load(b + 1, z)
            store(B - 1, 0)
            store(B - 1, 1)
            for z in range(2):
                sp.wait_ge(s_o[z], 16 * B)

        @block.gpsimd
        def _(pool):
            nc.gpsimd.memset(power, -0.5).then_inc(s["power"], 1)
            pool.wait_ge(s["power"], 1)
            pool.wait_ge(s["w"], 16 * LOADS)
            with pool.Fori(0, B) as b:
                for z in range(2):
                    n = 2 * b + z
                    pool.wait_ge(s["var"], n + 1)
                    pool.wait_ge(s["hn"], CT * n)
                    nc.gpsimd.tensor_tensor(w.rstd, w.vareps, power, ALU.pow).then_inc(s["std"], 1)
                    pool.wait_ge(s_h[z], 48 * (b + 1))
                    pool.wait_ge(s["out"], n)
                    nc.gpsimd.tensor_tensor(xb[z], xs[z], b2_sb.unsqueeze(1).broadcast_to([P, CT, D]), ALU.add)\
                        .then_inc(s["xb"], 1)

        @block.tensor
        def _(pe):
            def turn(n):
                pe.wait_ge(s["hn"], CT * (n + 1))
                pe.wait_ge(s["ht"], n)
                for t in range(CT):
                    last = nc.tensor.transpose(bank[0][:, P * t:P * (t + 1)], hn[:, t, :], identf)
                last.then_inc(s["t"], 1)

            def hidden(n, z):
                pe.wait_ge(s["ht"], n + 1)
                for k in range(BLOCKS):
                    for half in (1, 0):
                        if half == 1:
                            pe.wait_ge(s["gate"], BLOCKS * n)
                        else:
                            pe.wait_ge(s["u"], BLOCKS * n)
                        nc.tensor.matmul(bank[1 + 2 * k + half][0:size[k], :],
                                         w1_sb[:, half, HB * k:HB * k + size[k]], ht[z], start=True, stop=True)\
                            .then_inc(s["a"], 1)

            def output(n):
                pe.wait_ge(s["u"], BLOCKS * (n + 1))
                pe.wait_ge(s["out"], n)
                for t in range(CT):
                    for k in range(BLOCKS):
                        last = nc.tensor.matmul(bank[7][:, P * t:P * (t + 1)], u[0:size[k], k, P * t:P * (t + 1)],
                                                w2_sb[0:size[k], k, :], start=(k == 0), stop=(k == BLOCKS - 1))
                last.then_inc(s["y"], 1)

            pe.wait_ge(s["w"], 16 * LOADS)
            turn(0)
            with pe.Fori(0, B - 1) as b:
                for z in range(2):
                    n = 2 * b + z
                    hidden(n, z)
                    turn(n + 1)
                    output(n)
            n = CHUNKS - 2
            hidden(n, 0)
            turn(n + 1)
            output(n)
            hidden(n + 1, 1)
            output(n + 1)

        @block.scalar
        def _(act):
            def turned(n, z):
                act.wait_ge(s["t"], n + 1)
                act.wait_ge(s["a"], 2 * BLOCKS * n)
                nc.scalar.activation(ht[z], bank[0], ACT.Identity, bias=ln_sb[:, 1:2], scale=ln_sb[:, 0:1])\
                    .then_inc(s["ht"], 1)

            def gates(n):
                for k in range(BLOCKS):
                    act.wait_ge(s["a"], 2 * BLOCKS * n + 2 * k + 1)
                    act.wait_ge(s["u"], BLOCKS * n)
                    r = size[k]
                    nc.scalar.activation(gate[0:r, k, :], bank[2 + 2 * k][0:r, :], ACT.Gelu, bias=b1_sb[0:r, 1, k:k + 1])\
                        .then_inc(s["gate"], 1)

            act.dma_start(w1_sb, w1[bass.ds(layer, 1), :, :].rearrange("a p (w n) -> (a p) w n", w=2)).then_inc(s["w"], 16)
            for k in range(BLOCKS):
                act.dma_start(w2_sb[0:size[k], k, :], w2[bass.ds(layer, 1), HB * k:HB * k + size[k], :].rearrange(
                    "a r n -> (a r) n")).then_inc(s["w"], 16)
            act.dma_start(b1_sb[0:HB], b1[bass.ds(layer, 1), :, :, :].rearrange("a r w k -> (a r) w k")).then_inc(s["w"], 16)
            act.dma_start(b2_sb, b2[bass.ds(layer, 1), :, :].rearrange("a p n -> (a p) n")).then_inc(s["w"], 16)
            act.dma_start(ln_sb, ln[bass.ds(layer, 1), :, :].rearrange("a p n -> (a p) n")).then_inc(s["w"], 16)
            act.wait_ge(s["w"], 16 * LOADS)
            turned(0, 0)
            with act.Fori(0, B - 1) as b:
                for z in range(2):
                    n = 2 * b + z
                    gates(n)
                    turned(n + 1, 1 - z)
            n = CHUNKS - 2
            gates(n)
            turned(n + 1, 1)
            gates(n + 1)

        @block.vector
        def _(dve):
            chain = Chain(dve, s["chain"])
            STEPS = LN_STEPS - 1

            def norm(b, z):
                n = 2 * b + z
                dve.wait_ge(s_h[z], 48 * (b + 1))
                w.stat_count = lambda: (CT - 1) * (n + 1)
                chain.base, chain.n = n * STEPS, 0

                def root():
                    dve.wait_ge(s["std"], n + 1)
                    dve.wait_ge(s["t"], n)
                layernorm(nc, dve, chain, hs[z], hn, w, root, s["var"], s["hn"])

            def post(b, z):
                n = 2 * b + z
                for k in range(BLOCKS):
                    r = size[k]
                    dve.wait_ge(s["gate"], BLOCKS * n + k + 1)
                    dve.wait_ge(s["a"], 2 * BLOCKS * n + 2 * k + 2)
                    dve.wait_ge(s["y"], n)
                    nc.vector.scalar_tensor_tensor(u[0:r, k, :], bank[1 + 2 * k][0:r, :], b1_sb[0:r, 0, k:k + 1],
                                                   gate[0:r, k, :], ALU.add, ALU.mult).then_inc(s["u"], 1)

            def finish(b, z):
                n = 2 * b + z
                dve.wait_ge(s["y"], n + 1)
                dve.wait_ge(s["xb"], n + 1)
                dve.wait_ge(s_o[z], 16 * b)
                nc.vector.tensor_tensor(outs[z], bank[7].rearrange("p (t d) -> p t d", t=CT), xb[z], ALU.add)\
                    .then_inc(s["out"], 1)

            dve.wait_ge(s["w"], 16 * LOADS)
            norm(0, 0)
            with dve.Fori(0, B - 1) as b:
                norm(b, 1)
                post(b, 0)
                finish(b, 0)
                norm(b + 1, 0)
                post(b, 1)
                finish(b, 1)
            norm(B - 1, 1)
            post(B - 1, 0)
            finish(B - 1, 0)
            post(B - 1, 1)
            finish(B - 1, 1)
    arena.at = mark



def middle_phase(nc, sem, arena, bank, identf, O, w_out, b_out, x, stream, wq, wkd, wku, wvu, wsw, bsw,
                 x1_out, xn_out, qk_parts, v_rows, logits):
    mark = arena.at
    E = 2 * D
    LR = 64
    w_out_sb = arena.f32(D)
    b_out_sb = arena.f32(D)
    wq_sb = arena.f32(2, D)
    wkd_sb = arena.f32(LR)
    wku_sb, wvu_sb = arena.f32(2, D), arena.f32(E)
    wsw_sb, bsw_sb = arena.f32(8), arena.f32(8)
    xs = [arena.f32(CT, D) for _ in range(2)]
    gs = [arena.f32(CT, D) for _ in range(2)]
    oc = arena.f32(CT, D)
    ot, sg = arena.f32(CW), arena.f32(CT, D)
    sp1, sp2 = arena.f32(CT, D), arena.f32(CT, D)
    x1 = [arena.f32(CT, D) for _ in range(2)]
    xn = [arena.f32(CT, D) for _ in range(2)]
    xt = arena.f32(CW)
    lat = arena.f32(CW)
    rest = arena.f32(2, CW)
    parts = arena.bf16(2, 2, 3, CW)
    vrow = arena.f32(CT, 8, 64)
    s = {n: sem("m_" + n) for n in ("w stat chain var std clear oc ot0 ot so sg s1 s2 x1 xn t xt q lat0 lat k v0 v "
                                    "lg lgo p1 r1 p2 p3 fill").split()}
    s_x = [sem(f"m_load{i}") for i in range(2)]
    s_o1 = [sem(f"m_o1{i}") for i in range(2)]
    s_oq, s_ov = sem("m_oq"), sem("m_ov")
    w = NormBuffers(nc, arena, s["stat"])
    LOADS = 8
    CHUNKS = 2 * B

    with nc.Block() as block:

        @block.sync
        def _(sp):
            def load(b, z):
                sp.dma_start(xs[z], x[bass.ds(b, 1), CW * z:CW * (z + 1), :].rearrange("a (t p) d -> p (a t) d", p=P))\
                    .then_inc(s_x[z], 16)
                sp.dma_start(gs[z], stream[2, bass.ds(b * (N + 1) + 1 + CW * z, CW), :].rearrange(
                    "(t p) d -> p t d", p=P)).then_inc(s_x[z], 16)

            def store(b, z):
                n = 2 * b + z
                for sig, src, dst in ((s["x1"], x1, x1_out), (s["xn"], xn, xn_out)):
                    sp.wait_ge(sig, (CT if src is xn else 1) * (n + 1))
                    sp.dma_start(dst[bass.ds(n * CT, CT), :, :].rearrange("t p d -> p t d"), src[z])\
                        .then_inc(s_o1[z], 16)
                for which in range(2):
                    sp.wait_ge(s["p3"], 2 * n + which + 1)
                    sp.wait_ge(s["p2"], 2 * n + which + 1)
                    for blk in range(2):
                        for half in range(2):
                            sp.dma_start(
                                qk_parts[bass.ds(4 * b + 2 * blk + half, 1), 3 * which:3 * which + 3, :,
                                         CW * z:CW * (z + 1)].rearrange("a n r t -> (a r) n t"),
                                parts[64 * half:64 * (half + 1), which, blk, :, :]).then_inc(s_oq, 16)
                sp.wait_ge(s["v"], 2 * (n + 1))
                for pair in range(4):
                    sp.dma_start(v_rows[bass.ds(4 * b + pair, 1), :, CT * z:CT * (z + 1), :].rearrange(
                        "a p t m -> (a p) t m"),
                        vrow[:, :, 2 * pair:2 * pair + 2, :].rearrange("p t h m -> p t (h m)")).then_inc(s_ov, 16)

            load(0, 0)
            load(0, 1)
            with sp.Fori(0, B - 1) as b:
                for z in range(2):
                    sp.wait_ge(s["x1"], 2 * b + z + 1)
                    load(b + 1, z)
                    store(b, z)
            store(B - 1, 0)
            store(B - 1, 1)
            for z in range(2):
                sp.wait_ge(s_o1[z], 32 * B)
            sp.wait_ge(s_oq, 16 * 8 * CHUNKS)
            sp.wait_ge(s_ov, 16 * 4 * CHUNKS)

        @block.gpsimd
        def _(pool):
            n = 0
            for piece, value in ((vrow, 0.0), (vrow[:, :, :, 32:33], 1.0), (wku_sb, 0.0), (wvu_sb, 0.0), (lat, 0.0)):
                nc.gpsimd.memset(piece, value).then_inc(s["clear"], 1)
                n += 1
                pool.wait_ge(s["clear"], n)
            flat = O.rearrange("p u t d -> p (u t d)")
            with pool.Fori(0, B) as b:
                for z in range(2):
                    n = 2 * b + z
                    pool.wait_ge(s["ot0"], n)
                    for g in range(4):
                        src = flat[:, bass.ds(b * (4 * TB * UR) + g * TB * UR + z * CT * UR, CT * UR)]
                        ins = nc.gpsimd.tensor_copy(oc[:, :, UR * g:UR * (g + 1)],
                                                    src.rearrange("p (t d) -> p t d", t=CT))
                        ins.then_inc(s["oc"], 1)

        @block.tensor
        def _(pe):
            pe.wait_ge(s["w"], 16 * LOADS)
            pe.wait_ge(s["clear"], 5)
            with pe.Fori(0, B) as b:
                for z in range(2):
                    n = 2 * b + z
                    pe.wait_ge(s["oc"], 4 * (n + 1))
                    pe.wait_ge(s["lat"], n)
                    for t in range(CT):
                        last = nc.tensor.transpose(bank[0][:, P * t:P * (t + 1)], oc[:, t, :], identf)
                    last.then_inc(s["ot0"], 1)
                    pe.wait_ge(s["ot"], n + 1)
                    pe.wait_ge(s["lgo"], n)
                    for t in range(CT):
                        last = nc.tensor.matmul(bank[1][:, P * t:P * (t + 1)], ot[:, P * t:P * (t + 1)], w_out_sb,
                                                start=True, stop=True)
                    last.then_inc(s["so"], 1)
                    pe.wait_ge(s["xn"], CT * (n + 1))
                    for t in range(CT):
                        last = nc.tensor.transpose(bank[2][:, P * t:P * (t + 1)], xn[z][:, t, :], identf)
                    last.then_inc(s["t"], 1)
                    pe.wait_ge(s["xt"], n + 1)
                    pe.wait_ge(s["r1"], 2 * n)
                    pe.wait_ge(s["p1"], 2 * n)
                    for blk in range(2):
                        last = nc.tensor.matmul(bank[3 + blk], wq_sb[:, blk, :], xt, start=True, stop=True)
                    last.then_inc(s["q"], 1)
                    nc.tensor.matmul(bank[0][0:LR, :], wkd_sb, xt, start=True, stop=True).then_inc(s["lat0"], 1)
                    pe.wait_ge(s["s1"], n + 1)
                    for t in range(CT):
                        last = nc.tensor.matmul(bank[1][:, 8 * t:8 * (t + 1)], xt[:, P * t:P * (t + 1)], wsw_sb,
                                                start=True, stop=True)
                    last.then_inc(s["lg"], 1)
                    pe.wait_ge(s["lat"], n + 1)
                    for blk in range(2):
                        last = nc.tensor.matmul(bank[5 + blk], wku_sb[:, blk, :], lat, start=True, stop=True)
                    last.then_inc(s["k"], 1)
                    for g in range(2):
                        pe.wait_ge(s["v"], 2 * n + g)
                        for t in range(2):
                            tt = 2 * g + t
                            last = nc.tensor.matmul(bank[7][:, E * t:E * (t + 1)], lat[:, P * tt:P * (tt + 1)], wvu_sb,
                                                    start=True, stop=True)
                        last.then_inc(s["v0"], 1)

        @block.scalar
        def _(act):
            for dst, src in ((w_out_sb, w_out), (b_out_sb, b_out), (wq_sb, wq.rearrange("p (c n) -> p c n", c=2)),
                             (wkd_sb, wkd), (wsw_sb, wsw), (bsw_sb, bsw)):
                act.dma_start(dst, src).then_inc(s["w"], 16)
            act.wait_ge(s["clear"], 5)
            act.dma_start(wku_sb[0:LR], wku.rearrange("p (c n) -> p c n", c=2)).then_inc(s["w"], 16)
            act.dma_start(wvu_sb[0:LR], wvu).then_inc(s["w"], 16)
            with act.Fori(0, B) as b:
                for z in range(2):
                    n = 2 * b + z
                    act.wait_ge(s_x[z], 32 * (b + 1))
                    act.wait_ge(s["s2"], n)
                    nc.scalar.activation(sg, gs[z], ACT.Silu).then_inc(s["sg"], 1)
                    act.wait_ge(s["ot0"], n + 1)
                    act.wait_ge(s["so"], n)
                    nc.scalar.activation(ot, bank[0], ACT.Copy).then_inc(s["ot"], 1)
                    act.wait_ge(s["var"], n + 1)
                    nc.scalar.activation(w.std, w.vareps, ACT.Sqrt).then_inc(s["std"], 1)
                    act.wait_ge(s["t"], n + 1)
                    act.wait_ge(s["v0"], 2 * n)
                    nc.scalar.activation(xt, bank[2], ACT.Copy).then_inc(s["xt"], 1)
                    act.wait_ge(s["lat0"], n + 1)
                    nc.scalar.activation(lat[0:LR], bank[0][0:LR, :], ACT.Copy).then_inc(s["lat"], 1)
                    for which in range(2):
                        m = 2 * n + which
                        act.wait_ge(s["qk"[which]], n + 1)
                        act.wait_ge(s_oq, 16 * 8 * n)
                        src = bank.run(3 + 2 * which, 2).rearrange("p (c t) -> p c t", c=2)
                        nc.scalar.activation(parts[:, which, :, 0, :], src, ACT.Copy).then_inc(s["p1"], 1)
                        act.wait_ge(s["r1"], m + 1)
                        nc.scalar.activation(parts[:, which, :, 1, :], rest, ACT.Copy).then_inc(s["p2"], 1)
                    act.wait_ge(s_ov, 16 * 4 * n)
                    for g in range(2):
                        act.wait_ge(s["v0"], 2 * n + g + 1)
                        nc.scalar.activation(vrow[:, 2 * g:2 * g + 2, :, 0:32],
                                             bank[7].rearrange("p (t h d) -> p t h d", t=2, h=8), ACT.Copy)\
                            .then_inc(s["v"], 1)

        @block.vector
        def _(dve):
            chain = Chain(dve, s["chain"])
            dve.wait_ge(s["w"], 16 * LOADS)
            with dve.Fori(0, B) as b:
                for z in range(2):
                    n = 2 * b + z
                    dve.wait_ge(s["so"], n + 1)
                    dve.wait_ge(s["s2"], n)
                    nc.vector.tensor_tensor(sp1, bank[1].rearrange("p (t d) -> p t d", t=CT),
                                            b_out_sb.unsqueeze(1).broadcast_to([P, CT, D]), ALU.add).then_inc(s["s1"], 1)
                    dve.wait_ge(s["s1"], n + 1)
                    dve.wait_ge(s["sg"], n + 1)
                    dve.wait_ge(s["x1"], n)
                    nc.vector.tensor_tensor(sp2, sp1, sg, ALU.mult).then_inc(s["s2"], 1)
                    dve.wait_ge(s["s2"], n + 1)
                    dve.wait_ge(s_o1[z], 32 * b)
                    dve.wait_ge(s_x[z], 32 * (b + 1))
                    nc.vector.tensor_tensor(x1[z], xs[z], sp2, ALU.add).then_inc(s["x1"], 1)
                    dve.wait_ge(s["x1"], n + 1)
                    w.stat_count = lambda: (CT - 1) * (n + 1)
                    chain.base, chain.n = n * LN_STEPS, 0
                    layernorm(nc, dve, chain, x1[z], xn[z], w, lambda: dve.wait_ge(s["std"], n + 1), s["var"], s["xn"])
                    dve.wait_ge(s["lg"], n + 1)
                    lg = logits.rearrange("p t e -> p (t e)")[:, bass.ds(n * (8 * CT), 8 * CT)]
                    nc.vector.tensor_tensor(lg.rearrange("p (t e) -> p t e", e=8),
                                            bank[1][:, 0:8 * CT].rearrange("p (t e) -> p t e", e=8),
                                            bsw_sb.unsqueeze(1).broadcast_to([P, CT, 8]), ALU.add).then_inc(s["lgo"], 1)
                    for which in range(2):
                        m = 2 * n + which
                        src = bank.run(3 + 2 * which, 2).rearrange("p (c t) -> p c t", c=2)
                        dve.wait_ge(s["p1"], m + 1)
                        dve.wait_ge(s["p2"], m)
                        dve.wait_ge(s["p3"], m)
                        nc.vector.tensor_tensor(rest, src, parts[:, which, :, 0, :], ALU.subtract).then_inc(s["r1"], 1)
                        dve.wait_ge(s["r1"], m + 1)
                        dve.wait_ge(s["p2"], m + 1)
                        nc.vector.tensor_tensor(parts[:, which, :, 2, :], rest, parts[:, which, :, 1, :], ALU.subtract)\
                            .then_inc(s["p3"], 1)
    arena.at = mark



EXPERTS, FF, CAP = 8, 512, B * N // 8


def experts_phase(nc, sem, arena, bank, identf, logits, token, iota8, first_k, ones, xn_dram, w1, b1, w2, b2,
                  slots, answers, gate):
    C = float(np.sqrt(2.0) / 1.41421)
    TE = TILES * EXPERTS
    mark = arena.at
    xs = arena.f32(TILES, D)
    zero = arena.f32(8 * D)
    shape = (TILES, EXPERTS)
    top, den, rden, pmax, ipmax, factor = (arena.f32(TILES) for _ in range(6))
    diff, ex, is_top, cand, onehot, counts, before, ranks, picked = (arena.f32(*shape) for _ in range(9))
    scan = [arena.f32(*shape) for _ in range(2)]
    route, pos, keep, target, home, spill = (arena.f32(TILES) for _ in range(6))
    put = arena.take(TILES).bitcast(U32)
    fetch = arena.take(TILES).bitcast(U32)
    keep_u = arena.take(TILES).bitcast(U32)
    inner = arena.at

    s = {n: sem("x_" + n) for n in "x zero z0 chain count scat t0 t h g y eo ld gather out silu cst b1".split()}
    s_w = [sem(f"x_w{i}") for i in range(2)]
    s_e = [sem(f"x_e{i}") for i in range(2)]

    with nc.Block() as block:

        @block.sync
        def _(sp):
            sp.dma_start(xs, xn_dram.rearrange("t p d -> p t d")).then_inc(s["x"], 16)
            sp.wait_ge(s["z0"], 1)
            for i in range(4):
                sp.dma_start(slots[1024 * i:1024 * (i + 1), :].rearrange("(p r) d -> p (r d)", p=P), zero)\
                    .then_inc(s["zero"], 16)
            sp.wait_ge(s["zero"], 64)

        @block.tensor
        def _(pe):
            pe.wait_ge(s["chain"], STEP_ONEHOT)
            pe.wait_ge(s["cst"], 2)
            flat = onehot.rearrange("p t e -> p (t e)")
            nc.tensor.matmul(bank[0][:, 0:TE], first_k, flat, start=True, stop=True).then_inc(s["count"], 1)
            nc.tensor.matmul(bank[1][:, 0:TE], ones, flat, start=True, stop=True).then_inc(s["count"], 1)

        @block.scalar
        def _(act):
            act.wait_ge(s["chain"], 2)
            nc.scalar.activation(ex, diff, ACT.Exp).then_inc(s["cst"], 1)

        @block.gpsimd
        def _(pool):
            nc.gpsimd.memset(zero, 0.0).then_inc(s["z0"], 1)
            pool.wait_ge(s["x"], 16)
            pool.wait_ge(s["zero"], 64)
            pool.wait_ge(s["ld"], 2)
            for t in range(TILES):
                nc.gpsimd.indirect_dma_start(slots, bass.IndirectOffsetOnAxis(ap=put[:, t:t + 1], axis=0),
                                             xs[:, t, :], None).then_inc(s["scat"], 16)
            pool.wait_ge(s["scat"], 16 * TILES)

        @block.vector
        def _(dve):
            chain = Chain(dve, s["chain"])
            over = lambda a: a.unsqueeze(2).broadcast_to([P, TILES, EXPERTS])
            row = lambda a: a.unsqueeze(1).broadcast_to([P, TILES, EXPERTS])
            v = nc.vector
            chain.step(v.tensor_reduce(top, logits, AX.X, ALU.max))
            chain.step(v.tensor_tensor(diff, logits, over(top), ALU.subtract))
            chain.step(v.tensor_tensor(is_top, logits, over(top), ALU.is_equal))
            chain.step(v.tensor_scalar(cand, is_top, -100.0, 100.0, ALU.mult, ALU.add))
            chain.step(v.tensor_tensor(cand, cand, row(iota8), ALU.add))
            chain.step(v.tensor_reduce(route, cand, AX.X, ALU.min))
            chain.step(v.tensor_tensor(onehot, over(route), row(iota8), ALU.is_equal))
            assert chain.n == STEP_ONEHOT
            dve.wait_ge(s["cst"], 1)
            chain.step(v.tensor_reduce(den, ex, AX.X, ALU.add))
            chain.step(v.reciprocal(pmax, den))
            chain.step(v.reciprocal(ipmax, pmax))
            chain.step(v.tensor_tensor(factor, pmax, ipmax, ALU.mult))
            v.tensor_copy(spill, token).then_inc(s["cst"], 1)
            dve.wait_ge(s["x"], 16)
            v.tensor_tensor(xs, xs, factor.unsqueeze(2).broadcast_to([P, TILES, D]), ALU.mult).then_inc(s["ld"], 1)
            dve.wait_ge(s["count"], 2)
            chain.step(v.tensor_copy(ranks, bank[0][:, 0:TE].rearrange("p (t e) -> p t e", e=EXPERTS)))
            chain.step(v.tensor_copy(counts, bank[1][:, 0:TE].rearrange("p (t e) -> p t e", e=EXPERTS)))
            now, k = counts, 1
            i = 0
            while k < TILES:
                nxt = scan[i % 2]
                chain.step(v.tensor_copy(nxt[:, 0:k, :], now[:, 0:k, :]))
                chain.step(v.tensor_tensor(nxt[:, k:, :], now[:, k:, :], now[:, :TILES - k, :], ALU.add))
                now, k, i = nxt, 2 * k, i + 1
            chain.step(v.tensor_tensor(before, now, counts, ALU.subtract))
            chain.step(v.tensor_tensor(ranks, ranks, before, ALU.add))
            chain.step(v.tensor_tensor(picked, ranks, onehot, ALU.mult))
            chain.step(v.tensor_reduce(pos, picked, AX.X, ALU.add))
            chain.step(v.tensor_scalar(pos, pos, -1.0, None, ALU.add))
            chain.step(v.tensor_scalar(keep, pos, float(CAP), None, ALU.is_lt))
            chain.step(v.tensor_copy(keep_u, keep))
            chain.step(v.scalar_tensor_tensor(home, route, float(CAP), pos, ALU.mult, ALU.add))
            chain.step(v.tensor_scalar(spill, token, float(EXPERTS * CAP), None, ALU.add))
            chain.step(v.tensor_tensor(home, home, spill, ALU.subtract))
            chain.step(v.tensor_tensor(home, home, keep, ALU.mult))
            chain.step(v.tensor_tensor(home, home, spill, ALU.add))
            chain.step(v.tensor_copy(put, home))
            chain.step(v.tensor_scalar(pos, pos, float(CAP - 1), None, ALU.min))
            chain.step(v.scalar_tensor_tensor(target, route, float(CAP), pos, ALU.mult, ALU.add))
            v.tensor_copy(fetch, target).then_inc(s["ld"], 1)

    RB = FF // P
    arena.at = inner
    w1_sb = [arena.f32(FF) for _ in range(2)]
    w2_sb = [arena.f32(RB, D) for _ in range(2)]
    b1_sb = [arena.f32(RB) for _ in range(2)]
    b1c = [arena.f32(RB) for _ in range(2)]
    b2_sb = [arena.f32(D) for _ in range(2)]
    buf = [arena.f32(CT, D) for _ in range(2)]
    buft = arena.f32(CW)
    hid = arena.f32(RB, CW)
    eo = [arena.f32(CT, D) for _ in range(2)]
    with nc.Block() as block:

        @block.sync
        def _(sp):
            def load(e, z):
                one = lambda t: t[bass.ds(e, 1)].rearrange("a p n -> (a p) n")
                sp.dma_start(buf[z], slots[bass.ds(e * CAP, CAP), :].rearrange("(t p) d -> p t d", p=P))\
                    .then_inc(s_w[z], 16)
                sp.dma_start(w1_sb[z], one(w1)).then_inc(s_w[z], 16)
                sp.dma_start(w2_sb[z], one(w2).rearrange("p (c d) -> p c d", c=RB)).then_inc(s_w[z], 16)
                sp.dma_start(b1_sb[z], one(b1)).then_inc(s_w[z], 16)
                sp.dma_start(b2_sb[z], one(b2)).then_inc(s_w[z], 16)

            def store(e, z):
                sp.wait_ge(s["eo"], e + 1)
                sp.dma_start(answers[bass.ds(e * CAP, CAP), :].rearrange("(t p) d -> p t d", p=P), eo[z])\
                    .then_inc(s_e[z], 16)

            load(0, 0)
            load(1, 1)
            with sp.Fori(0, EXPERTS // 2 - 1) as i:
                for z in range(2):
                    store(2 * i + z, z)
                    load(2 * i + z + 2, z)
            store(EXPERTS - 2, 0)
            store(EXPERTS - 1, 1)
            for z in range(2):
                sp.wait_ge(s_e[z], 16 * EXPERTS // 2)

        @block.tensor
        def _(pe):
            with pe.Fori(0, EXPERTS // 2) as i:
                for z in range(2):
                    e = 2 * i + z
                    pe.wait_ge(s_w[z], 80 * (i + 1))
                    pe.wait_ge(s["t"], e)
                    for t in range(CT):
                        last = nc.tensor.transpose(bank[0][:, P * t:P * (t + 1)], buf[z][:, t, :], identf)
                    last.then_inc(s["t0"], 1)
                    pe.wait_ge(s["t"], e + 1)
                    pe.wait_ge(s["g"], RB * e)
                    for r in range(RB):
                        nc.tensor.matmul(bank[1 + r], w1_sb[z][:, P * r:P * (r + 1)], buft, start=True, stop=True)\
                            .then_inc(s["h"], 1)
                    pe.wait_ge(s["g"], RB * (e + 1))
                    pe.wait_ge(s["eo"], e)
                    for t in range(CT):
                        for r in range(RB):
                            last = nc.tensor.matmul(bank[5][:, P * t:P * (t + 1)], hid[:, r, P * t:P * (t + 1)],
                                                    w2_sb[z][:, r, :], start=(r == 0), stop=(r == RB - 1))
                    last.then_inc(s["y"], 1)

        @block.scalar
        def _(act):
            with act.Fori(0, EXPERTS // 2) as i:
                for z in range(2):
                    e = 2 * i + z
                    act.wait_ge(s["t0"], e + 1)
                    act.wait_ge(s["h"], RB * e)
                    nc.scalar.activation(buft, bank[0], ACT.Copy).then_inc(s["t"], 1)
                    act.wait_ge(s["b1"], e + 1)
                    act.wait_ge(s["y"], e)
                    for r in range(RB):
                        act.wait_ge(s["h"], RB * e + r + 1)
                        nc.scalar.activation(hid[:, r, :], bank[1 + r], ACT.Gelu, bias=b1c[z][:, r:r + 1], scale=C)\
                            .then_inc(s["g"], 1)

        @block.vector
        def _(dve):
            with dve.Fori(0, EXPERTS // 2) as i:
                for z in range(2):
                    e = 2 * i + z
                    dve.wait_ge(s_w[z], 80 * (i + 1))
                    dve.wait_ge(s["g"], RB * e)
                    nc.vector.tensor_scalar(b1c[z], b1_sb[z], C, None, ALU.mult).then_inc(s["b1"], 1)
                    dve.wait_ge(s["y"], e + 1)
                    dve.wait_ge(s_e[z], 16 * i)
                    nc.vector.scalar_tensor_tensor(eo[z], bank[5].rearrange("p (t d) -> p t d", t=CT), 1.0 / C,
                                                   b2_sb[z].unsqueeze(1).broadcast_to([P, CT, D]), ALU.mult, ALU.add)\
                        .then_inc(s["eo"], 1)

    arena.at = inner
    got = arena.f32(TILES, D)
    kept = arena.take(TILES * D).bitcast(U32).rearrange("p (t d) -> p t d", d=D)
    with nc.Block() as block:

        @block.gpsimd
        def _(pool):
            for t in range(TILES):
                nc.gpsimd.indirect_dma_start(got[:, t, :], None, answers,
                                             bass.IndirectOffsetOnAxis(ap=fetch[:, t:t + 1], axis=0))\
                    .then_inc(s["gather"], 16)

        @block.vector
        def _(dve):
            nc.vector.tensor_copy(kept, keep_u.unsqueeze(2).broadcast_to([P, TILES, D])).then_inc(s["out"], 1)
            dve.wait_ge(s["out"], 1)
            dve.wait_ge(s["gather"], 16 * TILES)
            nc.vector.copy_predicated(xs, kept, got).then_inc(s["out"], 1)

        @block.scalar
        def _(act):
            act.wait_ge(s["out"], 2)
            nc.scalar.activation(gate, xs, ACT.Silu).then_inc(s["silu"], 1)
    arena.at = mark


STEP_ONEHOT = 7



def final_phase(nc, sem, arena, bank, identf, O, wo, x1, gate, out):
    mark = arena.at
    wo_sb = arena.f32(2, D)
    xs = [arena.f32(CT, D) for _ in range(2)]
    oc = arena.f32(CT, 2, D)
    ot = arena.f32(2, CW)
    m = arena.f32(CT, D)
    outs = [arena.f32(CT, D) for _ in range(2)]
    s = {n: sem("z_" + n) for n in "w oc t ot y m out".split()}
    s_x = [sem(f"z_x{i}") for i in range(2)]
    s_o = [sem(f"z_o{i}") for i in range(2)]
    CHUNKS = 2 * B

    with nc.Block() as block:

        @block.sync
        def _(sp):
            sp.dma_start(wo_sb, wo.rearrange("(c p) n -> p c n", p=P)).then_inc(s["w"], 16)
            with sp.Fori(0, B) as b:
                for z in range(2):
                    n = 2 * b + z
                    sp.wait_ge(s["out"], n)
                    sp.dma_start(xs[z], x1[bass.ds(n * CT, CT), :, :].rearrange("t p d -> p t d")).then_inc(s_x[z], 16)
                    sp.wait_ge(s["out"], n + 1)
                    sp.dma_start(out[bass.ds(b, 1), CW * z:CW * (z + 1), :].rearrange("a (t p) d -> p (a t) d", p=P),
                                 outs[z]).then_inc(s_o[z], 16)
            for z in range(2):
                sp.wait_ge(s_o[z], 16 * B)

        @block.gpsimd
        def _(pool):
            flat = O.rearrange("p u t d -> p (u t d)")
            W = 2 * UR
            with pool.Fori(0, B) as b:
                for z in range(2):
                    n = 2 * b + z
                    pool.wait_ge(s["t"], 2 * n)
                    for g in range(4):
                        src = flat[:, bass.ds(b * (4 * TB * W) + g * TB * W + z * CT * W, CT * W)]
                        nc.gpsimd.tensor_copy(oc.rearrange("p t c d -> p t (c d)")[:, :, W * g:W * (g + 1)],
                                              src.rearrange("p (t d) -> p t d", t=CT)).then_inc(s["oc"], 1)

        @block.tensor
        def _(pe):
            pe.wait_ge(s["w"], 16)
            with pe.Fori(0, B) as b:
                for z in range(2):
                    n = 2 * b + z
                    pe.wait_ge(s["oc"], 4 * (n + 1))
                    for c in range(2):
                        pe.wait_ge(s["ot"], 2 * n + c)
                        for t in range(CT):
                            last = nc.tensor.transpose(bank[c][:, P * t:P * (t + 1)], oc[:, t, c, :], identf)
                        last.then_inc(s["t"], 1)
                    pe.wait_ge(s["ot"], 2 * n + 2)
                    pe.wait_ge(s["m"], n)
                    for t in range(CT):
                        for c in range(2):
                            last = nc.tensor.matmul(bank[2][:, P * t:P * (t + 1)], ot[:, c, P * t:P * (t + 1)],
                                                    wo_sb[:, c, :], start=(c == 0), stop=(c == 1))
                    last.then_inc(s["y"], 1)

        @block.scalar
        def _(act):
            with act.Fori(0, B) as b:
                for z in range(2):
                    n = 2 * b + z
                    for c in range(2):
                        act.wait_ge(s["t"], 2 * n + c + 1)
                        act.wait_ge(s["y"], n)
                        nc.scalar.activation(ot[:, c, :], bank[c], ACT.Copy).then_inc(s["ot"], 1)

        @block.vector
        def _(dve):
            flat = gate.rearrange("p t d -> p (t d)")
            with dve.Fori(0, B) as b:
                for z in range(2):
                    n = 2 * b + z
                    dve.wait_ge(s["y"], n + 1)
                    dve.wait_ge(s["out"], n)
                    nc.vector.tensor_tensor(m.rearrange("p t d -> p (t d)"), bank[2],
                                            flat[:, bass.ds(n * CW, CW)], ALU.mult).then_inc(s["m"], 1)
                    dve.wait_ge(s["m"], n + 1)
                    dve.wait_ge(s_x[z], 16 * (b + 1))
                    dve.wait_ge(s_o[z], 16 * b)
                    nc.vector.tensor_tensor(outs[z], m, xs[z], ALU.add).then_inc(s["out"], 1)
    arena.at = mark



ARENA = 49000


def build(nc, t, out, stop=99):
    with ExitStack() as ctx:
        arena = Arena(ctx.enter_context(nc.sbuf_tensor("arena", [P, ARENA], F32)), ARENA)
        bank = Banks(ctx.enter_context(nc.psum_tensor("banks", [P, 8 * CW], F32)))

        def sem(name):
            return ctx.enter_context(nc.semaphore(name))

        def phase(run, *args):
            own = []

            def own_sem(name):
                own.append(nc.alloc_semaphore(name=name))
                return own[-1]

            run(nc, own_sem, arena, bank, *args)
            nc.all_engine_barrier()
            nc.clear_and_free_semaphores(own)
            nc.all_engine_barrier()

        def scratch(name, shape, dt=F32):
            return nc.dram_tensor(name, shape, dt).ap()

        identf, identb = arena.f32(P), arena.bf16(P)
        wide = arena.f32(2 * TILES * D)
        logits = arena.f32(TILES, EXPERTS)

        R = B * (N + 1)
        stream = scratch("stream", (3, R, D))
        mid = scratch("mid", (R, D))
        qk0, v0 = scratch("qk0", (UNITS, 6, UR, N), BF16), scratch("v0", (UNITS, P, TB, P))
        qk1, v1 = scratch("qk1", (UNITS, 6, 2 * UR, N), BF16), scratch("v1", (UNITS, P, TB, P))
        x1, xn1 = scratch("x1", (TILES, P, D)), scratch("xn1", (TILES, P, D))
        slots, answers = scratch("slots", (2 * B * N, D)), scratch("answers", (B * N, D))

        s_start, s_zero, s_rows, s_identb = sem("start"), sem("zero"), sem("zero_rows"), sem("identb")
        zero = arena.f32(D)
        with nc.Block() as block:
            @block.sync
            def _(sp):
                sp.dma_start(identf, t["identf"]).then_inc(s_start, 16)
                sp.wait_ge(s_start, 16)
                sp.wait_ge(s_zero, 1)
                for dst in (mid, stream[1], stream[2]):
                    sp.dma_start(dst[0:3 * (N + 1) + 1:N + 1, :], zero[0:B, :]).then_inc(s_rows, 16)
                sp.wait_ge(s_rows, 48)

            @block.vector
            def _(dve):
                dve.wait_ge(s_start, 16)
                nc.vector.tensor_copy(identb, identf).then_inc(s_identb, 1)
                dve.wait_ge(s_identb, 1)

            @block.gpsimd
            def _(pool):
                nc.gpsimd.memset(zero, 0.0).then_inc(s_zero, 1)

        O0 = wide[:, 0:TILES * D].rearrange("p (u t d) -> p u t d", u=UNITS, t=TB)
        O1 = wide.rearrange("p (u t d) -> p u t d", u=UNITS, t=TB)
        phase(enter_phase, identf, t["L0_attn_x"], [t[n] for n in ("wq", "wk", "wqs", "wks", "wv")],
                    (t["rope_cos"], t["rope_sin"]), stream[0], qk0, v0)
        if stop > 1:
            phase(attention_phase, identb, identf, "A", 4, 8, qk0, v0, O0)
        if stop > 2:
            with nc.Fori(0, 2) as layer:
                phase(local_attention, identf, layer, stream, mid, t["wqkv"], t["qk_scales"], t["wo"],
                                t["xpos"], t["masks"])
                phase(feed_forward, identf, layer, mid, stream, t["ln_gb"], t["w1"], t["b1"], t["w2"],
                             t["b2"])
        if stop > 3:
            phase(middle_phase, identf, O0, t["w_out"], t["b_out"], t["L0_attn_x"], stream, t["l1_wq"],
                         t["l1_wkd"], t["l1_wku"], t["l1_wvu"], t["l1_wsw"], t["l1_bsw"], x1, xn1, qk1, v1, logits)
        if stop > 4:
            iota8, token, gate = arena.f32(EXPERTS), arena.f32(TILES), arena.f32(TILES, D)
            first_k, ones = arena.f32(P), arena.f32(P)
            s_cst = sem("consts")
            with nc.Block() as block:
                @block.sync
                def _(sp):
                    for dst, name in ((iota8, "iota8"), (token, "token"), (first_k, "first_k"), (ones, "ones")):
                        sp.dma_start(dst, t[name]).then_inc(s_cst, 16)
                    sp.wait_ge(s_cst, 64)
            phase(experts_phase, identf, logits, token, iota8, first_k, ones, xn1, t["l1_w1"],
                          t["l1_b1"], t["l1_w2"], t["l1_b2"], slots, answers, gate)
        if stop > 5:
            phase(attention_phase, identb, identf, "B", 2, 32, qk1, v1, O1)
            phase(final_phase, identf, O1, t["l1_wo"], x1, gate, out)



def layouts(a):
    import numpy as _np
    c = _np.ascontiguousarray
    rep = lambda v: c(_np.broadcast_to(v, (P,) + v.shape))
    w = a["L0_attn_w_qkv"]
    half = (_np.arange(D) // 8) * 8 + (_np.arange(D) % 8 + 4) % 8
    t = {"L0_attn_x": a["L0_attn_x"]}
    t["wq"], t["wk"], t["wv"] = c(w[0:D].T), c(w[D:2 * D].T), c(w[2 * D:].T)
    t["wqs"], t["wks"] = c(w[0:D][half].T), c(w[D:2 * D][half].T)
    t["w_out"], t["b_out"] = c(a["L0_attn_w_out"].T), rep(a["L0_attn_b_out"])
    t["wqkv"], t["wo"], t["w1"] = a["L0_ffn_wqkv"], a["L0_ffn_wo"], a["L0_ffn_w1"]
    t["w2"] = a["L0_ffn_w2"]
    b1 = _np.zeros((2, 2, BLOCKS * HB), _np.float32)
    b1[:, :, :HID] = a["L0_ffn_b1"].reshape(2, 2, HID)
    t["b1"] = c(b1.reshape(2, 2, BLOCKS, HB).transpose(0, 3, 1, 2))
    t["b2"] = c(_np.broadcast_to(a["L0_ffn_b2"][:, None, :], (2, P, D)))
    t["ln_gb"] = c(_np.stack([a["L0_ffn_ln_g"], a["L0_ffn_ln_b"]], axis=-1))
    qk = _np.stack([a["L0_ffn_q_scale"], a["L0_ffn_k_scale"]], axis=1)
    swapped = _np.concatenate([qk[..., DH // 2:], qk[..., :DH // 2]], axis=-1)
    t["qk_scales"] = c(_np.broadcast_to(_np.stack([qk, swapped], axis=1)[:, None], (2, P, 2, 2, DH)))
    t["l1_wq"], t["l1_wkd"] = c(a["L1_attn_Wq"].T), c(a["L1_attn_Wkv_down"].T)
    t["l1_wku"], t["l1_wvu"] = c(a["L1_attn_Wk_up"].T), c(a["L1_attn_Wv_up"].T)
    t["l1_wo"] = c(a["L1_attn_Wo"].T)
    t["l1_wsw"], t["l1_bsw"] = a["L1_ffn_W_sw"], rep(a["L1_ffn_b_sw"])
    t["l1_w1"] = a["L1_ffn_W1"]
    t["l1_b1"] = c(a["L1_ffn_b1"].reshape(EXPERTS, FF // P, P).transpose(0, 2, 1))
    t["l1_w2"] = c(a["L1_ffn_W2"].reshape(EXPERTS, FF // P, P, D).transpose(0, 2, 1, 3).reshape(EXPERTS, P, -1))
    t["l1_b2"] = c(_np.broadcast_to(a["L1_ffn_b2"][:, None, :], (EXPERTS, P, D)))
    return t


def tables():
    import numpy as _np
    f = _np.float32
    c = _np.ascontiguousarray
    t = {}
    inv = f(1.0) / f(10000.0) ** (_np.arange(0, 8, 2, dtype=f) / f(8))
    ang = _np.arange(N, dtype=f)[:, None] * inv[None, :]
    cos, sin = _np.cos(ang).T, _np.sin(ang).T
    t["rope_cos"] = c(_np.tile(_np.concatenate([cos, cos]), (16, 1)).astype(f))
    t["rope_sin"] = c(_np.tile(_np.concatenate([-sin, sin]), (16, 1)).astype(f))
    idx = _np.arange(0, DH, 2, dtype=f)
    inv = f(1.0) / f(10000.0) ** (idx / f(DH))
    pos = _np.arange(N, dtype=f)
    ang = pos[:, None] * inv[None, :]
    base = (idx + f(0.4 * DH)) / f(1.4 * DH)
    scale = base[None, :] ** ((pos - f(N // 2)) / f(WINDOW // 2))[:, None]
    cos, sin = _np.cos(ang), _np.sin(ang)
    both = []
    for q in (True, False):
        m = scale if q else f(1.0) / scale
        both.append((_np.concatenate([cos * m, cos * m], -1), _np.concatenate([-sin * m, sin * m], -1)))
    xpos = _np.stack([_np.stack([b[x] for b in both], 1) for x in range(2)])
    t["xpos"] = c(xpos.reshape(2, TB, P, 2, DH).transpose(2, 0, 1, 3, 4).astype(f))
    k, p = _np.arange(SPAN)[None, :], _np.arange(P)[:, None]
    seen = (k >= p) & (k <= p + WINDOW)
    inside = _np.where(seen, f(0), f(NEG))
    first = _np.where(seen & (k >= WINDOW), f(0), f(NEG))
    t["masks"] = c(_np.stack([first, inside, inside, inside], 1).astype(f))
    t["identf"] = _np.eye(P, dtype=f)
    t["iota8"] = c(_np.tile(_np.arange(EXPERTS, dtype=f), (P, 1)))
    t["token"] = c((_np.arange(TILES)[None, :] * P + _np.arange(P)[:, None]).astype(f))
    t["first_k"] = _np.triu(_np.ones((P, P), f))
    t["ones"] = _np.ones((P, P), f)
    return t


def kernel(**inputs):
    import numpy as _np
    import concourse.bacc as _bacc
    from concourse import mybir as _mybir
    from concourse.bass_utils import run_bass_kernel_spmd as _run

    nc = _bacc.Bacc("TRN2", target_bir_lowering=False, num_devices=1)
    arrays, aps = {}, {}
    for name, a in {**layouts({k: _np.asarray(v) for k, v in inputs.items()}), **tables()}.items():
        a = _np.ascontiguousarray(a)
        arrays[f"in_{name}"] = a
        aps[name] = nc.dram_tensor(f"in_{name}", a.shape, _mybir.dt.from_np(a.dtype), kind="ExternalInput").ap()
    out = nc.dram_tensor("out_0_dram", (B, N, D), _mybir.dt.float32, kind="ExternalOutput").ap()
    build(nc, aps, out)
    r = _run(nc, [arrays], core_ids=[0])
    return r.results[0]["out_0_dram"]
```

```python
from contextlib import ExitStack

import numpy as np
import concourse.bass as bass
from concourse import mybir

F32 = mybir.dt.float32
BF16 = mybir.dt.bfloat16
U32 = mybir.dt.uint32
ALU = mybir.AluOpType
ACT = mybir.ActivationFunctionType
AX = mybir.AxisListType

P = 128
B, N, D = 4, 1024, 128
TB = N // P
TILES = B * TB
CT = 4
CW = CT * P
EPS = 1e-5
UNITS = 16
UR = D // 4


class Arena:

    def __init__(self, tensor, words):
        self.tensor, self.words, self.at = tensor, words, 0

    def take(self, words):
        piece = self.tensor[:, self.at:self.at + words]
        self.at += words + words % 2
        assert self.at <= self.words, f"the SBUF arena is full: {self.at}"
        return piece

    def f32(self, *shape):
        return split(self.take(int(np.prod(shape))), shape)

    def bf16(self, *shape):
        n = int(np.prod(shape))
        return split(self.take((n + 1) // 2).bitcast(BF16)[:, 0:n], shape)


class Banks:

    def __init__(self, tensor):
        self.tensor = tensor

    def __getitem__(self, n):
        return self.tensor[:, CW * n:CW * (n + 1)]

    def run(self, n, count):
        return self.tensor[:, CW * n:CW * (n + count)]


def split(piece, shape):
    if len(shape) == 1:
        return piece
    names = "abcd"[:len(shape)]
    return piece.rearrange(f"p ({' '.join(names)}) -> p {' '.join(names)}", **dict(zip(names[1:], shape[1:])))


class Chain:

    def __init__(self, eng, sem):
        self.eng, self.sem, self.base, self.n = eng, sem, 0, 0

    def step(self, ins):
        self.n += 1
        ins.then_inc(self.sem, 1)
        self.eng.wait_ge(self.sem, self.base + self.n)

    def loop(self, turn, per_turn, before):
        self.base, self.n = before + turn * per_turn, 0



def attention_phase(nc, sem, arena, bank, identb, identf, name, heads, hd, qk_parts, v_rows, out_rows):
    M = P // heads
    sets = 4 // heads
    if sets == 1:
        q_blocks, k_blocks = [[0, 1, 2, 0, 1, 0]], [[0, 0, 0, 1, 1, 2]]
    else:
        q_blocks, k_blocks = [[0, 1, 0], [1, 2, 0]], [[0, 0, 1], [1, 0, 2]]
    KP = 96
    FILLED = len(q_blocks[0]) * hd == KP
    MR = 3
    NL = 2 * sum(len(b) for b in q_blocks) + 1
    scale = float(hd) ** -0.5
    HT = heads * CT
    GROUPS = 2 * TB
    STEPS = GROUPS * heads
    HALF = STEPS // 2
    RING = 2 * heads

    LAG = STEPS * 3 // 16
    extra = {heads + 3: ("out", 1), LAG + 3: ("turn", 1), HALF + heads + 3: ("out", 0), LAG + HALF + 3: ("turn", 0)}
    AHEAD = STEPS - LAG
    FIRST = AHEAD + 1
    JOBS = STEPS + 4

    def plan(first, last):
        jobs = []
        for step in range(STEPS):
            if step < LAG:
                jobs.append((step, "max", AHEAD + step))
            elif not last:
                jobs.append((step, "next", step - LAG))
            if step in extra and not (first and extra[step] == ("out", 1)) and not (last and extra[step] == ("turn", 0)):
                jobs.append((step, *extra[step]))
        return [(step, n + first, kind, which) for n, (step, kind, which) in enumerate(jobs)]

    def id_of(kind, which, last=False):
        return next(n for _, n, k, w in plan(False, last) if (k, w) == (kind, which))

    mark = arena.at
    Q = [arena.bf16(sets, 2, heads, CW) for _ in range(2)]
    K = [arena.bf16(sets, heads, N) for _ in range(2)]
    V = [arena.f32(TB, P) for _ in range(2)]
    probs = arena.f32(RING, CW)
    halfmax = arena.f32(HT, 2)
    negmax = arena.f32(HT)
    rest = arena.f32(2, HT)
    maxall = arena.bf16(P)
    maxparts = maxall[:, 0:MR * HT].rearrange("p (m n) -> p m n", m=MR)
    maxrows = [arena.bf16(P) for _ in range(2)]
    accs = arena.f32(N)
    rden = arena.f32(2, CT * heads)

    s_zeros = sem(name + "_zeros")
    s_cleared = [sem(f"{name}_cleared{i}") for i in range(2)]
    s_load = [sem(f"{name}_load{i}") for i in range(2)]
    s_rows = [[sem(f"{name}_rows{i}{half}") for half in range(2)] for i in range(2)]
    s_job = sem(name + "_job")
    s_jobdone = sem(name + "_jobdone")
    s_parts = sem(name + "_parts")
    s_st = sem(name + "_st")
    s_exp = sem(name + "_exp")
    s_pv = sem(name + "_pv")
    s_acc = sem(name + "_acc")
    s_chain = sem(name + "_chain")

    def sbank(n):
        return bank[n % 3]

    def stbank(n):
        return bank[3 + n % 3]

    acc = [bank[6], bank[7]]

    def turn_free(eng, done, base, n, before, first=0):
        if n >= 3 + first:
            eng.wait_ge(done, base + (n - 2))
        elif before:
            eng.wait_ge(done, base + (first + 1 - before + max(j for j in range(before) if j % 3 == n % 3)))

    LINKS = 6
    CHAIN = 2 * LINKS + 2

    def job_base(u):
        return u * JOBS + (FIRST - 1)

    def arrived(loads, u, s):
        return 16 * loads * (u // 2 + 1) if isinstance(u, int) else (u - s) * (8 * loads) + 16 * loads

    with nc.Block() as block:

        def clear(memset, wait, s):
            pieces = [] if FILLED else [(Q[s][0:KP], 0.0), (K[s][0:KP], 0.0)]
            for n, (rows, value) in enumerate(pieces + [(K[s][KP:P], 1.0)]):
                memset(rows, value).then_inc(s_cleared[s], 1)
                wait(s_cleared[s], n + 1)
        CLEARED = 1 if FILLED else 3

        @block.gpsimd
        def _(pool):
            clear(nc.gpsimd.memset, pool.wait_ge, 1)

        @block.sync
        def _(sp):
            def load(u, s):
                for which, blocks in enumerate((q_blocks, k_blocks)):
                    for st in range(sets):
                        for i, part in enumerate(blocks[st]):
                            src = qk_parts[bass.ds(u, 1), 3 * which + part, :, :]
                            if which == 0:
                                dst = Q[s][hd * i:hd * (i + 1), st, :, :, :]
                                src = src.rearrange("a (h d) (x t) -> (a d) x h t", d=hd, x=2)
                            else:
                                dst = K[s][hd * i:hd * (i + 1), st, :, :]
                                src = src.rearrange("a (h d) t -> (a d) h t", d=hd)
                            sp.dma_start(dst, src).then_inc(s_load[s], 16)

            def load_values(u, s):
                sp.dma_start(V[s], v_rows[bass.ds(u, 1), :, :, :].rearrange("a p c m -> (a p) c m"))\
                    .then_inc(s_load[s], 16)

            def rows(s, half, done):
                sp.wait_ge(s_jobdone, done)
                for m in range(MR):
                    sp.dma_start(Q[s][KP + m:KP + m + 1, sets - 1, half, :, :].rearrange("p h (t q) -> p (h t) q", q=P),
                                 maxrows[half][HT * m:HT * (m + 1), :]).then_inc(s_rows[s][half], 16)

            def unit(u, s, following):
                if following:
                    sp.wait_ge(s_exp, u * STEPS)
                    load(u + 1, 1 - s)
                    sp.wait_ge(s_pv, u * GROUPS)
                    load_values(u + 1, 1 - s)
                rows(s, 1, job_base(u) + id_of("turn", 1, not following) + 1)
                if following:
                    rows(1 - s, 0, job_base(u) + id_of("turn", 0) + 1)

            sp.wait_ge(s_cleared[0], CLEARED)
            load(0, 0)
            load_values(0, 0)
            rows(0, 0, HALF + 4 + 1)
            sp.wait_ge(s_cleared[1], CLEARED)
            unit(0, 0, True)
            with sp.Fori(0, UNITS // 2 - 1) as i:
                unit(2 * i + 1, 1, True)
                unit(2 * i + 2, 0, True)
            unit(UNITS - 1, 1, False)
            sp.wait_ge(s_rows[1][1], 16 * MR * (UNITS // 2))

        @block.tensor
        def _(pe):
            def max_scores(s, k, n, wait):
                half, h, t, keys = k // HALF, k % HALF // (2 * CT), k // 2 % CT, k % 2
                wait()
                nc.tensor.matmul(sbank(n), Q[s][0:KP, 0, half, h, P * t:P * (t + 1)],
                                 K[s][0:KP, 0, h, CW * keys:CW * (keys + 1)], start=True, stop=True).then_inc(s_job, 1)

            def max_transpose(u, half, n, wait):
                pe.wait_ge(s_parts, 2 * u + half + 1)
                wait()
                nc.tensor.transpose(sbank(n)[:, 0:P // 2].bitcast(BF16), maxall, identb).then_inc(s_job, 1)

            def outputs(u, half, n, wait):
                pe.wait_ge(s_acc, 2 * u + half + 1)
                wait()
                for t in range(CT):
                    last = nc.tensor.transpose(sbank(n)[:, P * t:P * (t + 1)],
                                               accs[:, CW * half + P * t:CW * half + P * (t + 1)], identf)
                last.then_inc(s_job, 1)

            def shifted_scores(u, s, step, first):
                half, c, h = step // HALF, step // heads % TB, step % heads
                turn_free(pe, s_exp, STEPS * u, step, 0 if first else STEPS)
                for st in range(sets):
                    rows = KP + MR if st == sets - 1 else KP
                    last = nc.tensor.matmul(stbank(step), K[s][0:rows, st, h, P * c:P * (c + 1)],
                                            Q[s][0:rows, st, half, h, :], start=(st == 0), stop=(st == sets - 1))
                last.then_inc(s_st, 1)

            def values(u, s, g, first):
                half, c = divmod(g, TB)
                pe.wait_ge(s_exp, STEPS * u + heads * (g + 1))
                if c == 0 and not first:
                    pe.wait_ge(s_acc, 2 * u + half - 1)
                for h in range(heads):
                    last = nc.tensor.matmul(acc[half][M * h:M * (h + 1), :], V[s][:, c, M * h:M * (h + 1)],
                                            probs[:, (heads * g + h) % RING, :],
                                            start=(c == 0), stop=(c == TB - 1), tile_position=(0, M * h))
                last.then_inc(s_pv, 1)

            def unit(u, s, before, first=False, last=False):
                base = job_base(u)
                jobs = plan(first, last)
                for step in range(STEPS):
                    if step % HALF == 0:
                        pe.wait_ge(s_rows[s][step // HALF], arrived(MR, u, s))
                    shifted_scores(u, s, step, first)
                    if step == LAG and not last:
                        pe.wait_ge(s_load[1 - s], arrived(NL, u + 1, 1 - s))
                    for _, n, kind, which in (j for j in jobs if j[0] == step):
                        def wait():
                            turn_free(pe, s_jobdone, base, n, before, int(first))
                        if kind == "max":
                            max_scores(s, which, n, wait)
                        elif kind == "next":
                            max_scores(1 - s, which, n, wait)
                        elif kind == "turn":
                            max_transpose(u + 1 - which, which, n, wait)
                        else:
                            outputs(u - which, which, n, wait)
                    if step % heads == heads - 1:
                        if step >= heads:
                            values(u, s, step // heads - 1, first)
                        elif not first:
                            values(u - 1, 1 - s, GROUPS - 1, False)

            pe.wait_ge(s_load[0], 16 * NL)
            n = 0
            for k in range(AHEAD):
                max_scores(0, k, n, lambda: turn_free(pe, s_jobdone, 0, n, 0))
                n += 1
                if k == HALF + 3:
                    max_transpose(0, 0, n, lambda: turn_free(pe, s_jobdone, 0, n, 0))
                    n += 1
            unit(0, 0, FIRST, first=True)
            with pe.Fori(0, UNITS // 2 - 1) as i:
                unit(2 * i + 1, 1, JOBS)
                unit(2 * i + 2, 0, JOBS)
            unit(UNITS - 1, 1, JOBS, last=True)
            values(UNITS - 1, 1, GROUPS - 1, False)
            n = len(plan(False, True))
            outputs(UNITS - 1, 1, n, lambda: turn_free(pe, s_jobdone, job_base(UNITS - 1), n, 0))

        @block.scalar
        def _(act):
            def outputs(u, half, earlier):
                if earlier:
                    act.wait_ge(s_job, job_base(u - 1 + half) + id_of("out", half) + 1)
                act.wait_ge(s_pv, GROUPS * u + TB * (half + 1))
                nc.scalar.activation(accs[:, CW * half:CW * (half + 1)], acc[half], ACT.Copy).then_inc(s_acc, 1)

            def unit(u, second=False, first=False):
                for n in range(STEPS):
                    act.wait_ge(s_st, STEPS * u + n + 1)
                    if n >= RING or not first:
                        act.wait_ge(s_pv, GROUPS * u + n // heads - 1)
                    nc.scalar.activation(probs[:, n % RING, :], stbank(n), ACT.Exp, scale=scale).then_inc(s_exp, 1)
                    if n == heads and not first:
                        outputs(u - 1, 1, not second)
                    if n == HALF + heads:
                        outputs(u, 0, not first)

            unit(0, first=True)
            unit(1, second=True)
            with act.Fori(0, UNITS // 2 - 1) as i:
                unit(2 * i + 2)
                unit(2 * i + 3)
            outputs(UNITS - 1, 1, True)

        @block.vector
        def _(dve):
            chain = Chain(dve, s_chain)
            nc.vector.memset(maxall, 0.0).then_inc(s_zeros, 1)
            clear(nc.vector.memset, dve.wait_ge, 0)
            dve.wait_ge(s_zeros, 1)

            def maxima(k, n, base):
                pair = k % HALF // 2
                nc.vector.tensor_reduce(halfmax[:, pair, k % 2:k % 2 + 1], sbank(n), AX.X, ALU.max)\
                    .then_inc(s_jobdone, 1)
                if k % HALF < HALF - 1:
                    return
                dve.wait_ge(s_jobdone, base + n + 1)
                chain.step(nc.vector.tensor_tensor(negmax, halfmax[:, :, 0], halfmax[:, :, 1], ALU.max))
                chain.step(nc.vector.tensor_scalar(negmax, negmax, -1.0, None, ALU.mult))
                chain.step(nc.vector.tensor_copy(maxparts[:, 0, :], negmax))
                chain.step(nc.vector.tensor_tensor(rest[:, 0, :], negmax, maxparts[:, 0, :], ALU.subtract))
                chain.step(nc.vector.tensor_copy(maxparts[:, 1, :], rest[:, 0, :]))
                chain.step(nc.vector.tensor_tensor(rest[:, 1, :], rest[:, 0, :], maxparts[:, 1, :], ALU.subtract))
                nc.vector.tensor_copy(maxparts[:, 2, :], rest[:, 1, :]).then_inc(s_parts, 1)

            def rows(u, s, half, n, earlier):
                if earlier:
                    dve.wait_ge(s_rows[1 - s][half], arrived(MR, u - 1, 1 - s))
                nc.vector.tensor_copy(maxrows[half], sbank(n)[:, 0:P // 2].bitcast(BF16)).then_inc(s_jobdone, 1)

            def outputs(u, half, n):
                out = sbank(n).rearrange("p (t h m) -> p t h m", t=CT, h=heads)
                rd = rden[:, half, :].rearrange("p (t h) -> p t h", t=CT)
                chain.step(nc.vector.reciprocal(rd, out[:, :, :, hd]))
                dst = out_rows[:, bass.ds(u, 1), CT * half:CT * (half + 1), :]
                nc.vector.tensor_tensor(
                    dst.rearrange("p a t (h d) -> p (a t) h d", d=hd), out[:, :, :, 0:hd],
                    rd.unsqueeze(3).broadcast_to([P, CT, heads, hd]), ALU.mult).then_inc(s_jobdone, 1)

            def unit(u, s, first=False, last=False):
                base = job_base(u)
                for _, n, kind, which in plan(first, last):
                    dve.wait_ge(s_job, base + n + 1)
                    if kind in ("max", "next"):
                        maxima(which, n, base)
                    elif kind == "turn":
                        of = u + 1 - which
                        rows(of, s if which else 1 - s, which, n, not (first and which))
                    else:
                        outputs(u - which, which, n)

            n = 0
            for k in range(AHEAD):
                dve.wait_ge(s_job, n + 1)
                maxima(k, n, 0)
                n += 1
                if k == HALF + 3:
                    dve.wait_ge(s_job, n + 1)
                    rows(0, 0, 0, n, False)
                    n += 1
            unit(0, 0, first=True)
            with dve.Fori(0, UNITS // 2 - 1) as i:
                chain.loop(2 * i, CHAIN, LINKS + CHAIN - 1)
                unit(2 * i + 1, 1)
                chain.loop(2 * i + 1, CHAIN, LINKS + CHAIN - 1)
                unit(2 * i + 2, 0)
            chain.loop(UNITS - 2, CHAIN, LINKS + CHAIN - 1)
            unit(UNITS - 1, 1, last=True)
            n = len(plan(False, True))
            dve.wait_ge(s_job, job_base(UNITS - 1) + n + 1)
            outputs(UNITS - 1, 1, n)
    arena.at = mark



LN_STEPS = 7


def layernorm(nc, dve, chain, x, out, w, std_wait, std_signal, out_sem, eps=EPS):
    for t in range(CT):
        ins = nc.vector.bn_stats(w.stats[:, t, :], x[:, t, :])
        if t < CT - 1:
            ins.then_inc(w.stat_sem, 1)
    chain.step(ins)
    chain.eng.wait_ge(w.stat_sem, w.stat_count())
    even, odd = w.stats[:, :, 1:3], w.stats[:, :, 4:6]
    chain.step(nc.vector.tensor_tensor(w.both, even, odd, ALU.add))
    chain.step(nc.vector.tensor_tensor(w.diff, w.stats[:, :, 1], w.stats[:, :, 4], ALU.subtract))
    chain.step(nc.vector.tensor_tensor(w.diff2, w.diff, w.diff, ALU.mult))
    chain.step(nc.vector.tensor_scalar(w.var, w.both[:, :, 1], 1.0 / D, eps, ALU.mult, ALU.add))
    nc.vector.scalar_tensor_tensor(w.vareps, w.diff2, 0.25, w.var, ALU.mult, ALU.add).then_inc(std_signal, 1)
    chain.step(nc.vector.tensor_scalar(w.mean, w.both[:, :, 0], 0.5, None, ALU.mult))
    std_wait()
    if w.invert is not None:
        chain.step(w.invert())
    for t in range(CT):
        ins = nc.vector.tensor_scalar(out[:, t, :], x[:, t, :], w.mean[:, t:t + 1], w.rstd[:, t:t + 1],
                                      ALU.subtract, ALU.mult)
        ins.then_inc(out_sem, 1)


class NormBuffers:
    def __init__(self, nc, arena, stat_sem):
        self.stats, self.both = arena.f32(CT, 6), arena.f32(CT, 2)
        self.diff, self.diff2, self.var = arena.f32(CT), arena.f32(CT), arena.f32(CT)
        self.vareps, self.mean, self.std, self.rstd = arena.f32(CT), arena.f32(CT), arena.f32(CT), arena.f32(CT)
        self.stat_sem = stat_sem
        self.invert = lambda: nc.vector.reciprocal(self.rstd, self.std)



def enter_phase(nc, sem, arena, bank, identf, x, weights, ropes, xn_out, qk_parts, v_rows):
    mark = arena.at
    w_all = arena.f32(5, D)
    cos, sin = arena.f32(N), arena.f32(N)
    xs = [arena.f32(CT, D) for _ in range(2)]
    xn = [arena.f32(CT, D) for _ in range(2)]
    xt = [arena.f32(CW) for _ in range(2)]
    t1, t2, rot = arena.f32(2, CW), arena.f32(2, CW), arena.f32(2, CW)
    rest = arena.f32(2, CW)
    parts = [arena.bf16(2, 3, CW) for _ in range(2)]
    vrow = [arena.f32(CT, 16, 32) for _ in range(2)]
    zero = arena.f32(D)
    s_stat = sem("e_stat")
    w = NormBuffers(nc, arena, s_stat)

    s_const = sem("e_const")
    s_x = [sem(f"e_x{i}") for i in range(2)]
    s_zero = sem("e_zero")
    s_var, s_std = sem("e_var"), sem("e_std")
    s_xn = sem("e_xn")
    s_xnout = [sem(f"e_xnout{i}") for i in range(2)]
    s_t = sem("e_t")
    s_xt = sem("e_xt")
    s_qk = sem("e_qk")
    s_v = sem("e_v")
    s_vrow = sem("e_vrow")
    s_t12 = sem("e_t12")
    s_rot = sem("e_rot")
    s_p1, s_r1, s_p2, s_p3 = sem("e_p1"), sem("e_r1"), sem("e_p2"), sem("e_p3")
    s_out = [sem(f"e_out{i}") for i in range(2)]
    s_fill = sem("e_fill")
    s_chain = sem("e_chain")
    OUTS = 8
    CHUNKS = 2 * B

    with nc.Block() as block:

        @block.sync
        def _(sp):
            def load(b):
                for s in range(2):
                    sp.dma_start(xs[s], x[bass.ds(b, 1), CW * s:CW * (s + 1), :].rearrange(
                        "a (t p) d -> p (a t) d", p=P)).then_inc(s_x[s], 16)

            def store(b, s):
                n = 2 * b + s
                sp.wait_ge(s_xn, CT * (n + 1))
                sp.dma_start(xn_out[bass.ds(b * (N + 1) + 1 + CW * s, CW), :].rearrange("(t p) d -> p t d", p=P),
                             xn[s]).then_inc(s_xnout[s], 16)
                sp.wait_ge(s_vrow, n + 1)
                for g in range(4):
                    sp.dma_start(v_rows[bass.ds(4 * b + g, 1), :, CT * s:CT * (s + 1), :].rearrange(
                        "a p t m -> (a p) t m"),
                        vrow[s][:, :, 4 * g:4 * g + 4, :].rearrange("p t h m -> p t (h m)")).then_inc(s_out[s], 16)
                sp.wait_ge(s_p3, n + 1)
                sp.wait_ge(s_p2, n + 1)
                for g in range(4):
                    sp.dma_start(qk_parts[bass.ds(4 * b + g, 1), :, :, CW * s:CW * (s + 1)].rearrange(
                        "a n r t -> (a r) n t"),
                        parts[s][UR * g:UR * (g + 1), :, :, :].rearrange("r w n t -> r (w n) t"))\
                        .then_inc(s_out[s], 16)

            for i in range(5):
                sp.dma_start(w_all[:, i, :], weights[i]).then_inc(s_const, 16)
            sp.dma_start(cos, ropes[0]).then_inc(s_const, 16)
            sp.dma_start(sin, ropes[1]).then_inc(s_const, 16)
            load(0)
            sp.wait_ge(s_zero, 1)
            sp.dma_start(xn_out[0:3 * (N + 1) + 1:N + 1, :], zero[0:B, :]).then_inc(s_fill, 16)
            with sp.Fori(0, B - 1) as b:
                store(b, 0)
                sp.wait_ge(s_xn, CT * 2 * (b + 1))
                load(b + 1)
                store(b, 1)
            store(B - 1, 0)
            store(B - 1, 1)
            for s in range(2):
                sp.wait_ge(s_xnout[s], 16 * B)
                sp.wait_ge(s_out[s], 16 * OUTS * B)
            sp.wait_ge(s_fill, 16)

        @block.gpsimd
        def _(pool):
            nc.gpsimd.memset(zero, 0.0).then_inc(s_zero, 1)
            for s in range(2):
                pool.wait_ge(s_zero, 2 * s + 1)
                nc.gpsimd.memset(vrow[s], 0.0).then_inc(s_zero, 1)
                pool.wait_ge(s_zero, 2 * s + 2)
                nc.gpsimd.memset(vrow[s][:, :, :, 8:9], 1.0).then_inc(s_zero, 1)
            with pool.Fori(0, CHUNKS) as n:
                pool.wait_ge(s_t12, 3 * (n + 1))
                pool.wait_ge(s_p1, n)
                pool.wait_ge(s_r1, n)
                nc.gpsimd.tensor_tensor(rot, t1, t2, ALU.add).then_inc(s_rot, 1)

        @block.tensor
        def _(pe):
            pe.wait_ge(s_const, 16 * 7)
            with pe.Fori(0, B) as b:
                for s in range(2):
                    n = 2 * b + s
                    pe.wait_ge(s_xn, CT * (n + 1))
                    for t in range(CT):
                        last = nc.tensor.transpose(bank[0][:, P * t:P * (t + 1)], xn[s][:, t, :], identf)
                    last.then_inc(s_t, 1)
                    pe.wait_ge(s_xt, n + 1)
                    pe.wait_ge(s_t12, 3 * n)
                    for i in range(4):
                        last = nc.tensor.matmul(bank[2 + i], w_all[:, i, :], xt[s], start=True, stop=True)
                    last.then_inc(s_qk, 1)
                    pe.wait_ge(s_vrow, n)
                    for t in range(CT):
                        last = nc.tensor.matmul(bank[1][:, P * t:P * (t + 1)], xt[s][:, P * t:P * (t + 1)],
                                                w_all[:, 4, :], start=True, stop=True)
                    last.then_inc(s_v, 1)

        @block.scalar
        def _(act):
            def root(n):
                act.wait_ge(s_var, n + 1)
                nc.scalar.activation(w.std, w.vareps, ACT.Sqrt).then_inc(s_std, 1)

            def post(b, s):
                n = 2 * b + s
                act.wait_ge(s_t, n + 1)
                nc.scalar.activation(xt[s], bank[0], ACT.Copy).then_inc(s_xt, 1)
                act.wait_ge(s_v, n + 1)
                act.wait_ge(s_out[s], 16 * OUTS * b)
                nc.scalar.activation(vrow[s][:, :, :, 0:8],
                                     bank[1].rearrange("p (t h d) -> p t h d", t=CT, h=16), ACT.Copy).then_inc(s_vrow, 1)
                act.wait_ge(s_rot, n + 1)
                nc.scalar.activation(parts[s][:, :, 0, :], rot, ACT.Copy).then_inc(s_p1, 1)
                act.wait_ge(s_r1, n + 1)
                nc.scalar.activation(parts[s][:, :, 1, :], rest, ACT.Copy).then_inc(s_p2, 1)

            act.wait_ge(s_zero, 5)
            root(0)
            with act.Fori(0, B - 1) as b:
                root(2 * b + 1)
                post(b, 0)
                root(2 * b + 2)
                post(b, 1)
            root(2 * B - 1)
            post(B - 1, 0)
            post(B - 1, 1)

        @block.vector
        def _(dve):
            chain = Chain(dve, s_chain)

            def norm(b, s):
                n = 2 * b + s
                dve.wait_ge(s_x[s], 16 * (b + 1))
                dve.wait_ge(s_t, n)
                dve.wait_ge(s_xnout[s], 16 * b)
                w.stat_count = lambda: (CT - 1) * (n + 1)
                chain.base, chain.n = n * LN_STEPS, 0
                layernorm(nc, dve, chain, xs[s], xn[s], w, lambda: dve.wait_ge(s_std, n + 1), s_var, s_xn)

            def rotate(b, s):
                n = 2 * b + s
                dve.wait_ge(s_qk, n + 1)
                dve.wait_ge(s_rot, n)
                place = slice(CW * s, CW * (s + 1))
                both = bank.run(2, 2).rearrange("p (w t) -> p w t", w=2)
                partner = bank.run(4, 2).rearrange("p (w t) -> p w t", w=2)
                nc.vector.tensor_tensor(t1, both, cos[:, place].unsqueeze(1).broadcast_to([P, 2, CW]), ALU.mult)\
                    .then_inc(s_t12, 1)
                nc.vector.tensor_tensor(t2, partner, sin[:, place].unsqueeze(1).broadcast_to([P, 2, CW]), ALU.mult)\
                    .then_inc(s_t12, 2)
                dve.wait_ge(s_p1, n + 1)
                dve.wait_ge(s_p2, n)
                dve.wait_ge(s_p3, n)
                nc.vector.tensor_tensor(rest, rot, parts[s][:, :, 0, :], ALU.subtract).then_inc(s_r1, 1)
                dve.wait_ge(s_r1, n + 1)
                dve.wait_ge(s_p2, n + 1)
                nc.vector.tensor_tensor(parts[s][:, :, 2, :], rest, parts[s][:, :, 1, :], ALU.subtract).then_inc(s_p3, 1)

            dve.wait_ge(s_const, 16 * 7)
            norm(0, 0)
            with dve.Fori(0, B - 1) as b:
                norm(b, 1)
                rotate(b, 0)
                norm(b + 1, 0)
                rotate(b, 1)
            norm(B - 1, 1)
            rotate(B - 1, 0)
            rotate(B - 1, 1)
    arena.at = mark



HEADS, DH = 8, 64
INNER = HEADS * DH
WINDOW = 64
SPAN = P + WINDOW
HID = 341
NEG = -1e30


def local_attention(nc, sem, arena, bank, identf, identb, layer, stream, mid, wqkv, q_scales, wo, tables, masks):
    mark = arena.at
    PAIRS = HEADS // 2
    G = 4
    R4 = 4
    wq = arena.f32(3, INNER)
    wo_sb = arena.f32(PAIRS, D)
    scales = arena.f32(2, 2, DH)
    tabs = arena.f32(2, TB, 2, DH)
    mask_f = arena.f32(2, 2 * SPAN)
    mask = arena.bf16(2 * 2 * SPAN)
    hs = [arena.f32(D) for _ in range(R4)]
    xs = [arena.f32(D) for _ in range(R4)]
    outs = [arena.f32(D) for _ in range(R4)]
    ht = arena.f32(P)
    sq = arena.f32(2 * HEADS, DH)
    ss, clipped, rnorm = arena.f32(2 * HEADS), arena.f32(2 * HEADS), arena.f32(2 * HEADS)
    power = arena.f32(2 * HEADS)
    t1, t2, rot = arena.f32(2, HEADS, DH), arena.f32(2, HEADS, DH), arena.f32(2, HEADS, DH)
    qk = arena.f32(2, INNER)
    qa, qb = arena.f32(PAIRS, P), arena.f32(PAIRS, P)
    kt = [arena.f32(PAIRS, SPAN) for _ in range(2)]
    v = [arena.f32(INNER) for _ in range(R4)]
    top, negtop, den, rden = arena.f32(HEADS), arena.f32(HEADS), arena.f32(HEADS), arena.f32(HEADS)
    p = arena.f32(HEADS, 2 * P)
    pt = arena.f32(HEADS, 2 * P)
    ot = arena.f32(PAIRS, P)

    s = {n: sem("l_" + n) for n in (
        "w tab clear ht0 ht qkv sq ss clip rn t1 rot qk qt qa kt tail v s top neg e den norm pt pta ptv o ot y "
        "out").split()}
    s_h = [sem(f"l_h{r}") for r in range(R4)]
    s_x = [sem(f"l_x{r}") for r in range(R4)]
    s_o = [sem(f"l_o{r}") for r in range(R4)]
    LOOP = TILES // R4 - 1
    WEIGHTS = 16 * 5

    def shift(q, r, k):
        return q + (r + k) // R4, (r + k) % R4

    def staged(q, r, k):
        y = shift(q, r, k)
        if isinstance(y[0], int) and not 0 <= R4 * y[0] + y[1] < TILES:
            return None
        return y

    def turns(eng, turn):
        for r in range(R4):
            turn(-1, r)
        with eng.Fori(0, LOOP) as q:
            for r in range(R4):
                turn(q, r)
        for r in range(R4):
            turn(LOOP, r)

    with nc.Block() as block:

        @block.sync
        def _(sp):
            def rows(q, r):
                return (R4 * q + r) * P + q // (TB // R4)

            def load_shifted(q, r):
                if not (isinstance(q, int) and q == 0):
                    sp.wait_ge(s["ht0"], R4 * (q - 1) + r + 1)
                for lo, hi, at in ((0, D // 2, 1), (D // 2, D, 0)):
                    sp.dma_start(hs[r][:, lo:hi], stream[bass.ds(layer, 1), bass.ds(rows(q, r) + at, P), lo:hi].rearrange(
                        "a r d -> (a r) d")).then_inc(s_h[r], 16)

            def load(q, r):
                if not (isinstance(q, int) and q == 0):
                    sp.wait_ge(s["out"], R4 * (q - 1) + r + 1)
                sp.dma_start(xs[r], stream[bass.ds(layer, 1), bass.ds(rows(q, r) + 1, P), :].rearrange(
                    "a r d -> (a r) d")).then_inc(s_x[r], 16)

            def store(q, r):
                sp.wait_ge(s["out"], R4 * q + r + 1)
                sp.dma_start(mid[bass.ds(rows(q, r) + 1, P), :], outs[r]).then_inc(s_o[r], 16)

            sp.dma_start(wq, wqkv[bass.ds(layer, 1), :, :].rearrange("a p (w n) -> (a p) w n", w=3)).then_inc(s["w"], 16)
            sp.dma_start(wo_sb, wo[bass.ds(layer, 1), :, :].rearrange("a (c p) n -> (a p) c n", p=P)).then_inc(s["w"], 16)
            sp.dma_start(scales, q_scales[bass.ds(layer, 1), :, :, :, :].rearrange("a p x w d -> (a p) x w d"))\
                .then_inc(s["w"], 16)
            sp.dma_start(tabs, tables).then_inc(s["w"], 16)
            sp.dma_start(mask_f, masks).then_inc(s["w"], 16)

            def turn(q, r):
                for k, what in ((4, load_shifted), (0, store), (4, load)):
                    if staged(q, r, k):
                        what(*staged(q, r, k))

            turns(sp, turn)
            sp.wait_ge(s["w"], WEIGHTS)
            for r in range(R4):
                sp.wait_ge(s_o[r], 16 * TILES // R4)

        @block.gpsimd
        def _(pool):
            n = 0
            for piece, value in ((qa, 0.0), (qb, 0.0), (p, 0.0), (kt[1], 0.0), (v[R4 - 1], 0.0), (power, -0.5)):
                nc.gpsimd.memset(piece, value).then_inc(s["clear"], 1)
                n += 1
                pool.wait_ge(s["clear"], n)

            def rotate(q, r):
                n = R4 * q + r
                pool.wait_ge(s["clip"], n + 1)
                nc.gpsimd.tensor_tensor(rnorm, clipped, power, ALU.pow).then_inc(s["rn"], 1)
                pool.wait_ge(s["t1"], 3 * (n + 1))
                nc.gpsimd.tensor_tensor(rot, t1, t2, ALU.add).then_inc(s["rot"], 1)
                pool.wait_ge(s["rot"], n + 1)
                pool.wait_ge(s["rn"], n + 1)
                pool.wait_ge(s["qt"], n)
                nc.gpsimd.tensor_tensor(
                    qk.rearrange("p w (h d) -> p (w h) d", d=DH), rot.rearrange("p w h d -> p (w h) d"),
                    rnorm.unsqueeze(2).broadcast_to([P, 2 * HEADS, DH]), ALU.mult).then_inc(s["qk"], 1)

            def turn(q, r):
                if staged(q, r, 4):
                    rotate(*staged(q, r, 4))

            turns(pool, turn)

        @block.tensor
        def _(pe):
            def transpose_stream(q, r):
                n = R4 * q + r
                pe.wait_ge(s_h[r], 32 * (q + 1))
                pe.wait_ge(s["v"], n)
                nc.tensor.transpose(bank[2][:, 0:P], hs[r], identf).then_inc(s["ht0"], 1)

            def project(q, r):
                n = R4 * q + r
                pe.wait_ge(s["ht"], n + 1)
                pe.wait_ge(s["t1"], 3 * n)
                pe.wait_ge(s["sq"], n)
                for w in range(2):
                    last = nc.tensor.matmul(bank[w], ht, wq[:, w, :], start=True, stop=True)
                last.then_inc(s["qkv"], 1)
                nc.tensor.matmul(bank[2], ht, wq[:, 2, :], start=True, stop=True).then_inc(s["qkv"], 1)

            def turn_qk(q, r):
                n = R4 * q + r
                pe.wait_ge(s["qk"], n + 1)
                for w in range(2):
                    for c in range(PAIRS):
                        last = nc.tensor.transpose(bank[3 + w][:, P * c:P * (c + 1)], qk[:, w, P * c:P * (c + 1)], identf)
                last.then_inc(s["qt"], 1)

            def scores(q, r, g):
                n = R4 * q + r
                if g == 0:
                    pe.wait_ge(s["qa"], 2 * (n + 1))
                    pe.wait_ge(s["kt"], n + 1)
                    pe.wait_ge(s["tail"], n + 1)
                pe.wait_ge(s["e"], HEADS * n + G * g)
                at = q % (TB // R4) * (2 * SPAN) if r == 0 else 2 * SPAN
                for b in range(2):
                    nc.tensor.matmul(bank[5 + b][:, 0:2 * SPAN], identb, mask[:, bass.ds(at, 2 * SPAN)],
                                     start=True, stop=False)
                    for j in range(2):
                        h = G * g + 2 * b + j
                        last = nc.tensor.matmul(bank[5 + b][:, SPAN * j:SPAN * (j + 1)], (qa, qb)[h % 2][:, h // 2, :],
                                                kt[r % 2][:, h // 2, :], start=False, stop=(j == 1))
                last.then_inc(s["s"], 1)

            def turn_probs(q, r, g):
                n = R4 * q + r
                pe.wait_ge(s["norm"], 2 * n + g + 1)
                if g == 0:
                    pe.wait_ge(s["pta"], 2 * n)
                    pe.wait_ge(s["ptv"], 2 * n)
                elif staged(q, r, 2):
                    pe.wait_ge(s["qa"], 2 * (n + 3))
                    pe.wait_ge(s["kt"], n + 3)
                for j in range(G):
                    for c in range(2):
                        last = nc.tensor.transpose(bank[3 + j // 2][:, 2 * P * (j % 2) + P * c:2 * P * (j % 2) + P * (c + 1)],
                                                   p[:, G * g + j, P * c:P * (c + 1)], identf)
                last.then_inc(s["pt"], 1)

            def values(q, r, g):
                n = R4 * q + r
                pe.wait_ge(s["pta"], 2 * n + g + 1)
                pe.wait_ge(s["ptv"], 2 * n + g + 1)
                if g == 0:
                    pe.wait_ge(s["v"], n + 1)
                    pe.wait_ge(s["out"], n)
                for pair in range(2):
                    for c in range(2):
                        for j in range(2):
                            h = G * g + 2 * pair + j
                            last = nc.tensor.matmul(
                                bank[7][DH * j:DH * (j + 1), P * (h // 2):P * (h // 2 + 1)],
                                v[(r - 1) % R4 if c == 0 else r][:, DH * h:DH * (h + 1)], pt[:, h, P * c:P * (c + 1)],
                                start=(c == 0), stop=(c == 1), tile_position=(0, DH * j))
                last.then_inc(s["o"], 1)

            def project_out(q, r):
                pe.wait_ge(s["ot"], R4 * q + r + 1)
                for c in range(PAIRS):
                    last = nc.tensor.matmul(bank[7][:, 0:D], ot[:, c, :], wo_sb[:, c, :],
                                            start=(c == 0), stop=(c == PAIRS - 1))
                last.then_inc(s["y"], 1)

            def turn(q, r):
                for k, what, more in ((2, scores, (0,)), (0, project_out, ()), (1, turn_probs, (0,)),
                                      (4, transpose_stream, ()), (2, scores, (1,)), (1, values, (0,)), (3, turn_qk, ()),
                                      (4, project, ()), (1, turn_probs, (1,)), (1, values, (1,))):
                    if staged(q, r, k):
                        what(*staged(q, r, k), *more)

            pe.wait_ge(s["w"], WEIGHTS)
            pe.wait_ge(s["clear"], 6)
            pe.wait_ge(s["tab"], 3)
            turns(pe, turn)

        @block.scalar
        def _(act):
            def stream_copy(q, r):
                n = R4 * q + r
                act.wait_ge(s["ht0"], n + 1)
                act.wait_ge(s["qkv"], 2 * n)
                nc.scalar.activation(ht, bank[2][:, 0:P], ACT.Copy).then_inc(s["ht"], 1)

            def squares(q, r):
                n = R4 * q + r
                act.wait_ge(s["qkv"], 2 * n + 1)
                act.wait_ge(s["ss"], n)
                nc.scalar.activation(sq, bank.run(0, 2).rearrange("p (h d) -> p h d", d=DH), ACT.Square)\
                    .then_inc(s["sq"], 1)

            def values_copy(q, r):
                n = R4 * q + r
                act.wait_ge(s["qkv"], 2 * n + 2)
                if not (isinstance(q, int) and q == 0):
                    act.wait_ge(s["o"], 2 * (n - 2))
                nc.scalar.activation(v[r], bank[2], ACT.Copy).then_inc(s["v"], 1)

            def keys(q, r):
                n = R4 * q + r
                act.wait_ge(s["qt"], n + 1)
                act.wait_ge(s["tail"], n)
                nc.scalar.activation(kt[r % 2][:, :, WINDOW:SPAN], bank[4].rearrange("p (c t) -> p c t", c=PAIRS),
                                     ACT.Copy).then_inc(s["kt"], 1)

            def exps(q, r, g):
                n = R4 * q + r
                act.wait_ge(s["neg"], 2 * n + g + 1)
                if not (isinstance(q, int) and R4 * q + r == 0):
                    act.wait_ge(s["pt"], 2 * n + g - 1)
                for j in range(G):
                    h = G * g + j
                    nc.scalar.activation(p[:, h, WINDOW:2 * P], bank[5 + j // 2][:, SPAN * (j % 2):SPAN * (j % 2 + 1)],
                                         ACT.Exp, bias=negtop[:, h:h + 1], scale=8.0, accum_out=den[:, h:h + 1])\
                        .then_inc(s["e"], 1)

            def probs_copy(q, r, g):
                n = R4 * q + r
                act.wait_ge(s["pt"], 2 * n + g + 1)
                act.wait_ge(s["o"], 2 * n)
                nc.scalar.activation(pt[:, G * g:G * g + 2, :], bank[3].rearrange("p (h t) -> p h t", h=2), ACT.Copy)\
                    .then_inc(s["pta"], 1)

            def out_copy(q, r):
                n = R4 * q + r
                act.wait_ge(s["o"], 2 * n + 2)
                act.wait_ge(s["y"], n)
                nc.scalar.activation(ot, bank[7].rearrange("p (c t) -> p c t", c=PAIRS), ACT.Copy).then_inc(s["ot"], 1)

            def turn(q, r):
                for k, what, more in ((1, probs_copy, (0,)), (4, stream_copy, ()), (2, exps, (0,)), (3, keys, ()),
                                      (4, squares, ()), (1, probs_copy, (1,)), (2, exps, (1,)), (1, out_copy, ()),
                                      (4, values_copy, ())):
                    if staged(q, r, k):
                        what(*staged(q, r, k), *more)

            act.wait_ge(s["clear"], 6)
            turns(act, turn)

        @block.vector
        def _(dve):
            def norms(q, r):
                n = R4 * q + r
                dve.wait_ge(s["sq"], n + 1)
                dve.wait_ge(s["rn"], n)
                nc.vector.tensor_reduce(ss, sq, AX.X, ALU.add).then_inc(s["ss"], 1)
                dve.wait_ge(s["ss"], n + 1)
                nc.vector.tensor_scalar(clipped, ss, 1e-24, None, ALU.max).then_inc(s["clip"], 1)
                dve.wait_ge(s["rot"], n)
                t = q % (TB // R4) * R4 + r
                both = bank.run(0, 2).rearrange("p (w h d) -> p w h d", w=2, h=HEADS)
                flat = tabs.rearrange("p x t w d -> p (x t w d)")
                H = DH // 2

                def table(x, lo, hi):
                    one = flat[:, bass.ds(t * (2 * DH) + x * TB * 2 * DH, 2 * DH)].rearrange("p (w d) -> p w d", w=2)
                    return one[:, :, lo:hi].unsqueeze(2).broadcast_to([P, 2, HEADS, hi - lo])

                nc.vector.tensor_tensor(t1, both, table(0, 0, DH), ALU.mult).then_inc(s["t1"], 1)
                nc.vector.tensor_tensor(t2[:, :, :, 0:H], both[:, :, :, H:DH], table(1, 0, H), ALU.mult)\
                    .then_inc(s["t1"], 1)
                nc.vector.tensor_tensor(t2[:, :, :, H:DH], both[:, :, :, 0:H], table(1, H, DH), ALU.mult)\
                    .then_inc(s["t1"], 1)

            def queries(q, r):
                n = R4 * q + r
                dve.wait_ge(s["qt"], n + 1)
                dve.wait_ge(s["s"], 2 * n)
                nc.vector.tensor_copy(qa[0:DH], bank[3][0:DH].rearrange("p (c t) -> p c t", c=PAIRS)).then_inc(s["qa"], 1)
                nc.vector.tensor_copy(qb[DH:P], bank[3][DH:P].rearrange("p (c t) -> p c t", c=PAIRS)).then_inc(s["qa"], 1)
                dve.wait_ge(s["kt"], n)
                nc.vector.tensor_copy(kt[r % 2][:, :, 0:WINDOW], kt[1 - r % 2][:, :, P:SPAN]).then_inc(s["tail"], 1)

            def maxima(q, r, g):
                n = R4 * q + r
                dve.wait_ge(s["s"], 2 * n + g + 1)
                part = slice(G * g, G * (g + 1))
                both = bank.run(5, 2).rearrange("p (b n) -> p b n", b=2)[:, :, 0:2 * SPAN]
                nc.vector.tensor_reduce(top[:, part].rearrange("p (b h) -> p b h", b=2),
                                        both.rearrange("p b (h n) -> p b h n", h=2), AX.X, ALU.max).then_inc(s["top"], 1)
                dve.wait_ge(s["top"], 2 * n + g + 1)
                nc.vector.tensor_scalar(negtop[:, part], top[:, part], -8.0, None, ALU.mult).then_inc(s["neg"], 1)

            def normalize(q, r, g):
                n = R4 * q + r
                dve.wait_ge(s["e"], HEADS * n + G * (g + 1))
                part = slice(G * g, G * (g + 1))
                nc.vector.reciprocal(rden[:, part], den[:, part]).then_inc(s["den"], 1)
                dve.wait_ge(s["den"], 2 * n + g + 1)
                nc.vector.tensor_tensor(p[:, part, WINDOW:2 * P], p[:, part, WINDOW:2 * P],
                                        rden[:, part].unsqueeze(2).broadcast_to([P, G, SPAN]), ALU.mult)\
                    .then_inc(s["norm"], 1)

            def probs_copy(q, r, g):
                n = R4 * q + r
                dve.wait_ge(s["pt"], 2 * n + g + 1)
                dve.wait_ge(s["o"], 2 * n)
                nc.vector.tensor_copy(pt[:, G * g + 2:G * g + 4, :], bank[4].rearrange("p (h t) -> p h t", h=2))\
                    .then_inc(s["ptv"], 1)

            def finish(q, r):
                dve.wait_ge(s["y"], R4 * q + r + 1)
                dve.wait_ge(s_x[r], 16 * (q + 1))
                dve.wait_ge(s_o[r], 16 * q)
                nc.vector.tensor_tensor(outs[r], bank[7][:, 0:D], xs[r], ALU.add).then_inc(s["out"], 1)

            def turn(q, r):
                for k, what, more in ((2, maxima, (0,)), (0, finish, ()), (1, probs_copy, (0,)), (2, maxima, (1,)),
                                      (3, queries, ()), (2, normalize, (0,)), (1, probs_copy, (1,)), (4, norms, ()),
                                      (2, normalize, (1,))):
                    if staged(q, r, k):
                        what(*staged(q, r, k), *more)

            dve.wait_ge(s["w"], WEIGHTS)
            dve.wait_ge(s["clear"], 6)
            for x in range(2):
                nc.vector.tensor_tensor(tabs[:, x], tabs[:, x],
                                        scales[:, x].unsqueeze(1).broadcast_to([P, TB, 2, DH]), ALU.mult)\
                    .then_inc(s["tab"], 1)
            nc.vector.tensor_copy(mask, mask_f.rearrange("p m n -> p (m n)")).then_inc(s["tab"], 1)
            dve.wait_ge(s["tab"], 3)
            turns(dve, turn)
    arena.at = mark


BLOCKS = 3
HB = -(-HID // BLOCKS)


def feed_forward(nc, sem, arena, bank, identf, layer, mid, stream, ln, w1, b1, w2, b2):
    mark = arena.at
    size = [HB, HB, HID - 2 * HB]
    w1_sb = arena.f32(2, HID)
    w2_sb = arena.f32(BLOCKS, D)
    b1_sb = arena.f32(2, BLOCKS)
    b2_sb = arena.f32(D)
    ln_sb = arena.f32(2)
    hs = [arena.f32(CT, D) for _ in range(2)]
    xs = [arena.f32(CT, D) for _ in range(2)]
    hn = arena.f32(CT, D)
    ht = [arena.f32(CW) for _ in range(2)]
    gate = arena.f32(BLOCKS, CW)
    u = arena.f32(BLOCKS, CW)
    xb = [arena.f32(CT, D) for _ in range(2)]
    outs = [arena.f32(CT, D) for _ in range(2)]
    power = arena.f32(CT)
    s = {n: sem("f_" + n) for n in "w power stat chain var std hn t ht a gate u y xb out".split()}
    s_h = [sem(f"f_h{i}") for i in range(2)]
    s_o = [sem(f"f_o{i}") for i in range(2)]
    w = NormBuffers(nc, arena, s["stat"])
    w.invert = None
    CHUNKS = 2 * B
    LOADS = 7

    with nc.Block() as block:

        @block.sync
        def _(sp):
            def load(b, z):
                row = b * (N + 1) + CW * z
                for dst, r, lo, hi in ((hs[z], row + 1, 0, D // 2), (hs[z], row, D // 2, D), (xs[z], row + 1, 0, D)):
                    sp.dma_start(dst[:, :, lo:hi], mid[bass.ds(r, CW), lo:hi].rearrange("(t p) d -> p t d", p=P))\
                        .then_inc(s_h[z], 16)

            def store(b, z):
                sp.wait_ge(s["out"], 2 * b + z + 1)
                sp.dma_start(stream[bass.ds(layer + 1, 1), bass.ds(b * (N + 1) + CW * z + 1, CW), :].rearrange(
                    "a (t p) d -> p (a t) d", p=P), outs[z]).then_inc(s_o[z], 16)

            load(0, 0)
            load(0, 1)
            with sp.Fori(0, B - 1) as b:
                for z in range(2):
                    store(b, z)
                    sp.wait_ge(s["xb"], 2 * b + z + 1)
                    load(b + 1, z)
            store(B - 1, 0)
            store(B - 1, 1)
            for z in range(2):
                sp.wait_ge(s_o[z], 16 * B)

        @block.gpsimd
        def _(pool):
            nc.gpsimd.memset(power, -0.5).then_inc(s["power"], 1)
            pool.wait_ge(s["power"], 1)
            pool.wait_ge(s["w"], 16 * LOADS)
            with pool.Fori(0, B) as b:
                for z in range(2):
                    n = 2 * b + z
                    pool.wait_ge(s["var"], n + 1)
                    pool.wait_ge(s["hn"], CT * n)
                    nc.gpsimd.tensor_tensor(w.rstd, w.vareps, power, ALU.pow).then_inc(s["std"], 1)
                    pool.wait_ge(s_h[z], 48 * (b + 1))
                    pool.wait_ge(s["out"], n)
                    nc.gpsimd.tensor_tensor(xb[z], xs[z], b2_sb.unsqueeze(1).broadcast_to([P, CT, D]), ALU.add)\
                        .then_inc(s["xb"], 1)

        @block.tensor
        def _(pe):
            def turn(n):
                pe.wait_ge(s["hn"], CT * (n + 1))
                pe.wait_ge(s["ht"], n)
                for t in range(CT):
                    last = nc.tensor.transpose(bank[0][:, P * t:P * (t + 1)], hn[:, t, :], identf)
                last.then_inc(s["t"], 1)

            def hidden(n, z):
                pe.wait_ge(s["ht"], n + 1)
                for k in range(BLOCKS):
                    for half in (1, 0):
                        if half == 1:
                            pe.wait_ge(s["gate"], BLOCKS * n)
                        else:
                            pe.wait_ge(s["u"], BLOCKS * n)
                        nc.tensor.matmul(bank[1 + 2 * k + half][0:size[k], :],
                                         w1_sb[:, half, HB * k:HB * k + size[k]], ht[z], start=True, stop=True)\
                            .then_inc(s["a"], 1)

            def output(n):
                pe.wait_ge(s["u"], BLOCKS * (n + 1))
                pe.wait_ge(s["out"], n)
                for t in range(CT):
                    for k in range(BLOCKS):
                        last = nc.tensor.matmul(bank[7][:, P * t:P * (t + 1)], u[0:size[k], k, P * t:P * (t + 1)],
                                                w2_sb[0:size[k], k, :], start=(k == 0), stop=(k == BLOCKS - 1))
                last.then_inc(s["y"], 1)

            pe.wait_ge(s["w"], 16 * LOADS)
            turn(0)
            with pe.Fori(0, B - 1) as b:
                for z in range(2):
                    n = 2 * b + z
                    hidden(n, z)
                    turn(n + 1)
                    output(n)
            n = CHUNKS - 2
            hidden(n, 0)
            turn(n + 1)
            output(n)
            hidden(n + 1, 1)
            output(n + 1)

        @block.scalar
        def _(act):
            def turned(n, z):
                act.wait_ge(s["t"], n + 1)
                act.wait_ge(s["a"], 2 * BLOCKS * n)
                nc.scalar.activation(ht[z], bank[0], ACT.Identity, bias=ln_sb[:, 1:2], scale=ln_sb[:, 0:1])\
                    .then_inc(s["ht"], 1)

            def gates(n):
                for k in range(BLOCKS):
                    act.wait_ge(s["a"], 2 * BLOCKS * n + 2 * k + 1)
                    act.wait_ge(s["u"], BLOCKS * n)
                    r = size[k]
                    nc.scalar.activation(gate[0:r, k, :], bank[2 + 2 * k][0:r, :], ACT.Gelu, bias=b1_sb[0:r, 1, k:k + 1])\
                        .then_inc(s["gate"], 1)

            act.dma_start(w1_sb, w1[bass.ds(layer, 1), :, :].rearrange("a p (w n) -> (a p) w n", w=2)).then_inc(s["w"], 16)
            for k in range(BLOCKS):
                act.dma_start(w2_sb[0:size[k], k, :], w2[bass.ds(layer, 1), HB * k:HB * k + size[k], :].rearrange(
                    "a r n -> (a r) n")).then_inc(s["w"], 16)
            act.dma_start(b1_sb[0:HB], b1[bass.ds(layer, 1), :, :, :].rearrange("a r w k -> (a r) w k")).then_inc(s["w"], 16)
            act.dma_start(b2_sb, b2[bass.ds(layer, 1), :, :].rearrange("a p n -> (a p) n")).then_inc(s["w"], 16)
            act.dma_start(ln_sb, ln[bass.ds(layer, 1), :, :].rearrange("a p n -> (a p) n")).then_inc(s["w"], 16)
            act.wait_ge(s["w"], 16 * LOADS)
            turned(0, 0)
            with act.Fori(0, B - 1) as b:
                for z in range(2):
                    n = 2 * b + z
                    gates(n)
                    turned(n + 1, 1 - z)
            n = CHUNKS - 2
            gates(n)
            turned(n + 1, 1)
            gates(n + 1)

        @block.vector
        def _(dve):
            chain = Chain(dve, s["chain"])
            STEPS = LN_STEPS - 1

            def norm(b, z):
                n = 2 * b + z
                dve.wait_ge(s_h[z], 48 * (b + 1))
                w.stat_count = lambda: (CT - 1) * (n + 1)
                chain.base, chain.n = n * STEPS, 0

                def root():
                    dve.wait_ge(s["std"], n + 1)
                    dve.wait_ge(s["t"], n)
                layernorm(nc, dve, chain, hs[z], hn, w, root, s["var"], s["hn"])

            def post(b, z):
                n = 2 * b + z
                for k in range(BLOCKS):
                    r = size[k]
                    dve.wait_ge(s["gate"], BLOCKS * n + k + 1)
                    dve.wait_ge(s["a"], 2 * BLOCKS * n + 2 * k + 2)
                    dve.wait_ge(s["y"], n)
                    nc.vector.scalar_tensor_tensor(u[0:r, k, :], bank[1 + 2 * k][0:r, :], b1_sb[0:r, 0, k:k + 1],
                                                   gate[0:r, k, :], ALU.add, ALU.mult).then_inc(s["u"], 1)

            def finish(b, z):
                n = 2 * b + z
                dve.wait_ge(s["y"], n + 1)
                dve.wait_ge(s["xb"], n + 1)
                dve.wait_ge(s_o[z], 16 * b)
                nc.vector.tensor_tensor(outs[z], bank[7].rearrange("p (t d) -> p t d", t=CT), xb[z], ALU.add)\
                    .then_inc(s["out"], 1)

            dve.wait_ge(s["w"], 16 * LOADS)
            norm(0, 0)
            with dve.Fori(0, B - 1) as b:
                norm(b, 1)
                post(b, 0)
                finish(b, 0)
                norm(b + 1, 0)
                post(b, 1)
                finish(b, 1)
            norm(B - 1, 1)
            post(B - 1, 0)
            finish(B - 1, 0)
            post(B - 1, 1)
            finish(B - 1, 1)
    arena.at = mark



def middle_phase(nc, sem, arena, bank, identf, O, w_out, b_out, x, stream, wq, wkd, wku, wvu, wsw, bsw,
                 x1_out, xn_out, qk_parts, v_rows, logits):
    mark = arena.at
    E = 2 * D
    LR = 64
    w_out_sb = arena.f32(D)
    b_out_sb = arena.f32(D)
    wq_sb = arena.f32(2, D)
    wkd_sb = arena.f32(LR)
    wku_sb, wvu_sb = arena.f32(2, D), arena.f32(E)
    wsw_sb, bsw_sb = arena.f32(8), arena.f32(8)
    xs = [arena.f32(CT, D) for _ in range(2)]
    gs = [arena.f32(CT, D) for _ in range(2)]
    oc = arena.f32(CT, D)
    ot, sg = arena.f32(CW), arena.f32(CT, D)
    sp1, sp2 = arena.f32(CT, D), arena.f32(CT, D)
    x1 = [arena.f32(CT, D) for _ in range(2)]
    xn = [arena.f32(CT, D) for _ in range(2)]
    xt = arena.f32(CW)
    lat = arena.f32(CW)
    rest = arena.f32(2, CW)
    parts = arena.bf16(2, 2, 3, CW)
    vrow = arena.f32(CT, 8, 64)
    s = {n: sem("m_" + n) for n in ("w stat chain var std clear oc ot0 ot so sg s1 s2 x1 xn t xt q lat0 lat k v0 v "
                                    "lg lgo p1 r1 p2 p3 fill").split()}
    s_x = [sem(f"m_load{i}") for i in range(2)]
    s_o1 = [sem(f"m_o1{i}") for i in range(2)]
    s_oq, s_ov = sem("m_oq"), sem("m_ov")
    w = NormBuffers(nc, arena, s["stat"])
    LOADS = 8
    CHUNKS = 2 * B

    with nc.Block() as block:

        @block.sync
        def _(sp):
            def load(b, z):
                sp.dma_start(xs[z], x[bass.ds(b, 1), CW * z:CW * (z + 1), :].rearrange("a (t p) d -> p (a t) d", p=P))\
                    .then_inc(s_x[z], 16)
                sp.dma_start(gs[z], stream[2, bass.ds(b * (N + 1) + 1 + CW * z, CW), :].rearrange(
                    "(t p) d -> p t d", p=P)).then_inc(s_x[z], 16)

            def store(b, z):
                n = 2 * b + z
                for sig, src, dst in ((s["x1"], x1, x1_out), (s["xn"], xn, xn_out)):
                    sp.wait_ge(sig, (CT if src is xn else 1) * (n + 1))
                    sp.dma_start(dst[bass.ds(n * CT, CT), :, :].rearrange("t p d -> p t d"), src[z])\
                        .then_inc(s_o1[z], 16)
                for which in range(2):
                    sp.wait_ge(s["p3"], 2 * n + which + 1)
                    sp.wait_ge(s["p2"], 2 * n + which + 1)
                    for blk in range(2):
                        for half in range(2):
                            sp.dma_start(
                                qk_parts[bass.ds(4 * b + 2 * blk + half, 1), 3 * which:3 * which + 3, :,
                                         CW * z:CW * (z + 1)].rearrange("a n r t -> (a r) n t"),
                                parts[64 * half:64 * (half + 1), which, blk, :, :]).then_inc(s_oq, 16)
                sp.wait_ge(s["v"], 2 * (n + 1))
                for pair in range(4):
                    sp.dma_start(v_rows[bass.ds(4 * b + pair, 1), :, CT * z:CT * (z + 1), :].rearrange(
                        "a p t m -> (a p) t m"),
                        vrow[:, :, 2 * pair:2 * pair + 2, :].rearrange("p t h m -> p t (h m)")).then_inc(s_ov, 16)

            load(0, 0)
            load(0, 1)
            with sp.Fori(0, B - 1) as b:
                for z in range(2):
                    sp.wait_ge(s["x1"], 2 * b + z + 1)
                    load(b + 1, z)
                    store(b, z)
            store(B - 1, 0)
            store(B - 1, 1)
            for z in range(2):
                sp.wait_ge(s_o1[z], 32 * B)
            sp.wait_ge(s_oq, 16 * 8 * CHUNKS)
            sp.wait_ge(s_ov, 16 * 4 * CHUNKS)

        @block.gpsimd
        def _(pool):
            n = 0
            for piece, value in ((vrow, 0.0), (vrow[:, :, :, 32:33], 1.0), (wku_sb, 0.0), (wvu_sb, 0.0), (lat, 0.0)):
                nc.gpsimd.memset(piece, value).then_inc(s["clear"], 1)
                n += 1
                pool.wait_ge(s["clear"], n)
            flat = O.rearrange("p u t d -> p (u t d)")
            with pool.Fori(0, B) as b:
                for z in range(2):
                    n = 2 * b + z
                    pool.wait_ge(s["ot0"], n)
                    for g in range(4):
                        src = flat[:, bass.ds(b * (4 * TB * UR) + g * TB * UR + z * CT * UR, CT * UR)]
                        ins = nc.gpsimd.tensor_copy(oc[:, :, UR * g:UR * (g + 1)],
                                                    src.rearrange("p (t d) -> p t d", t=CT))
                        ins.then_inc(s["oc"], 1)

        @block.tensor
        def _(pe):
            pe.wait_ge(s["w"], 16 * LOADS)
            pe.wait_ge(s["clear"], 5)
            with pe.Fori(0, B) as b:
                for z in range(2):
                    n = 2 * b + z
                    pe.wait_ge(s["oc"], 4 * (n + 1))
                    pe.wait_ge(s["lat"], n)
                    for t in range(CT):
                        last = nc.tensor.transpose(bank[0][:, P * t:P * (t + 1)], oc[:, t, :], identf)
                    last.then_inc(s["ot0"], 1)
                    pe.wait_ge(s["ot"], n + 1)
                    pe.wait_ge(s["lgo"], n)
                    for t in range(CT):
                        last = nc.tensor.matmul(bank[1][:, P * t:P * (t + 1)], ot[:, P * t:P * (t + 1)], w_out_sb,
                                                start=True, stop=True)
                    last.then_inc(s["so"], 1)
                    pe.wait_ge(s["xn"], CT * (n + 1))
                    for t in range(CT):
                        last = nc.tensor.transpose(bank[2][:, P * t:P * (t + 1)], xn[z][:, t, :], identf)
                    last.then_inc(s["t"], 1)
                    pe.wait_ge(s["xt"], n + 1)
                    pe.wait_ge(s["r1"], 2 * n)
                    pe.wait_ge(s["p1"], 2 * n)
                    for blk in range(2):
                        last = nc.tensor.matmul(bank[3 + blk], wq_sb[:, blk, :], xt, start=True, stop=True)
                    last.then_inc(s["q"], 1)
                    nc.tensor.matmul(bank[0][0:LR, :], wkd_sb, xt, start=True, stop=True).then_inc(s["lat0"], 1)
                    pe.wait_ge(s["s1"], n + 1)
                    for t in range(CT):
                        last = nc.tensor.matmul(bank[1][:, 8 * t:8 * (t + 1)], xt[:, P * t:P * (t + 1)], wsw_sb,
                                                start=True, stop=True)
                    last.then_inc(s["lg"], 1)
                    pe.wait_ge(s["lat"], n + 1)
                    for blk in range(2):
                        last = nc.tensor.matmul(bank[5 + blk], wku_sb[:, blk, :], lat, start=True, stop=True)
                    last.then_inc(s["k"], 1)
                    for g in range(2):
                        pe.wait_ge(s["v"], 2 * n + g)
                        for t in range(2):
                            tt = 2 * g + t
                            last = nc.tensor.matmul(bank[7][:, E * t:E * (t + 1)], lat[:, P * tt:P * (tt + 1)], wvu_sb,
                                                    start=True, stop=True)
                        last.then_inc(s["v0"], 1)

        @block.scalar
        def _(act):
            for dst, src in ((w_out_sb, w_out), (b_out_sb, b_out), (wq_sb, wq.rearrange("p (c n) -> p c n", c=2)),
                             (wkd_sb, wkd), (wsw_sb, wsw), (bsw_sb, bsw)):
                act.dma_start(dst, src).then_inc(s["w"], 16)
            act.wait_ge(s["clear"], 5)
            act.dma_start(wku_sb[0:LR], wku.rearrange("p (c n) -> p c n", c=2)).then_inc(s["w"], 16)
            act.dma_start(wvu_sb[0:LR], wvu).then_inc(s["w"], 16)
            with act.Fori(0, B) as b:
                for z in range(2):
                    n = 2 * b + z
                    act.wait_ge(s_x[z], 32 * (b + 1))
                    act.wait_ge(s["s2"], n)
                    nc.scalar.activation(sg, gs[z], ACT.Silu).then_inc(s["sg"], 1)
                    act.wait_ge(s["ot0"], n + 1)
                    act.wait_ge(s["so"], n)
                    nc.scalar.activation(ot, bank[0], ACT.Copy).then_inc(s["ot"], 1)
                    act.wait_ge(s["var"], n + 1)
                    nc.scalar.activation(w.std, w.vareps, ACT.Sqrt).then_inc(s["std"], 1)
                    act.wait_ge(s["t"], n + 1)
                    act.wait_ge(s["v0"], 2 * n)
                    nc.scalar.activation(xt, bank[2], ACT.Copy).then_inc(s["xt"], 1)
                    act.wait_ge(s["lat0"], n + 1)
                    nc.scalar.activation(lat[0:LR], bank[0][0:LR, :], ACT.Copy).then_inc(s["lat"], 1)
                    for which in range(2):
                        m = 2 * n + which
                        act.wait_ge(s["qk"[which]], n + 1)
                        act.wait_ge(s_oq, 16 * 8 * n)
                        src = bank.run(3 + 2 * which, 2).rearrange("p (c t) -> p c t", c=2)
                        nc.scalar.activation(parts[:, which, :, 0, :], src, ACT.Copy).then_inc(s["p1"], 1)
                        act.wait_ge(s["r1"], m + 1)
                        nc.scalar.activation(parts[:, which, :, 1, :], rest, ACT.Copy).then_inc(s["p2"], 1)
                    act.wait_ge(s_ov, 16 * 4 * n)
                    for g in range(2):
                        act.wait_ge(s["v0"], 2 * n + g + 1)
                        nc.scalar.activation(vrow[:, 2 * g:2 * g + 2, :, 0:32],
                                             bank[7].rearrange("p (t h d) -> p t h d", t=2, h=8), ACT.Copy)\
                            .then_inc(s["v"], 1)

        @block.vector
        def _(dve):
            chain = Chain(dve, s["chain"])
            dve.wait_ge(s["w"], 16 * LOADS)
            with dve.Fori(0, B) as b:
                for z in range(2):
                    n = 2 * b + z
                    dve.wait_ge(s["so"], n + 1)
                    dve.wait_ge(s["s2"], n)
                    nc.vector.tensor_tensor(sp1, bank[1].rearrange("p (t d) -> p t d", t=CT),
                                            b_out_sb.unsqueeze(1).broadcast_to([P, CT, D]), ALU.add).then_inc(s["s1"], 1)
                    dve.wait_ge(s["s1"], n + 1)
                    dve.wait_ge(s["sg"], n + 1)
                    dve.wait_ge(s["x1"], n)
                    nc.vector.tensor_tensor(sp2, sp1, sg, ALU.mult).then_inc(s["s2"], 1)
                    dve.wait_ge(s["s2"], n + 1)
                    dve.wait_ge(s_o1[z], 32 * b)
                    dve.wait_ge(s_x[z], 32 * (b + 1))
                    nc.vector.tensor_tensor(x1[z], xs[z], sp2, ALU.add).then_inc(s["x1"], 1)
                    dve.wait_ge(s["x1"], n + 1)
                    w.stat_count = lambda: (CT - 1) * (n + 1)
                    chain.base, chain.n = n * LN_STEPS, 0
                    layernorm(nc, dve, chain, x1[z], xn[z], w, lambda: dve.wait_ge(s["std"], n + 1), s["var"], s["xn"])
                    dve.wait_ge(s["lg"], n + 1)
                    lg = logits.rearrange("p t e -> p (t e)")[:, bass.ds(n * (8 * CT), 8 * CT)]
                    nc.vector.tensor_tensor(lg.rearrange("p (t e) -> p t e", e=8),
                                            bank[1][:, 0:8 * CT].rearrange("p (t e) -> p t e", e=8),
                                            bsw_sb.unsqueeze(1).broadcast_to([P, CT, 8]), ALU.add).then_inc(s["lgo"], 1)
                    for which in range(2):
                        m = 2 * n + which
                        src = bank.run(3 + 2 * which, 2).rearrange("p (c t) -> p c t", c=2)
                        dve.wait_ge(s["p1"], m + 1)
                        dve.wait_ge(s["p2"], m)
                        dve.wait_ge(s["p3"], m)
                        nc.vector.tensor_tensor(rest, src, parts[:, which, :, 0, :], ALU.subtract).then_inc(s["r1"], 1)
                        dve.wait_ge(s["r1"], m + 1)
                        dve.wait_ge(s["p2"], m + 1)
                        nc.vector.tensor_tensor(parts[:, which, :, 2, :], rest, parts[:, which, :, 1, :], ALU.subtract)\
                            .then_inc(s["p3"], 1)
    arena.at = mark



EXPERTS, FF, CAP = 8, 512, B * N // 8


def experts_phase(nc, sem, arena, bank, identf, logits, token, iota8, first_k, ones, xn_dram, w1, b1, w2, b2,
                  slots, answers, gate):
    C = float(np.sqrt(2.0) / 1.41421)
    TE = TILES * EXPERTS
    mark = arena.at
    xs = arena.f32(TILES, D)
    zero = arena.f32(8 * D)
    shape = (TILES, EXPERTS)
    top, den, rden, pmax, ipmax, factor = (arena.f32(TILES) for _ in range(6))
    diff, ex, is_top, cand, onehot, counts, before, ranks, picked = (arena.f32(*shape) for _ in range(9))
    scan = [arena.f32(*shape) for _ in range(2)]
    route, pos, keep, target, home, spill = (arena.f32(TILES) for _ in range(6))
    put = arena.take(TILES).bitcast(U32)
    fetch = arena.take(TILES).bitcast(U32)
    keep_u = arena.take(TILES).bitcast(U32)
    inner = arena.at

    s = {n: sem("x_" + n) for n in "x zero z0 chain count scat t0 t h g y eo ld gather out silu cst b1".split()}
    s_w = [sem(f"x_w{i}") for i in range(2)]
    s_e = [sem(f"x_e{i}") for i in range(2)]

    with nc.Block() as block:

        @block.sync
        def _(sp):
            sp.dma_start(xs, xn_dram.rearrange("t p d -> p t d")).then_inc(s["x"], 16)
            sp.wait_ge(s["z0"], 1)
            for i in range(4):
                sp.dma_start(slots[1024 * i:1024 * (i + 1), :].rearrange("(p r) d -> p (r d)", p=P), zero)\
                    .then_inc(s["zero"], 16)
            sp.wait_ge(s["zero"], 64)

        @block.tensor
        def _(pe):
            pe.wait_ge(s["chain"], STEP_ONEHOT)
            pe.wait_ge(s["cst"], 2)
            flat = onehot.rearrange("p t e -> p (t e)")
            nc.tensor.matmul(bank[0][:, 0:TE], first_k, flat, start=True, stop=True).then_inc(s["count"], 1)
            nc.tensor.matmul(bank[1][:, 0:TE], ones, flat, start=True, stop=True).then_inc(s["count"], 1)

        @block.scalar
        def _(act):
            act.wait_ge(s["chain"], 2)
            nc.scalar.activation(ex, diff, ACT.Exp).then_inc(s["cst"], 1)

        @block.gpsimd
        def _(pool):
            nc.gpsimd.memset(zero, 0.0).then_inc(s["z0"], 1)
            pool.wait_ge(s["x"], 16)
            pool.wait_ge(s["zero"], 64)
            pool.wait_ge(s["ld"], 2)
            for t in range(TILES):
                nc.gpsimd.indirect_dma_start(slots, bass.IndirectOffsetOnAxis(ap=put[:, t:t + 1], axis=0),
                                             xs[:, t, :], None).then_inc(s["scat"], 16)
            pool.wait_ge(s["scat"], 16 * TILES)

        @block.vector
        def _(dve):
            chain = Chain(dve, s["chain"])
            over = lambda a: a.unsqueeze(2).broadcast_to([P, TILES, EXPERTS])
            row = lambda a: a.unsqueeze(1).broadcast_to([P, TILES, EXPERTS])
            v = nc.vector
            chain.step(v.tensor_reduce(top, logits, AX.X, ALU.max))
            chain.step(v.tensor_tensor(diff, logits, over(top), ALU.subtract))
            chain.step(v.tensor_tensor(is_top, logits, over(top), ALU.is_equal))
            chain.step(v.tensor_scalar(cand, is_top, -100.0, 100.0, ALU.mult, ALU.add))
            chain.step(v.tensor_tensor(cand, cand, row(iota8), ALU.add))
            chain.step(v.tensor_reduce(route, cand, AX.X, ALU.min))
            chain.step(v.tensor_tensor(onehot, over(route), row(iota8), ALU.is_equal))
            assert chain.n == STEP_ONEHOT
            dve.wait_ge(s["cst"], 1)
            chain.step(v.tensor_reduce(den, ex, AX.X, ALU.add))
            chain.step(v.reciprocal(pmax, den))
            chain.step(v.reciprocal(ipmax, pmax))
            chain.step(v.tensor_tensor(factor, pmax, ipmax, ALU.mult))
            v.tensor_copy(spill, token).then_inc(s["cst"], 1)
            dve.wait_ge(s["x"], 16)
            v.tensor_tensor(xs, xs, factor.unsqueeze(2).broadcast_to([P, TILES, D]), ALU.mult).then_inc(s["ld"], 1)
            dve.wait_ge(s["count"], 2)
            chain.step(v.tensor_copy(ranks, bank[0][:, 0:TE].rearrange("p (t e) -> p t e", e=EXPERTS)))
            chain.step(v.tensor_copy(counts, bank[1][:, 0:TE].rearrange("p (t e) -> p t e", e=EXPERTS)))
            now, k = counts, 1
            i = 0
            while k < TILES:
                nxt = scan[i % 2]
                chain.step(v.tensor_copy(nxt[:, 0:k, :], now[:, 0:k, :]))
                chain.step(v.tensor_tensor(nxt[:, k:, :], now[:, k:, :], now[:, :TILES - k, :], ALU.add))
                now, k, i = nxt, 2 * k, i + 1
            chain.step(v.tensor_tensor(before, now, counts, ALU.subtract))
            chain.step(v.tensor_tensor(ranks, ranks, before, ALU.add))
            chain.step(v.tensor_tensor(picked, ranks, onehot, ALU.mult))
            chain.step(v.tensor_reduce(pos, picked, AX.X, ALU.add))
            chain.step(v.tensor_scalar(pos, pos, -1.0, None, ALU.add))
            chain.step(v.tensor_scalar(keep, pos, float(CAP), None, ALU.is_lt))
            chain.step(v.tensor_copy(keep_u, keep))
            chain.step(v.scalar_tensor_tensor(home, route, float(CAP), pos, ALU.mult, ALU.add))
            chain.step(v.tensor_scalar(spill, token, float(EXPERTS * CAP), None, ALU.add))
            chain.step(v.tensor_tensor(home, home, spill, ALU.subtract))
            chain.step(v.tensor_tensor(home, home, keep, ALU.mult))
            chain.step(v.tensor_tensor(home, home, spill, ALU.add))
            chain.step(v.tensor_copy(put, home))
            chain.step(v.tensor_scalar(pos, pos, float(CAP - 1), None, ALU.min))
            chain.step(v.scalar_tensor_tensor(target, route, float(CAP), pos, ALU.mult, ALU.add))
            v.tensor_copy(fetch, target).then_inc(s["ld"], 1)

    RB = FF // P
    arena.at = inner
    w1_sb = [arena.f32(FF) for _ in range(2)]
    w2_sb = [arena.f32(RB, D) for _ in range(2)]
    b1_sb = [arena.f32(RB) for _ in range(2)]
    b1c = [arena.f32(RB) for _ in range(2)]
    b2_sb = [arena.f32(D) for _ in range(2)]
    buf = [arena.f32(CT, D) for _ in range(2)]
    buft = arena.f32(CW)
    hid = arena.f32(RB, CW)
    eo = [arena.f32(CT, D) for _ in range(2)]
    with nc.Block() as block:

        @block.sync
        def _(sp):
            def load(e, z):
                one = lambda t: t[bass.ds(e, 1)].rearrange("a p n -> (a p) n")
                sp.dma_start(buf[z], slots[bass.ds(e * CAP, CAP), :].rearrange("(t p) d -> p t d", p=P))\
                    .then_inc(s_w[z], 16)
                sp.dma_start(w1_sb[z], one(w1)).then_inc(s_w[z], 16)
                sp.dma_start(w2_sb[z], one(w2).rearrange("p (c d) -> p c d", c=RB)).then_inc(s_w[z], 16)
                sp.dma_start(b1_sb[z], one(b1)).then_inc(s_w[z], 16)
                sp.dma_start(b2_sb[z], one(b2)).then_inc(s_w[z], 16)

            def store(e, z):
                sp.wait_ge(s["eo"], e + 1)
                sp.dma_start(answers[bass.ds(e * CAP, CAP), :].rearrange("(t p) d -> p t d", p=P), eo[z])\
                    .then_inc(s_e[z], 16)

            load(0, 0)
            load(1, 1)
            with sp.Fori(0, EXPERTS // 2 - 1) as i:
                for z in range(2):
                    store(2 * i + z, z)
                    load(2 * i + z + 2, z)
            store(EXPERTS - 2, 0)
            store(EXPERTS - 1, 1)
            for z in range(2):
                sp.wait_ge(s_e[z], 16 * EXPERTS // 2)

        @block.tensor
        def _(pe):
            with pe.Fori(0, EXPERTS // 2) as i:
                for z in range(2):
                    e = 2 * i + z
                    pe.wait_ge(s_w[z], 80 * (i + 1))
                    pe.wait_ge(s["t"], e)
                    for t in range(CT):
                        last = nc.tensor.transpose(bank[0][:, P * t:P * (t + 1)], buf[z][:, t, :], identf)
                    last.then_inc(s["t0"], 1)
                    pe.wait_ge(s["t"], e + 1)
                    pe.wait_ge(s["g"], RB * e)
                    for r in range(RB):
                        nc.tensor.matmul(bank[1 + r], w1_sb[z][:, P * r:P * (r + 1)], buft, start=True, stop=True)\
                            .then_inc(s["h"], 1)
                    pe.wait_ge(s["g"], RB * (e + 1))
                    pe.wait_ge(s["eo"], e)
                    for t in range(CT):
                        for r in range(RB):
                            last = nc.tensor.matmul(bank[5][:, P * t:P * (t + 1)], hid[:, r, P * t:P * (t + 1)],
                                                    w2_sb[z][:, r, :], start=(r == 0), stop=(r == RB - 1))
                    last.then_inc(s["y"], 1)

        @block.scalar
        def _(act):
            with act.Fori(0, EXPERTS // 2) as i:
                for z in range(2):
                    e = 2 * i + z
                    act.wait_ge(s["t0"], e + 1)
                    act.wait_ge(s["h"], RB * e)
                    nc.scalar.activation(buft, bank[0], ACT.Copy).then_inc(s["t"], 1)
                    act.wait_ge(s["b1"], e + 1)
                    act.wait_ge(s["y"], e)
                    for r in range(RB):
                        act.wait_ge(s["h"], RB * e + r + 1)
                        nc.scalar.activation(hid[:, r, :], bank[1 + r], ACT.Gelu, bias=b1c[z][:, r:r + 1], scale=C)\
                            .then_inc(s["g"], 1)

        @block.vector
        def _(dve):
            with dve.Fori(0, EXPERTS // 2) as i:
                for z in range(2):
                    e = 2 * i + z
                    dve.wait_ge(s_w[z], 80 * (i + 1))
                    dve.wait_ge(s["g"], RB * e)
                    nc.vector.tensor_scalar(b1c[z], b1_sb[z], C, None, ALU.mult).then_inc(s["b1"], 1)
                    dve.wait_ge(s["y"], e + 1)
                    dve.wait_ge(s_e[z], 16 * i)
                    nc.vector.scalar_tensor_tensor(eo[z], bank[5].rearrange("p (t d) -> p t d", t=CT), 1.0 / C,
                                                   b2_sb[z].unsqueeze(1).broadcast_to([P, CT, D]), ALU.mult, ALU.add)\
                        .then_inc(s["eo"], 1)

    arena.at = inner
    got = arena.f32(TILES, D)
    kept = arena.take(TILES * D).bitcast(U32).rearrange("p (t d) -> p t d", d=D)
    with nc.Block() as block:

        @block.gpsimd
        def _(pool):
            for t in range(TILES):
                nc.gpsimd.indirect_dma_start(got[:, t, :], None, answers,
                                             bass.IndirectOffsetOnAxis(ap=fetch[:, t:t + 1], axis=0))\
                    .then_inc(s["gather"], 16)

        @block.vector
        def _(dve):
            nc.vector.tensor_copy(kept, keep_u.unsqueeze(2).broadcast_to([P, TILES, D])).then_inc(s["out"], 1)
            dve.wait_ge(s["out"], 1)
            dve.wait_ge(s["gather"], 16 * TILES)
            nc.vector.copy_predicated(xs, kept, got).then_inc(s["out"], 1)

        @block.scalar
        def _(act):
            act.wait_ge(s["out"], 2)
            nc.scalar.activation(gate, xs, ACT.Silu).then_inc(s["silu"], 1)
    arena.at = mark


STEP_ONEHOT = 7



def final_phase(nc, sem, arena, bank, identf, O, wo, x1, gate, out):
    mark = arena.at
    wo_sb = arena.f32(2, D)
    xs = [arena.f32(CT, D) for _ in range(2)]
    oc = arena.f32(CT, 2, D)
    ot = arena.f32(2, CW)
    m = arena.f32(CT, D)
    outs = [arena.f32(CT, D) for _ in range(2)]
    s = {n: sem("z_" + n) for n in "w oc t ot y m out".split()}
    s_x = [sem(f"z_x{i}") for i in range(2)]
    s_o = [sem(f"z_o{i}") for i in range(2)]
    CHUNKS = 2 * B

    with nc.Block() as block:

        @block.sync
        def _(sp):
            sp.dma_start(wo_sb, wo.rearrange("(c p) n -> p c n", p=P)).then_inc(s["w"], 16)
            with sp.Fori(0, B) as b:
                for z in range(2):
                    n = 2 * b + z
                    sp.wait_ge(s["out"], n)
                    sp.dma_start(xs[z], x1[bass.ds(n * CT, CT), :, :].rearrange("t p d -> p t d")).then_inc(s_x[z], 16)
                    sp.wait_ge(s["out"], n + 1)
                    sp.dma_start(out[bass.ds(b, 1), CW * z:CW * (z + 1), :].rearrange("a (t p) d -> p (a t) d", p=P),
                                 outs[z]).then_inc(s_o[z], 16)
            for z in range(2):
                sp.wait_ge(s_o[z], 16 * B)

        @block.gpsimd
        def _(pool):
            flat = O.rearrange("p u t d -> p (u t d)")
            W = 2 * UR
            with pool.Fori(0, B) as b:
                for z in range(2):
                    n = 2 * b + z
                    pool.wait_ge(s["t"], 2 * n)
                    for g in range(4):
                        src = flat[:, bass.ds(b * (4 * TB * W) + g * TB * W + z * CT * W, CT * W)]
                        nc.gpsimd.tensor_copy(oc.rearrange("p t c d -> p t (c d)")[:, :, W * g:W * (g + 1)],
                                              src.rearrange("p (t d) -> p t d", t=CT)).then_inc(s["oc"], 1)

        @block.tensor
        def _(pe):
            pe.wait_ge(s["w"], 16)
            with pe.Fori(0, B) as b:
                for z in range(2):
                    n = 2 * b + z
                    pe.wait_ge(s["oc"], 4 * (n + 1))
                    for c in range(2):
                        pe.wait_ge(s["ot"], 2 * n + c)
                        for t in range(CT):
                            last = nc.tensor.transpose(bank[c][:, P * t:P * (t + 1)], oc[:, t, c, :], identf)
                        last.then_inc(s["t"], 1)
                    pe.wait_ge(s["ot"], 2 * n + 2)
                    pe.wait_ge(s["m"], n)
                    for t in range(CT):
                        for c in range(2):
                            last = nc.tensor.matmul(bank[2][:, P * t:P * (t + 1)], ot[:, c, P * t:P * (t + 1)],
                                                    wo_sb[:, c, :], start=(c == 0), stop=(c == 1))
                    last.then_inc(s["y"], 1)

        @block.scalar
        def _(act):
            with act.Fori(0, B) as b:
                for z in range(2):
                    n = 2 * b + z
                    for c in range(2):
                        act.wait_ge(s["t"], 2 * n + c + 1)
                        act.wait_ge(s["y"], n)
                        nc.scalar.activation(ot[:, c, :], bank[c], ACT.Copy).then_inc(s["ot"], 1)

        @block.vector
        def _(dve):
            flat = gate.rearrange("p t d -> p (t d)")
            with dve.Fori(0, B) as b:
                for z in range(2):
                    n = 2 * b + z
                    dve.wait_ge(s["y"], n + 1)
                    dve.wait_ge(s["out"], n)
                    nc.vector.tensor_tensor(m.rearrange("p t d -> p (t d)"), bank[2],
                                            flat[:, bass.ds(n * CW, CW)], ALU.mult).then_inc(s["m"], 1)
                    dve.wait_ge(s["m"], n + 1)
                    dve.wait_ge(s_x[z], 16 * (b + 1))
                    dve.wait_ge(s_o[z], 16 * b)
                    nc.vector.tensor_tensor(outs[z], m, xs[z], ALU.add).then_inc(s["out"], 1)
    arena.at = mark



ARENA = 49000


def build(nc, t, out, stop=99):
    with ExitStack() as ctx:
        arena = Arena(ctx.enter_context(nc.sbuf_tensor("arena", [P, ARENA], F32)), ARENA)
        bank = Banks(ctx.enter_context(nc.psum_tensor("banks", [P, 8 * CW], F32)))

        def sem(name):
            return ctx.enter_context(nc.semaphore(name))

        def phase(run, *args):
            own = []

            def own_sem(name):
                own.append(nc.alloc_semaphore(name=name))
                return own[-1]

            run(nc, own_sem, arena, bank, *args)
            nc.all_engine_barrier()
            nc.clear_and_free_semaphores(own)
            nc.all_engine_barrier()

        def scratch(name, shape, dt=F32):
            return nc.dram_tensor(name, shape, dt).ap()

        identf, identb = arena.f32(P), arena.bf16(P)
        wide = arena.f32(2 * TILES * D)
        logits = arena.f32(TILES, EXPERTS)

        R = B * (N + 1)
        stream = scratch("stream", (3, R, D))
        mid = scratch("mid", (R, D))
        qk0, v0 = scratch("qk0", (UNITS, 6, UR, N), BF16), scratch("v0", (UNITS, P, TB, P))
        qk1, v1 = scratch("qk1", (UNITS, 6, 2 * UR, N), BF16), scratch("v1", (UNITS, P, TB, P))
        x1, xn1 = scratch("x1", (TILES, P, D)), scratch("xn1", (TILES, P, D))
        slots, answers = scratch("slots", (2 * B * N, D)), scratch("answers", (B * N, D))

        s_start, s_zero, s_rows, s_identb = sem("start"), sem("zero"), sem("zero_rows"), sem("identb")
        zero = arena.f32(D)
        with nc.Block() as block:
            @block.sync
            def _(sp):
                sp.dma_start(identf, t["identf"]).then_inc(s_start, 16)
                sp.wait_ge(s_start, 16)
                sp.wait_ge(s_zero, 1)
                for dst in (mid, stream[1], stream[2]):
                    sp.dma_start(dst[0:3 * (N + 1) + 1:N + 1, :], zero[0:B, :]).then_inc(s_rows, 16)
                sp.wait_ge(s_rows, 48)

            @block.vector
            def _(dve):
                dve.wait_ge(s_start, 16)
                nc.vector.tensor_copy(identb, identf).then_inc(s_identb, 1)
                dve.wait_ge(s_identb, 1)

            @block.gpsimd
            def _(pool):
                nc.gpsimd.memset(zero, 0.0).then_inc(s_zero, 1)

        O0 = wide[:, 0:TILES * D].rearrange("p (u t d) -> p u t d", u=UNITS, t=TB)
        O1 = wide.rearrange("p (u t d) -> p u t d", u=UNITS, t=TB)
        phase(enter_phase, identf, t["L0_attn_x"], [t[n] for n in ("wq", "wk", "wqs", "wks", "wv")],
                    (t["rope_cos"], t["rope_sin"]), stream[0], qk0, v0)
        if stop > 1:
            phase(attention_phase, identb, identf, "A", 4, 8, qk0, v0, O0)
        if stop > 2:
            with nc.Fori(0, 2) as layer:
                phase(local_attention, identf, identb, layer, stream, mid, t["wqkv"], t["qk_scales"], t["wo"],
                                t["xpos"], t["masks"])
                phase(feed_forward, identf, layer, mid, stream, t["ln_gb"], t["w1"], t["b1"], t["w2"],
                             t["b2"])
        if stop > 3:
            phase(middle_phase, identf, O0, t["w_out"], t["b_out"], t["L0_attn_x"], stream, t["l1_wq"],
                         t["l1_wkd"], t["l1_wku"], t["l1_wvu"], t["l1_wsw"], t["l1_bsw"], x1, xn1, qk1, v1, logits)
        if stop > 4:
            iota8, token, gate = arena.f32(EXPERTS), arena.f32(TILES), arena.f32(TILES, D)
            first_k, ones = arena.f32(P), arena.f32(P)
            s_cst = sem("consts")
            with nc.Block() as block:
                @block.sync
                def _(sp):
                    for dst, name in ((iota8, "iota8"), (token, "token"), (first_k, "first_k"), (ones, "ones")):
                        sp.dma_start(dst, t[name]).then_inc(s_cst, 16)
                    sp.wait_ge(s_cst, 64)
            phase(experts_phase, identf, logits, token, iota8, first_k, ones, xn1, t["l1_w1"],
                          t["l1_b1"], t["l1_w2"], t["l1_b2"], slots, answers, gate)
        if stop > 5:
            phase(attention_phase, identb, identf, "B", 2, 32, qk1, v1, O1)
            phase(final_phase, identf, O1, t["l1_wo"], x1, gate, out)



def layouts(a):
    import numpy as _np
    c = _np.ascontiguousarray
    rep = lambda v: c(_np.broadcast_to(v, (P,) + v.shape))
    w = a["L0_attn_w_qkv"]
    half = (_np.arange(D) // 8) * 8 + (_np.arange(D) % 8 + 4) % 8
    t = {"L0_attn_x": a["L0_attn_x"]}
    t["wq"], t["wk"], t["wv"] = c(w[0:D].T), c(w[D:2 * D].T), c(w[2 * D:].T)
    t["wqs"], t["wks"] = c(w[0:D][half].T), c(w[D:2 * D][half].T)
    t["w_out"], t["b_out"] = c(a["L0_attn_w_out"].T), rep(a["L0_attn_b_out"])
    t["wqkv"], t["wo"], t["w1"] = a["L0_ffn_wqkv"], a["L0_ffn_wo"], a["L0_ffn_w1"]
    t["w2"] = a["L0_ffn_w2"]
    b1 = _np.zeros((2, 2, BLOCKS * HB), _np.float32)
    b1[:, :, :HID] = a["L0_ffn_b1"].reshape(2, 2, HID)
    t["b1"] = c(b1.reshape(2, 2, BLOCKS, HB).transpose(0, 3, 1, 2))
    t["b2"] = c(_np.broadcast_to(a["L0_ffn_b2"][:, None, :], (2, P, D)))
    t["ln_gb"] = c(_np.stack([a["L0_ffn_ln_g"], a["L0_ffn_ln_b"]], axis=-1))
    qk = _np.stack([a["L0_ffn_q_scale"], a["L0_ffn_k_scale"]], axis=1)
    swapped = _np.concatenate([qk[..., DH // 2:], qk[..., :DH // 2]], axis=-1)
    t["qk_scales"] = c(_np.broadcast_to(_np.stack([qk, swapped], axis=1)[:, None], (2, P, 2, 2, DH)))
    t["l1_wq"], t["l1_wkd"] = c(a["L1_attn_Wq"].T), c(a["L1_attn_Wkv_down"].T)
    t["l1_wku"], t["l1_wvu"] = c(a["L1_attn_Wk_up"].T), c(a["L1_attn_Wv_up"].T)
    t["l1_wo"] = c(a["L1_attn_Wo"].T)
    t["l1_wsw"], t["l1_bsw"] = a["L1_ffn_W_sw"], rep(a["L1_ffn_b_sw"])
    t["l1_w1"] = a["L1_ffn_W1"]
    t["l1_b1"] = c(a["L1_ffn_b1"].reshape(EXPERTS, FF // P, P).transpose(0, 2, 1))
    t["l1_w2"] = c(a["L1_ffn_W2"].reshape(EXPERTS, FF // P, P, D).transpose(0, 2, 1, 3).reshape(EXPERTS, P, -1))
    t["l1_b2"] = c(_np.broadcast_to(a["L1_ffn_b2"][:, None, :], (EXPERTS, P, D)))
    return t


def tables():
    import numpy as _np
    f = _np.float32
    c = _np.ascontiguousarray
    t = {}
    inv = f(1.0) / f(10000.0) ** (_np.arange(0, 8, 2, dtype=f) / f(8))
    ang = _np.arange(N, dtype=f)[:, None] * inv[None, :]
    cos, sin = _np.cos(ang).T, _np.sin(ang).T
    t["rope_cos"] = c(_np.tile(_np.concatenate([cos, cos]), (16, 1)).astype(f))
    t["rope_sin"] = c(_np.tile(_np.concatenate([-sin, sin]), (16, 1)).astype(f))
    idx = _np.arange(0, DH, 2, dtype=f)
    inv = f(1.0) / f(10000.0) ** (idx / f(DH))
    pos = _np.arange(N, dtype=f)
    ang = pos[:, None] * inv[None, :]
    base = (idx + f(0.4 * DH)) / f(1.4 * DH)
    scale = base[None, :] ** ((pos - f(N // 2)) / f(WINDOW // 2))[:, None]
    cos, sin = _np.cos(ang), _np.sin(ang)
    both = []
    for q in (True, False):
        m = scale if q else f(1.0) / scale
        both.append((_np.concatenate([cos * m, cos * m], -1), _np.concatenate([-sin * m, sin * m], -1)))
    xpos = _np.stack([_np.stack([b[x] for b in both], 1) for x in range(2)])
    t["xpos"] = c(xpos.reshape(2, TB, P, 2, DH).transpose(2, 0, 1, 3, 4).astype(f))
    k, p = _np.arange(SPAN)[None, :], _np.arange(P)[:, None]
    seen = (k >= p) & (k <= p + WINDOW)
    inside = _np.where(seen, f(0), f(NEG))
    first = _np.where(seen & (k >= WINDOW), f(0), f(NEG))
    t["masks"] = c(_np.stack([_np.tile(first, 2), _np.tile(inside, 2)], 1).astype(f))
    t["identf"] = _np.eye(P, dtype=f)
    t["iota8"] = c(_np.tile(_np.arange(EXPERTS, dtype=f), (P, 1)))
    t["token"] = c((_np.arange(TILES)[None, :] * P + _np.arange(P)[:, None]).astype(f))
    t["first_k"] = _np.triu(_np.ones((P, P), f))
    t["ones"] = _np.ones((P, P), f)
    return t


def kernel(**inputs):
    import numpy as _np
    import concourse.bacc as _bacc
    from concourse import mybir as _mybir
    from concourse.bass_utils import run_bass_kernel_spmd as _run

    nc = _bacc.Bacc("TRN2", target_bir_lowering=False, num_devices=1)
    arrays, aps = {}, {}
    for name, a in {**layouts({k: _np.asarray(v) for k, v in inputs.items()}), **tables()}.items():
        a = _np.ascontiguousarray(a)
        arrays[f"in_{name}"] = a
        aps[name] = nc.dram_tensor(f"in_{name}", a.shape, _mybir.dt.from_np(a.dtype), kind="ExternalInput").ap()
    out = nc.dram_tensor("out_0_dram", (B, N, D), _mybir.dt.float32, kind="ExternalOutput").ap()
    build(nc, aps, out)
    r = _run(nc, [arrays], core_ids=[0])
    return r.results[0]["out_0_dram"]
```

```python
from contextlib import ExitStack

import numpy as np
import concourse.bass as bass
from concourse import mybir

F32 = mybir.dt.float32
BF16 = mybir.dt.bfloat16
U32 = mybir.dt.uint32
ALU = mybir.AluOpType
ACT = mybir.ActivationFunctionType
AX = mybir.AxisListType

P = 128
B, N, D = 4, 1024, 128
TB = N // P
TILES = B * TB
CT = 4
CW = CT * P
EPS = 1e-5
UNITS = 16
UR = D // 4


class Arena:

    def __init__(self, tensor, words):
        self.tensor, self.words, self.at = tensor, words, 0

    def take(self, words):
        piece = self.tensor[:, self.at:self.at + words]
        self.at += words + words % 2
        assert self.at <= self.words, f"the SBUF arena is full: {self.at}"
        return piece

    def f32(self, *shape):
        return split(self.take(int(np.prod(shape))), shape)

    def bf16(self, *shape):
        n = int(np.prod(shape))
        return split(self.take((n + 1) // 2).bitcast(BF16)[:, 0:n], shape)


class Banks:

    def __init__(self, tensor):
        self.tensor = tensor

    def __getitem__(self, n):
        return self.tensor[:, CW * n:CW * (n + 1)]

    def run(self, n, count):
        return self.tensor[:, CW * n:CW * (n + count)]


def split(piece, shape):
    if len(shape) == 1:
        return piece
    names = "abcd"[:len(shape)]
    return piece.rearrange(f"p ({' '.join(names)}) -> p {' '.join(names)}", **dict(zip(names[1:], shape[1:])))


def later(turn, than=0):
    return not isinstance(turn, int) or turn > than


class Chain:

    def __init__(self, eng, sem):
        self.eng, self.sem, self.base, self.n = eng, sem, 0, 0

    def step(self, ins):
        self.n += 1
        ins.then_inc(self.sem, 1)
        self.eng.wait_ge(self.sem, self.base + self.n)

    def loop(self, turn, per_turn, before):
        self.base, self.n = before + turn * per_turn, 0



def attention_phase(nc, sem, arena, bank, identb, identf, name, heads, hd, qk_parts, v_rows, out_rows, beside=None):
    M = P // heads
    sets = 4 // heads
    if sets == 1:
        q_blocks, k_blocks = [[0, 1, 2, 0, 1, 0]], [[0, 0, 0, 1, 1, 2]]
    else:
        q_blocks, k_blocks = [[0, 1, 0], [1, 2, 0]], [[0, 0, 1], [1, 0, 2]]
    KP = 96
    FILLED = len(q_blocks[0]) * hd == KP
    MR = 3
    NL = 2 * sum(len(b) for b in q_blocks) + 1
    scale = float(hd) ** -0.5
    HT = heads * CT
    GROUPS = 2 * TB
    STEPS = GROUPS * heads
    HALF = STEPS // 2
    RING = 2 * heads

    LAG = STEPS // 4
    extra = {heads + 3: ("out", 1), LAG + heads: ("turn", 1), HALF + heads + 3: ("out", 0), LAG + HALF + heads: ("turn", 0)}
    AHEAD = STEPS - LAG
    FIRST = AHEAD + 1
    JOBS = STEPS + 4

    def plan(first, last):
        jobs = []
        for step in range(STEPS):
            if step < LAG:
                jobs.append((step, "max", AHEAD + step))
            elif not last:
                jobs.append((step, "next", step - LAG))
            if step in extra and not (first and extra[step] == ("out", 1)) and not (last and extra[step] == ("turn", 0)):
                jobs.append((step, *extra[step]))
        return [(step, n + first, kind, which) for n, (step, kind, which) in enumerate(jobs)]

    def id_of(kind, which, last=False):
        return next(n for _, n, k, w in plan(False, last) if (k, w) == (kind, which))

    mark = arena.at
    Q = [arena.bf16(sets, 2, heads, CW) for _ in range(2)]
    K = [arena.bf16(sets, heads, N) for _ in range(2)]
    V = [arena.f32(TB, P) for _ in range(2)]
    probs = arena.f32(RING, CW)
    halfmax = arena.f32(HT, 2)
    rowmax, zeros = arena.f32(HT), arena.f32(HT)
    rest = arena.f32(3, HT)
    maxall = arena.bf16(P)
    maxparts = maxall[:, 0:MR * HT].rearrange("p (m n) -> p m n", m=MR)
    maxrows = [arena.bf16(P) for _ in range(2)]
    accs = arena.f32(N)
    rden = arena.f32(2, CT * heads)

    s_zeros = sem(name + "_zeros")
    s_cleared = [sem(f"{name}_cleared{i}") for i in range(2)]
    s_load = [sem(f"{name}_load{i}") for i in range(2)]
    s_rows = [[sem(f"{name}_rows{i}{half}") for half in range(2)] for i in range(2)]
    s_job = sem(name + "_job")
    s_jobdone = sem(name + "_jobdone")
    s_max = sem(name + "_max")
    s_parts = sem(name + "_parts")
    s_split = sem(name + "_split")
    s_st = sem(name + "_st")
    s_exp = sem(name + "_exp")
    s_pv = sem(name + "_pv")
    s_acc = sem(name + "_acc")
    s_chain = sem(name + "_chain")

    def sbank(n):
        return bank[n % 3]

    def stbank(n):
        return bank[3 + n % 3]

    acc = [bank[6], bank[7]]

    def turn_free(eng, done, base, n, before, first=0):
        if n >= 3 + first:
            eng.wait_ge(done, base + (n - 2))
        elif before:
            eng.wait_ge(done, base + (first + 1 - before + max(j for j in range(before) if j % 3 == n % 3)))

    CHAIN = 2

    def job_base(u):
        return u * JOBS + (FIRST - 1)

    def arrived(loads, u, s):
        return 16 * loads * (u // 2 + 1) if isinstance(u, int) else (u - s) * (8 * loads) + 16 * loads

    with nc.Block() as block:

        def clear(memset, wait, s):
            pieces = [] if FILLED else [(Q[s][0:KP], 0.0), (K[s][0:KP], 0.0)]
            for n, (rows, value) in enumerate(pieces + [(K[s][KP:P], 1.0)]):
                memset(rows, value).then_inc(s_cleared[s], 1)
                wait(s_cleared[s], n + 1)
        CLEARED = 1 if FILLED else 3

        def load(eng, u, s, which):
            blocks = k_blocks if which else q_blocks
            for st in range(sets):
                for i, part in enumerate(blocks[st]):
                    src = qk_parts[bass.ds(u, 1), 3 * which + part, :, :]
                    if which == 0:
                        dst = Q[s][hd * i:hd * (i + 1), st, :, :, :]
                        src = src.rearrange("a (h d) (x t) -> (a d) x h t", d=hd, x=2)
                    else:
                        dst = K[s][hd * i:hd * (i + 1), st, :, :]
                        src = src.rearrange("a (h d) t -> (a d) h t", d=hd)
                    eng.dma_start(dst, src).then_inc(s_load[s], 16)

        @block.gpsimd
        def _(pool):
            for n, piece in enumerate((maxall, zeros)):
                nc.gpsimd.memset(piece, 0.0).then_inc(s_zeros, 1)
                pool.wait_ge(s_zeros, n + 1)
            clear(nc.gpsimd.memset, pool.wait_ge, 1)
            with pool.Fori(0, 2 * UNITS) as j:
                pool.wait_ge(s_max, j + 1)
                nc.gpsimd.tensor_tensor(rest[:, 0, :], zeros, rowmax, ALU.subtract).then_inc(s_split, 1)
                pool.wait_ge(s_split, 5 * j + 1)
                nc.gpsimd.tensor_tensor(maxparts[:, 0, :], rest[:, 0, :], zeros, ALU.subtract).then_inc(s_split, 1)
                pool.wait_ge(s_split, 5 * j + 2)
                nc.gpsimd.tensor_tensor(rest[:, 1, :], rest[:, 0, :], maxparts[:, 0, :], ALU.subtract).then_inc(s_split, 1)
                pool.wait_ge(s_split, 5 * j + 3)
                nc.gpsimd.tensor_tensor(maxparts[:, 1, :], rest[:, 1, :], zeros, ALU.subtract).then_inc(s_split, 1)
                pool.wait_ge(s_split, 5 * j + 4)
                nc.gpsimd.tensor_tensor(rest[:, 2, :], rest[:, 1, :], maxparts[:, 1, :], ALU.subtract).then_inc(s_split, 1)
                pool.wait_ge(s_split, 5 * j + 5)
                nc.gpsimd.tensor_tensor(maxparts[:, 2, :], rest[:, 2, :], zeros, ALU.subtract).then_inc(s_parts, 1)
            if beside:
                beside(pool)

        @block.sync
        def _(sp):
            def load_values(u, s):
                sp.dma_start(V[s], v_rows[bass.ds(u, 1), :, :, :].rearrange("a p c m -> (a p) c m"))\
                    .then_inc(s_load[s], 16)

            def rows(s, half, done):
                sp.wait_ge(s_jobdone, done)
                for m in range(MR):
                    sp.dma_start(Q[s][KP + m:KP + m + 1, sets - 1, half, :, :].rearrange("p h (t q) -> p (h t) q", q=P),
                                 maxrows[half][HT * m:HT * (m + 1), :]).then_inc(s_rows[s][half], 16)

            def unit(u, s, following):
                if following:
                    sp.wait_ge(s_exp, u * STEPS)
                    load(sp, u + 1, 1 - s, 0)
                    load(sp, u + 1, 1 - s, 1)
                    sp.wait_ge(s_pv, u * GROUPS)
                    load_values(u + 1, 1 - s)
                rows(s, 1, job_base(u) + id_of("turn", 1, not following) + 1)
                if following:
                    rows(1 - s, 0, job_base(u) + id_of("turn", 0) + 1)

            if not FILLED:
                sp.wait_ge(s_cleared[0], 1)
            load(sp, 0, 0, 0)
            load_values(0, 0)
            rows(0, 0, HALF + 4 + 1)
            sp.wait_ge(s_cleared[1], CLEARED)
            unit(0, 0, True)
            with sp.Fori(0, UNITS // 2 - 1) as i:
                unit(2 * i + 1, 1, True)
                unit(2 * i + 2, 0, True)
            unit(UNITS - 1, 1, False)
            sp.wait_ge(s_rows[1][1], 16 * MR * (UNITS // 2))

        @block.tensor
        def _(pe):
            def max_scores(s, k, n, wait):
                half, h, t, keys = k // HALF, k % HALF // (2 * CT), k // 2 % CT, k % 2
                wait()
                nc.tensor.matmul(sbank(n), Q[s][0:KP, 0, half, h, P * t:P * (t + 1)],
                                 K[s][0:KP, 0, h, CW * keys:CW * (keys + 1)], start=True, stop=True).then_inc(s_job, 1)

            def max_transpose(u, half, n, wait):
                pe.wait_ge(s_parts, 2 * u + half + 1)
                wait()
                nc.tensor.transpose(sbank(n)[:, 0:P // 2].bitcast(BF16), maxall, identb).then_inc(s_job, 1)

            def outputs(u, half, n, wait):
                pe.wait_ge(s_acc, 2 * u + half + 1)
                wait()
                for t in range(CT):
                    last = nc.tensor.transpose(sbank(n)[:, P * t:P * (t + 1)],
                                               accs[:, CW * half + P * t:CW * half + P * (t + 1)], identf)
                last.then_inc(s_job, 1)

            def shifted_scores(u, s, step, first):
                half, c, h = step // HALF, step // heads % TB, step % heads
                turn_free(pe, s_exp, STEPS * u, step, 0 if first else STEPS)
                for st in range(sets):
                    rows = KP + MR if st == sets - 1 else KP
                    last = nc.tensor.matmul(stbank(step), K[s][0:rows, st, h, P * c:P * (c + 1)],
                                            Q[s][0:rows, st, half, h, :], start=(st == 0), stop=(st == sets - 1))
                last.then_inc(s_st, 1)

            def values(u, s, g, first):
                half, c = divmod(g, TB)
                pe.wait_ge(s_exp, STEPS * u + heads * (g + 1))
                if c == 0 and not first:
                    pe.wait_ge(s_acc, 2 * u + half - 1)
                for h in range(heads):
                    last = nc.tensor.matmul(acc[half][M * h:M * (h + 1), :], V[s][:, c, M * h:M * (h + 1)],
                                            probs[:, (heads * g + h) % RING, :],
                                            start=(c == 0), stop=(c == TB - 1), tile_position=(0, M * h))
                last.then_inc(s_pv, 1)

            def unit(u, s, before, first=False, last=False):
                base = job_base(u)
                jobs = plan(first, last)
                for step in range(STEPS):
                    if step % HALF == 0:
                        pe.wait_ge(s_rows[s][step // HALF], arrived(MR, u, s))
                    shifted_scores(u, s, step, first)
                    if step == LAG and not last:
                        pe.wait_ge(s_load[1 - s], arrived(NL, u + 1, 1 - s))
                    for _, n, kind, which in (j for j in jobs if j[0] == step):
                        def wait():
                            turn_free(pe, s_jobdone, base, n, before, int(first))
                        if kind == "max":
                            max_scores(s, which, n, wait)
                        elif kind == "next":
                            max_scores(1 - s, which, n, wait)
                        elif kind == "turn":
                            max_transpose(u + 1 - which, which, n, wait)
                        else:
                            outputs(u - which, which, n, wait)
                    if step % heads == heads - 1:
                        if step >= heads:
                            values(u, s, step // heads - 1, first)
                        elif not first:
                            values(u - 1, 1 - s, GROUPS - 1, False)

            pe.wait_ge(s_load[0], 16 * NL)
            n = 0
            for k in range(AHEAD):
                max_scores(0, k, n, lambda: turn_free(pe, s_jobdone, 0, n, 0))
                n += 1
                if k == HALF + 3:
                    max_transpose(0, 0, n, lambda: turn_free(pe, s_jobdone, 0, n, 0))
                    n += 1
            unit(0, 0, FIRST, first=True)
            with pe.Fori(0, UNITS // 2 - 1) as i:
                unit(2 * i + 1, 1, JOBS)
                unit(2 * i + 2, 0, JOBS)
            unit(UNITS - 1, 1, JOBS, last=True)
            values(UNITS - 1, 1, GROUPS - 1, False)
            n = len(plan(False, True))
            outputs(UNITS - 1, 1, n, lambda: turn_free(pe, s_jobdone, job_base(UNITS - 1), n, 0))

        @block.scalar
        def _(act):
            def outputs(u, half, earlier):
                if earlier:
                    act.wait_ge(s_job, job_base(u - 1 + half) + id_of("out", half) + 1)
                act.wait_ge(s_pv, GROUPS * u + TB * (half + 1))
                nc.scalar.activation(accs[:, CW * half:CW * (half + 1)], acc[half], ACT.Copy).then_inc(s_acc, 1)

            def unit(u, second=False, first=False):
                for n in range(STEPS):
                    act.wait_ge(s_st, STEPS * u + n + 1)
                    if n >= RING or not first:
                        act.wait_ge(s_pv, GROUPS * u + n // heads - 1)
                    nc.scalar.activation(probs[:, n % RING, :], stbank(n), ACT.Exp, scale=scale).then_inc(s_exp, 1)
                    if n == heads and not first:
                        outputs(u - 1, 1, not second)
                    if n == HALF + heads:
                        outputs(u, 0, not first)

            act.wait_ge(s_cleared[0], CLEARED)
            load(act, 0, 0, 1)
            unit(0, first=True)
            unit(1, second=True)
            with act.Fori(0, UNITS // 2 - 1) as i:
                unit(2 * i + 2)
                unit(2 * i + 3)
            outputs(UNITS - 1, 1, True)

        @block.vector
        def _(dve):
            chain = Chain(dve, s_chain)
            clear(nc.vector.memset, dve.wait_ge, 0)

            def maxima(u, k, n, base):
                pair = k % HALF // 2
                nc.vector.tensor_reduce(halfmax[:, pair, k % 2:k % 2 + 1], sbank(n), AX.X, ALU.max)\
                    .then_inc(s_jobdone, 1)
                if k % HALF < HALF - 1:
                    return
                dve.wait_ge(s_jobdone, base + n + 1)
                j = 2 * u + k // HALF
                dve.wait_ge(s_parts, j)
                nc.vector.tensor_tensor(rowmax, halfmax[:, :, 0], halfmax[:, :, 1], ALU.max).then_inc(s_max, 1)
                dve.wait_ge(s_max, j + 1)

            def rows(u, s, half, n, earlier):
                if earlier:
                    dve.wait_ge(s_rows[1 - s][half], arrived(MR, u - 1, 1 - s))
                nc.vector.tensor_copy(maxrows[half], sbank(n)[:, 0:P // 2].bitcast(BF16)).then_inc(s_jobdone, 1)

            def outputs(u, half, n):
                out = sbank(n).rearrange("p (t h m) -> p t h m", t=CT, h=heads)
                rd = rden[:, half, :].rearrange("p (t h) -> p t h", t=CT)
                chain.step(nc.vector.reciprocal(rd, out[:, :, :, hd]))
                dst = out_rows[:, bass.ds(u, 1), CT * half:CT * (half + 1), :]
                nc.vector.tensor_tensor(
                    dst.rearrange("p a t (h d) -> p (a t) h d", d=hd), out[:, :, :, 0:hd],
                    rd.unsqueeze(3).broadcast_to([P, CT, heads, hd]), ALU.mult).then_inc(s_jobdone, 1)

            def unit(u, s, first=False, last=False):
                base = job_base(u)
                for _, n, kind, which in plan(first, last):
                    dve.wait_ge(s_job, base + n + 1)
                    if kind in ("max", "next"):
                        maxima(u if kind == "max" else u + 1, which, n, base)
                    elif kind == "turn":
                        of = u + 1 - which
                        rows(of, s if which else 1 - s, which, n, not (first and which))
                    else:
                        outputs(u - which, which, n)

            n = 0
            for k in range(AHEAD):
                dve.wait_ge(s_job, n + 1)
                maxima(0, k, n, 0)
                n += 1
                if k == HALF + 3:
                    dve.wait_ge(s_job, n + 1)
                    rows(0, 0, 0, n, False)
                    n += 1
            unit(0, 0, first=True)
            with dve.Fori(0, UNITS // 2 - 1) as i:
                chain.loop(2 * i, CHAIN, CHAIN - 1)
                unit(2 * i + 1, 1)
                chain.loop(2 * i + 1, CHAIN, CHAIN - 1)
                unit(2 * i + 2, 0)
            chain.loop(UNITS - 2, CHAIN, CHAIN - 1)
            unit(UNITS - 1, 1, last=True)
            n = len(plan(False, True))
            dve.wait_ge(s_job, job_base(UNITS - 1) + n + 1)
            outputs(UNITS - 1, 1, n)
    arena.at = mark



LN_STEPS = 7


def layernorm(nc, chain, x, out, w, std_wait, std_signal, out_sem, eps=EPS):
    for t in range(CT):
        ins = nc.vector.bn_stats(w.stats[:, t, :], x[:, t, :])
        if t < CT - 1:
            ins.then_inc(w.stat_sem, 1)
    chain.step(ins)
    chain.eng.wait_ge(w.stat_sem, w.stat_count())
    even, odd = w.stats[:, :, 1:3], w.stats[:, :, 4:6]
    chain.step(nc.vector.tensor_tensor(w.both, even, odd, ALU.add))
    chain.step(nc.vector.tensor_tensor(w.diff, w.stats[:, :, 1], w.stats[:, :, 4], ALU.subtract))
    chain.step(nc.vector.tensor_tensor(w.diff2, w.diff, w.diff, ALU.mult))
    chain.step(nc.vector.tensor_scalar(w.var, w.both[:, :, 1], 1.0 / D, eps, ALU.mult, ALU.add))
    nc.vector.scalar_tensor_tensor(w.vareps, w.diff2, 0.25, w.var, ALU.mult, ALU.add).then_inc(std_signal, 1)
    chain.step(nc.vector.tensor_scalar(w.mean, w.both[:, :, 0], 0.5, None, ALU.mult))
    std_wait()
    if w.invert is not None:
        chain.step(w.invert())
    for t in range(CT):
        ins = nc.vector.tensor_scalar(out[:, t, :], x[:, t, :], w.mean[:, t:t + 1], w.rstd[:, t:t + 1],
                                      ALU.subtract, ALU.mult)
        ins.then_inc(out_sem, 1)


class NormBuffers:
    def __init__(self, nc, arena, stat_sem):
        self.stats, self.both = arena.f32(CT, 6), arena.f32(CT, 2)
        self.diff, self.diff2, self.var = arena.f32(CT), arena.f32(CT), arena.f32(CT)
        self.vareps, self.mean, self.std, self.rstd = arena.f32(CT), arena.f32(CT), arena.f32(CT), arena.f32(CT)
        self.stat_sem = stat_sem
        self.invert = lambda: nc.vector.reciprocal(self.rstd, self.std)



CHUNKS = 2 * B


def chunk(q, r, k):
    b, z = q + (r + k) // 2, (r + k) % 2
    if isinstance(b, int) and not 0 <= b < B:
        return None
    return b, z


def chunk_turns(eng, stages):
    def turn(q, r):
        for k, what in stages:
            if chunk(q, r, k):
                what(*chunk(q, r, k))

    for q in (-2, -1):
        for r in range(2):
            turn(q, r)
    with eng.Fori(0, B - 2) as q:
        for r in range(2):
            turn(q, r)
    for q in (B - 2, B - 1):
        for r in range(2):
            turn(q, r)



def enter_phase(nc, sem, arena, bank, identf, x, weights, ropes, xn_out, qk_parts, v_rows):
    mark = arena.at
    w_all = arena.f32(5, D)
    cos, sin = arena.f32(N), arena.f32(N)
    xs = [arena.f32(CT, D) for _ in range(2)]
    xn = [arena.f32(CT, D) for _ in range(2)]
    xt = [arena.f32(CW) for _ in range(2)]
    t1, t2, rot = arena.f32(2, CW), arena.f32(2, CW), arena.f32(2, CW)
    rest = arena.f32(2, CW)
    parts = [arena.bf16(2, 3, CW) for _ in range(2)]
    vrow = [arena.f32(CT, 16, 32) for _ in range(2)]
    zero = arena.f32(D)
    s_stat = sem("e_stat")
    w = NormBuffers(nc, arena, s_stat)

    s_const = sem("e_const")
    s_x = [sem(f"e_x{i}") for i in range(2)]
    s_zero = sem("e_zero")
    s_var, s_std = sem("e_var"), sem("e_std")
    s_xn = sem("e_xn")
    s_xnout = [sem(f"e_xnout{i}") for i in range(2)]
    s_t = sem("e_t")
    s_xt = sem("e_xt")
    s_qk = sem("e_qk")
    s_v = sem("e_v")
    s_vrow = sem("e_vrow")
    s_t12 = sem("e_t12")
    s_rot = sem("e_rot")
    s_p1, s_r1, s_p2, s_p3 = sem("e_p1"), sem("e_r1"), sem("e_p2"), sem("e_p3")
    s_vout = [sem(f"e_vout{i}") for i in range(2)]
    s_pout = [sem(f"e_pout{i}") for i in range(2)]
    s_fill = sem("e_fill")
    s_chain = sem("e_chain")
    OUTS = 4

    with nc.Block() as block:

        @block.sync
        def _(sp):
            def load(b, s):
                sp.dma_start(xs[s], x[bass.ds(b, 1), CW * s:CW * (s + 1), :].rearrange(
                    "a (t p) d -> p (a t) d", p=P)).then_inc(s_x[s], 16)

            def load_later(b, s):
                if not later(b):
                    return
                sp.wait_ge(s_xn, CT * (2 * b + s - 1))
                load(b, s)

            def store_xn(b, s):
                sp.wait_ge(s_xn, CT * (2 * b + s + 1))
                sp.dma_start(xn_out[bass.ds(b * (N + 1) + 1 + CW * s, CW), :].rearrange("(t p) d -> p t d", p=P),
                             xn[s]).then_inc(s_xnout[s], 16)

            def store_v(b, s):
                sp.wait_ge(s_vrow, 2 * b + s + 1)
                for g in range(4):
                    sp.dma_start(v_rows[bass.ds(4 * b + g, 1), :, CT * s:CT * (s + 1), :].rearrange(
                        "a p t m -> (a p) t m"),
                        vrow[s][:, :, 4 * g:4 * g + 4, :].rearrange("p t h m -> p t (h m)")).then_inc(s_vout[s], 16)

            def store_qk(b, s):
                n = 2 * b + s
                sp.wait_ge(s_p2, n + 1)
                sp.wait_ge(s_p3, n + 1)
                for g in range(4):
                    sp.dma_start(qk_parts[bass.ds(4 * b + g, 1), :, :, CW * s:CW * (s + 1)].rearrange(
                        "a n r t -> (a r) n t"),
                        parts[s][UR * g:UR * (g + 1), :, :, :].rearrange("r w n t -> r (w n) t"))\
                        .then_inc(s_pout[s], 16)

            load(0, 0)
            load(0, 1)
            for i in range(5):
                sp.dma_start(w_all[:, i, :], weights[i]).then_inc(s_const, 16)
            sp.dma_start(cos, ropes[0]).then_inc(s_const, 16)
            sp.dma_start(sin, ropes[1]).then_inc(s_const, 16)
            sp.wait_ge(s_zero, 1)
            sp.dma_start(xn_out[0:3 * (N + 1) + 1:N + 1, :], zero[0:B, :]).then_inc(s_fill, 16)

            chunk_turns(sp, ((4, load_later), (3, store_xn), (1, store_v), (0, store_qk)))
            for s in range(2):
                sp.wait_ge(s_xnout[s], 16 * B)
                sp.wait_ge(s_vout[s], 16 * OUTS * B)
                sp.wait_ge(s_pout[s], 16 * OUTS * B)
            sp.wait_ge(s_fill, 16)

        @block.gpsimd
        def _(pool):
            nc.gpsimd.memset(zero, 0.0).then_inc(s_zero, 1)
            for s in range(2):
                pool.wait_ge(s_zero, 2 * s + 1)
                nc.gpsimd.memset(vrow[s], 0.0).then_inc(s_zero, 1)
                pool.wait_ge(s_zero, 2 * s + 2)
                nc.gpsimd.memset(vrow[s][:, :, :, 8:9], 1.0).then_inc(s_zero, 1)
            with pool.Fori(0, CHUNKS) as n:
                pool.wait_ge(s_t12, 3 * (n + 1))
                pool.wait_ge(s_p1, n)
                pool.wait_ge(s_r1, n)
                nc.gpsimd.tensor_tensor(rot, t1, t2, ALU.add).then_inc(s_rot, 1)

        @block.tensor
        def _(pe):
            def project(b, s):
                n = 2 * b + s
                pe.wait_ge(s_xt, n + 1)
                pe.wait_ge(s_t12, 3 * n)
                for i in range(4):
                    last = nc.tensor.matmul(bank[2 + i], w_all[:, i, :], xt[s], start=True, stop=True)
                last.then_inc(s_qk, 1)
                pe.wait_ge(s_vrow, n)
                for t in range(CT):
                    last = nc.tensor.matmul(bank[1][:, P * t:P * (t + 1)], xt[s][:, P * t:P * (t + 1)],
                                            w_all[:, 4, :], start=True, stop=True)
                last.then_inc(s_v, 1)

            def turn_stream(b, s):
                n = 2 * b + s
                pe.wait_ge(s_xn, CT * (n + 1))
                pe.wait_ge(s_xt, n)
                for t in range(CT):
                    last = nc.tensor.transpose(bank[0][:, P * t:P * (t + 1)], xn[s][:, t, :], identf)
                last.then_inc(s_t, 1)

            pe.wait_ge(s_const, 16 * 7)
            chunk_turns(pe, ((1, project), (2, turn_stream)))

        @block.scalar
        def _(act):
            def root(b, s):
                act.wait_ge(s_var, 2 * b + s + 1)
                nc.scalar.activation(w.std, w.vareps, ACT.Sqrt).then_inc(s_std, 1)

            def stream_copy(b, s):
                n = 2 * b + s
                act.wait_ge(s_t, n + 1)
                if later(b):
                    act.wait_ge(s_v, n - 1)
                nc.scalar.activation(xt[s], bank[0], ACT.Copy).then_inc(s_xt, 1)

            def values_copy(b, s):
                act.wait_ge(s_v, 2 * b + s + 1)
                act.wait_ge(s_vout[s], 16 * OUTS * b)
                nc.scalar.activation(vrow[s][:, :, :, 0:8],
                                     bank[1].rearrange("p (t h d) -> p t h d", t=CT, h=16), ACT.Copy).then_inc(s_vrow, 1)

            def first_part(b, s):
                act.wait_ge(s_rot, 2 * b + s + 1)
                act.wait_ge(s_pout[s], 16 * OUTS * b)
                nc.scalar.activation(parts[s][:, :, 0, :], rot, ACT.Copy).then_inc(s_p1, 1)

            def second_part(b, s):
                act.wait_ge(s_r1, 2 * b + s + 1)
                nc.scalar.activation(parts[s][:, :, 1, :], rest, ACT.Copy).then_inc(s_p2, 1)

            act.wait_ge(s_zero, 5)
            chunk_turns(act, ((1, values_copy), (2, stream_copy), (1, first_part), (3, root), (1, second_part)))

        @block.vector
        def _(dve):
            chain = Chain(dve, s_chain)

            def norm(b, s):
                n = 2 * b + s
                dve.wait_ge(s_x[s], 16 * (b + 1))
                if later(b):
                    dve.wait_ge(s_t, n - 1)
                dve.wait_ge(s_xnout[s], 16 * b)
                w.stat_count = lambda: (CT - 1) * (n + 1)
                chain.base, chain.n = n * LN_STEPS, 0
                layernorm(nc, chain, xs[s], xn[s], w, lambda: dve.wait_ge(s_std, n + 1), s_var, s_xn)

            def products(b, s):
                n = 2 * b + s
                dve.wait_ge(s_qk, n + 1)
                dve.wait_ge(s_rot, n)
                place = slice(CW * s, CW * (s + 1))
                both = bank.run(2, 2).rearrange("p (w t) -> p w t", w=2)
                partner = bank.run(4, 2).rearrange("p (w t) -> p w t", w=2)
                nc.vector.tensor_tensor(t1, both, cos[:, place].unsqueeze(1).broadcast_to([P, 2, CW]), ALU.mult)\
                    .then_inc(s_t12, 1)
                nc.vector.tensor_tensor(t2, partner, sin[:, place].unsqueeze(1).broadcast_to([P, 2, CW]), ALU.mult)\
                    .then_inc(s_t12, 2)

            def remainder(b, s):
                n = 2 * b + s
                dve.wait_ge(s_p1, n + 1)
                dve.wait_ge(s_p2, n)
                dve.wait_ge(s_p3, n)
                nc.vector.tensor_tensor(rest, rot, parts[s][:, :, 0, :], ALU.subtract).then_inc(s_r1, 1)

            def third_part(b, s):
                n = 2 * b + s
                dve.wait_ge(s_r1, n + 1)
                dve.wait_ge(s_p2, n + 1)
                nc.vector.tensor_tensor(parts[s][:, :, 2, :], rest, parts[s][:, :, 1, :], ALU.subtract).then_inc(s_p3, 1)

            dve.wait_ge(s_const, 16 * 7)
            chunk_turns(dve, ((1, products), (0, third_part), (3, norm), (1, remainder)))
    arena.at = mark



HEADS, DH = 8, 64
INNER = HEADS * DH
WINDOW = 64
SPAN = P + WINDOW
HID = 341
NEG = -1e30


def local_attention(nc, sem, arena, bank, identf, identb, layer, stream, mid, wqkv, q_scales, wo, tables, masks):
    mark = arena.at
    PAIRS = HEADS // 2
    G = 4
    R4 = 4
    wq = arena.f32(3, INNER)
    wo_sb = arena.f32(PAIRS, D)
    scales = arena.f32(2, 2, DH)
    tabs = arena.f32(2, TB, 2, DH)
    mask_f = arena.f32(2, 2 * SPAN)
    mask = arena.bf16(2 * 2 * SPAN)
    hs = [arena.f32(D) for _ in range(R4)]
    xs = [arena.f32(D) for _ in range(R4)]
    outs = [arena.f32(D) for _ in range(R4)]
    ht = [arena.f32(P) for _ in range(2)]
    sq = arena.f32(2 * HEADS, DH)
    ss, clipped, rnorm = arena.f32(2 * HEADS), arena.f32(2 * HEADS), arena.f32(2 * HEADS)
    power = arena.f32(2 * HEADS)
    t1, t2, rot = arena.f32(2, HEADS, DH), arena.f32(2, HEADS, DH), arena.f32(2, HEADS, DH)
    qk = arena.f32(2, INNER)
    qa, qb = arena.f32(PAIRS, P), arena.f32(PAIRS, P)
    kt = [arena.f32(PAIRS, SPAN) for _ in range(2)]
    v = [arena.f32(INNER) for _ in range(R4)]
    top, negtop, den, rden = arena.f32(HEADS), arena.f32(HEADS), arena.f32(HEADS), arena.f32(HEADS)
    p = [arena.f32(HEADS, 2 * P) for _ in range(2)]
    pt = arena.f32(HEADS, 2 * P)
    ot = arena.f32(PAIRS, P)

    s = {n: sem("l_" + n) for n in (
        "w tab clear zeros ht0 ht qk0 v0 sq ss clip rn t1 rot qk qt qa kt tail v s top neg e den norm pt pta ptv o ot y "
        "out").split()}
    s_h = [sem(f"l_h{r}") for r in range(R4)]
    s_x = [sem(f"l_x{r}") for r in range(R4)]
    s_o = [sem(f"l_o{r}") for r in range(R4)]
    LOOP = TILES // R4 - 2
    WEIGHTS = 16 * 5

    def shift(q, r, k):
        return q + (r + k) // R4, (r + k) % R4

    def staged(q, r, k):
        y = shift(q, r, k)
        if isinstance(y[0], int) and not 0 <= R4 * y[0] + y[1] < TILES:
            return None
        return y

    def turns(eng, turn):
        for q in (-2, -1):
            for r in range(R4):
                turn(q, r)
        with eng.Fori(0, LOOP) as q:
            for r in range(R4):
                turn(q, r)
        for q in (LOOP, LOOP + 1):
            for r in range(R4):
                turn(q, r)

    with nc.Block() as block:

        @block.sync
        def _(sp):
            def rows(q, r):
                return (R4 * q + r) * P + q // (TB // R4)

            def load_shifted(q, r):
                if later(q):
                    sp.wait_ge(s["ht0"], R4 * (q - 1) + r + 1)
                for lo, hi, at in ((0, D // 2, 1), (D // 2, D, 0)):
                    sp.dma_start(hs[r][:, lo:hi], stream[bass.ds(layer, 1), bass.ds(rows(q, r) + at, P), lo:hi].rearrange(
                        "a r d -> (a r) d")).then_inc(s_h[r], 16)

            def load(q, r):
                if later(q):
                    sp.wait_ge(s["out"], R4 * (q - 1) + r + 1)
                sp.dma_start(xs[r], stream[bass.ds(layer, 1), bass.ds(rows(q, r) + 1, P), :].rearrange(
                    "a r d -> (a r) d")).then_inc(s_x[r], 16)

            def store(q, r):
                sp.wait_ge(s["out"], R4 * q + r + 1)
                sp.dma_start(mid[bass.ds(rows(q, r) + 1, P), :], outs[r]).then_inc(s_o[r], 16)

            sp.dma_start(wq, wqkv[bass.ds(layer, 1), :, :].rearrange("a p (w n) -> (a p) w n", w=3)).then_inc(s["w"], 16)
            sp.dma_start(wo_sb, wo[bass.ds(layer, 1), :, :].rearrange("a (c p) n -> (a p) c n", p=P)).then_inc(s["w"], 16)
            sp.dma_start(scales, q_scales[bass.ds(layer, 1), :, :, :, :].rearrange("a p x w d -> (a p) x w d"))\
                .then_inc(s["w"], 16)
            sp.dma_start(tabs, tables).then_inc(s["w"], 16)
            sp.dma_start(mask_f, masks).then_inc(s["w"], 16)

            def turn(q, r):
                for k, what in ((5, load_shifted), (0, store), (4, load)):
                    if staged(q, r, k):
                        what(*staged(q, r, k))

            turns(sp, turn)
            sp.wait_ge(s["w"], WEIGHTS)
            for r in range(R4):
                sp.wait_ge(s_o[r], 16 * TILES // R4)

        @block.gpsimd
        def _(pool):
            n = 0
            for piece, value in ((qa[DH:P], 0.0), (qb[0:DH], 0.0), (v[R4 - 1], 0.0), (power, -0.5)):
                nc.gpsimd.memset(piece, value).then_inc(s["clear"], 1)
                n += 1
                pool.wait_ge(s["clear"], n)

            def rotate(q, r):
                n = R4 * q + r
                pool.wait_ge(s["t1"], 3 * (n + 1))
                pool.wait_ge(s["qk"], n)
                nc.gpsimd.tensor_tensor(rot, t1, t2, ALU.add).then_inc(s["rot"], 1)

            def normalize(q, r):
                n = R4 * q + r
                pool.wait_ge(s["clip"], n + 1)
                nc.gpsimd.tensor_tensor(rnorm, clipped, power, ALU.pow).then_inc(s["rn"], 1)
                pool.wait_ge(s["rot"], n + 1)
                pool.wait_ge(s["rn"], n + 1)
                pool.wait_ge(s["qt"], n)
                nc.gpsimd.tensor_tensor(
                    qk.rearrange("p w (h d) -> p (w h) d", d=DH), rot.rearrange("p w h d -> p (w h) d"),
                    rnorm.unsqueeze(2).broadcast_to([P, 2 * HEADS, DH]), ALU.mult).then_inc(s["qk"], 1)

            def turn(q, r):
                for k, what in ((4, normalize), (5, rotate)):
                    if staged(q, r, k):
                        what(*staged(q, r, k))

            turns(pool, turn)

        @block.tensor
        def _(pe):
            def transpose_stream(q, r):
                n = R4 * q + r
                pe.wait_ge(s_h[r], 32 * (q + 1))
                if later(n):
                    pe.wait_ge(s["v"], n - 1)
                nc.tensor.transpose(bank[2][:, 0:P], hs[r], identf).then_inc(s["ht0"], 1)

            def project_qk(q, r):
                n = R4 * q + r
                pe.wait_ge(s["ht"], n + 1)
                pe.wait_ge(s["t1"], 3 * n)
                pe.wait_ge(s["sq"], n)
                for w in range(2):
                    last = nc.tensor.matmul(bank[w], ht[r % 2], wq[:, w, :], start=True, stop=True)
                last.then_inc(s["qk0"], 1)

            def project_v(q, r):
                n = R4 * q + r
                pe.wait_ge(s["ht"], min(n + 2, TILES) if isinstance(n, int) else n + 2)
                nc.tensor.matmul(bank[2], ht[r % 2], wq[:, 2, :], start=True, stop=True).then_inc(s["v0"], 1)

            def turn_qk(q, r):
                n = R4 * q + r
                pe.wait_ge(s["qk"], n + 1)
                for w in range(2):
                    for c in range(PAIRS):
                        last = nc.tensor.transpose(bank[3 + w][:, P * c:P * (c + 1)], qk[:, w, P * c:P * (c + 1)], identf)
                last.then_inc(s["qt"], 1)

            def scores(q, r, g):
                n = R4 * q + r
                if g == 0:
                    pe.wait_ge(s["qa"], 2 * (n + 1))
                    pe.wait_ge(s["kt"], n + 1)
                    pe.wait_ge(s["tail"], n + 1)
                pe.wait_ge(s["e"], HEADS * n + G * g)
                at = q % (TB // R4) * (2 * SPAN) if r == 0 else 2 * SPAN
                for b in range(2):
                    nc.tensor.matmul(bank[5 + b][:, 0:2 * SPAN], identb, mask[:, bass.ds(at, 2 * SPAN)],
                                     start=True, stop=False)
                    for j in range(2):
                        h = G * g + 2 * b + j
                        last = nc.tensor.matmul(bank[5 + b][:, SPAN * j:SPAN * (j + 1)], (qa, qb)[h % 2][:, h // 2, :],
                                                kt[r % 2][:, h // 2, :], start=False, stop=(j == 1))
                last.then_inc(s["s"], 1)

            def turn_probs(q, r, g):
                n = R4 * q + r
                pe.wait_ge(s["norm"], 2 * n + g + 1)
                if g == 0:
                    pe.wait_ge(s["pta"], 2 * n)
                    pe.wait_ge(s["ptv"], 2 * n)
                elif staged(q, r, 2):
                    pe.wait_ge(s["qa"], 2 * (n + 3))
                    pe.wait_ge(s["kt"], n + 3)
                for j in range(G):
                    for c in range(2):
                        last = nc.tensor.transpose(bank[3 + j // 2][:, 2 * P * (j % 2) + P * c:2 * P * (j % 2) + P * (c + 1)],
                                                   p[r % 2][:, G * g + j, P * c:P * (c + 1)], identf)
                last.then_inc(s["pt"], 1)

            def values(q, r, g):
                n = R4 * q + r
                pe.wait_ge(s["pta"], 2 * n + g + 1)
                pe.wait_ge(s["ptv"], 2 * n + g + 1)
                if g == 0:
                    pe.wait_ge(s["v"], n + 1)
                    pe.wait_ge(s["out"], n)
                for pair in range(2):
                    for c in range(2):
                        for j in range(2):
                            h = G * g + 2 * pair + j
                            last = nc.tensor.matmul(
                                bank[7][DH * j:DH * (j + 1), P * (h // 2):P * (h // 2 + 1)],
                                v[(r - 1) % R4 if c == 0 else r][:, DH * h:DH * (h + 1)], pt[:, h, P * c:P * (c + 1)],
                                start=(c == 0), stop=(c == 1), tile_position=(0, DH * j))
                last.then_inc(s["o"], 1)

            def project_out(q, r):
                pe.wait_ge(s["ot"], R4 * q + r + 1)
                for c in range(PAIRS):
                    last = nc.tensor.matmul(bank[7][:, 0:D], ot[:, c, :], wo_sb[:, c, :],
                                            start=(c == 0), stop=(c == PAIRS - 1))
                last.then_inc(s["y"], 1)

            def turn(q, r):
                for k, what, more in ((2, scores, (0,)), (0, project_out, ()), (1, turn_probs, (0,)),
                                      (5, transpose_stream, ()), (2, scores, (1,)), (1, values, (0,)), (3, turn_qk, ()),
                                      (5, project_qk, ()), (4, project_v, ()), (1, turn_probs, (1,)),
                                      (1, values, (1,))):
                    if staged(q, r, k):
                        what(*staged(q, r, k), *more)

            pe.wait_ge(s["w"], WEIGHTS)
            pe.wait_ge(s["clear"], 4)
            pe.wait_ge(s["zeros"], 3)
            pe.wait_ge(s["tab"], 3)
            turns(pe, turn)

        @block.scalar
        def _(act):
            def stream_copy(q, r):
                n = R4 * q + r
                act.wait_ge(s["ht0"], n + 1)
                if later(n, 1):
                    act.wait_ge(s["v0"], n - 1)
                nc.scalar.activation(ht[r % 2], bank[2][:, 0:P], ACT.Copy).then_inc(s["ht"], 1)

            def squares(q, r):
                n = R4 * q + r
                act.wait_ge(s["qk0"], n + 1)
                act.wait_ge(s["ss"], n)
                nc.scalar.activation(sq, bank.run(0, 2).rearrange("p (h d) -> p h d", d=DH), ACT.Square)\
                    .then_inc(s["sq"], 1)

            def values_copy(q, r):
                n = R4 * q + r
                act.wait_ge(s["v0"], n + 1)
                if later(q):
                    act.wait_ge(s["o"], 2 * (n - 2))
                nc.scalar.activation(v[r], bank[2], ACT.Copy).then_inc(s["v"], 1)

            def keys(q, r):
                n = R4 * q + r
                act.wait_ge(s["qt"], n + 1)
                act.wait_ge(s["tail"], n)
                nc.scalar.activation(kt[r % 2][:, :, WINDOW:SPAN], bank[4].rearrange("p (c t) -> p c t", c=PAIRS),
                                     ACT.Copy).then_inc(s["kt"], 1)

            def exps(q, r, g):
                n = R4 * q + r
                act.wait_ge(s["neg"], 2 * n + g + 1)
                if later(n):
                    act.wait_ge(s["norm"], 2 * n + g - 1)
                if later(n, 1):
                    act.wait_ge(s["pt"], 2 * n + g - 3)
                for j in range(G):
                    h = G * g + j
                    nc.scalar.activation(p[r % 2][:, h, WINDOW:2 * P], bank[5 + j // 2][:, SPAN * (j % 2):SPAN * (j % 2 + 1)],
                                         ACT.Exp, bias=negtop[:, h:h + 1], scale=8.0, accum_out=den[:, h:h + 1])\
                        .then_inc(s["e"], 1)

            def probs_copy(q, r, g):
                n = R4 * q + r
                act.wait_ge(s["pt"], 2 * n + g + 1)
                act.wait_ge(s["o"], 2 * n)
                nc.scalar.activation(pt[:, G * g:G * g + 2, :], bank[3].rearrange("p (h t) -> p h t", h=2), ACT.Copy)\
                    .then_inc(s["pta"], 1)

            def out_copy(q, r):
                n = R4 * q + r
                act.wait_ge(s["o"], 2 * n + 2)
                act.wait_ge(s["y"], n)
                nc.scalar.activation(ot, bank[7].rearrange("p (c t) -> p c t", c=PAIRS), ACT.Copy).then_inc(s["ot"], 1)

            def turn(q, r):
                for k, what, more in ((2, exps, (0,)), (1, probs_copy, (0,)), (5, stream_copy, ()), (2, exps, (1,)),
                                      (3, keys, ()), (5, squares, ()), (1, probs_copy, (1,)), (1, out_copy, ()),
                                      (4, values_copy, ())):
                    if staged(q, r, k):
                        what(*staged(q, r, k), *more)

            act.wait_ge(s["clear"], 4)
            act.wait_ge(s["zeros"], 3)
            turns(act, turn)

        @block.vector
        def _(dve):
            def norms(q, r):
                n = R4 * q + r
                dve.wait_ge(s["sq"], n + 1)
                dve.wait_ge(s["rn"], n)
                nc.vector.tensor_reduce(ss, sq, AX.X, ALU.add).then_inc(s["ss"], 1)
                dve.wait_ge(s["ss"], n + 1)
                nc.vector.tensor_scalar(clipped, ss, 1e-24, None, ALU.max).then_inc(s["clip"], 1)

            def products(q, r):
                n = R4 * q + r
                dve.wait_ge(s["sq"], n + 1)
                dve.wait_ge(s["rot"], n)
                t = q % (TB // R4) * R4 + r
                both = bank.run(0, 2).rearrange("p (w h d) -> p w h d", w=2, h=HEADS)
                flat = tabs.rearrange("p x t w d -> p (x t w d)")
                H = DH // 2

                def table(x, lo, hi):
                    one = flat[:, bass.ds(t * (2 * DH) + x * TB * 2 * DH, 2 * DH)].rearrange("p (w d) -> p w d", w=2)
                    return one[:, :, lo:hi].unsqueeze(2).broadcast_to([P, 2, HEADS, hi - lo])

                nc.vector.tensor_tensor(t1, both, table(0, 0, DH), ALU.mult).then_inc(s["t1"], 1)
                nc.vector.tensor_tensor(t2[:, :, :, 0:H], both[:, :, :, H:DH], table(1, 0, H), ALU.mult)\
                    .then_inc(s["t1"], 1)
                nc.vector.tensor_tensor(t2[:, :, :, H:DH], both[:, :, :, 0:H], table(1, H, DH), ALU.mult)\
                    .then_inc(s["t1"], 1)

            def queries(q, r):
                n = R4 * q + r
                dve.wait_ge(s["qt"], n + 1)
                dve.wait_ge(s["s"], 2 * n)
                nc.vector.tensor_copy(qa[0:DH], bank[3][0:DH].rearrange("p (c t) -> p c t", c=PAIRS)).then_inc(s["qa"], 1)
                nc.vector.tensor_copy(qb[DH:P], bank[3][DH:P].rearrange("p (c t) -> p c t", c=PAIRS)).then_inc(s["qa"], 1)
                dve.wait_ge(s["kt"], n)
                nc.vector.tensor_copy(kt[r % 2][:, :, 0:WINDOW], kt[1 - r % 2][:, :, P:SPAN]).then_inc(s["tail"], 1)

            def maxima(q, r, g):
                n = R4 * q + r
                dve.wait_ge(s["s"], 2 * n + g + 1)
                part = slice(G * g, G * (g + 1))
                both = bank.run(5, 2).rearrange("p (b n) -> p b n", b=2)[:, :, 0:2 * SPAN]
                nc.vector.tensor_reduce(top[:, part].rearrange("p (b h) -> p b h", b=2),
                                        both.rearrange("p b (h n) -> p b h n", h=2), AX.X, ALU.max).then_inc(s["top"], 1)
                dve.wait_ge(s["top"], 2 * n + g + 1)
                nc.vector.tensor_scalar(negtop[:, part], top[:, part], -8.0, None, ALU.mult).then_inc(s["neg"], 1)

            def normalize(q, r, g):
                n = R4 * q + r
                dve.wait_ge(s["e"], HEADS * n + G * (g + 1))
                part = slice(G * g, G * (g + 1))
                nc.vector.reciprocal(rden[:, part], den[:, part]).then_inc(s["den"], 1)
                dve.wait_ge(s["den"], 2 * n + g + 1)
                nc.vector.tensor_tensor(p[r % 2][:, part, WINDOW:2 * P], p[r % 2][:, part, WINDOW:2 * P],
                                        rden[:, part].unsqueeze(2).broadcast_to([P, G, SPAN]), ALU.mult)\
                    .then_inc(s["norm"], 1)

            def probs_copy(q, r, g):
                n = R4 * q + r
                dve.wait_ge(s["pt"], 2 * n + g + 1)
                dve.wait_ge(s["o"], 2 * n)
                nc.vector.tensor_copy(pt[:, G * g + 2:G * g + 4, :], bank[4].rearrange("p (h t) -> p h t", h=2))\
                    .then_inc(s["ptv"], 1)

            def finish(q, r):
                dve.wait_ge(s["y"], R4 * q + r + 1)
                dve.wait_ge(s_x[r], 16 * (q + 1))
                dve.wait_ge(s_o[r], 16 * q)
                nc.vector.tensor_tensor(outs[r], bank[7][:, 0:D], xs[r], ALU.add).then_inc(s["out"], 1)

            def turn(q, r):
                for k, what, more in ((2, maxima, (0,)), (0, finish, ()), (4, norms, ()), (1, probs_copy, (0,)),
                                      (2, normalize, (0,)), (2, maxima, (1,)), (3, queries, ()), (2, normalize, (1,)),
                                      (1, probs_copy, (1,)), (5, products, ())):
                    if staged(q, r, k):
                        what(*staged(q, r, k), *more)

            dve.wait_ge(s["w"], WEIGHTS)
            dve.wait_ge(s["clear"], 4)
            for n, piece in enumerate((p[0][:, :, 0:WINDOW], p[1][:, :, 0:WINDOW], kt[1][:, :, P:SPAN])):
                nc.vector.memset(piece, 0.0).then_inc(s["zeros"], 1)
                dve.wait_ge(s["zeros"], n + 1)
            for x in range(2):
                nc.vector.tensor_tensor(tabs[:, x], tabs[:, x],
                                        scales[:, x].unsqueeze(1).broadcast_to([P, TB, 2, DH]), ALU.mult)\
                    .then_inc(s["tab"], 1)
            nc.vector.tensor_copy(mask, mask_f.rearrange("p m n -> p (m n)")).then_inc(s["tab"], 1)
            dve.wait_ge(s["tab"], 3)
            turns(dve, turn)
    arena.at = mark


BLOCKS = 3
HB = -(-HID // BLOCKS)


def feed_forward(nc, sem, arena, bank, identf, layer, mid, stream, ln, w1, b1, w2, b2):
    mark = arena.at
    size = [HB, HB, HID - 2 * HB]
    w1_sb = arena.f32(2, HID)
    w2_sb = arena.f32(BLOCKS, D)
    b1_sb = arena.f32(2, BLOCKS)
    b2_sb = arena.f32(D)
    ln_sb = arena.f32(2)
    hs = [arena.f32(CT, D) for _ in range(2)]
    xs = [arena.f32(CT, D) for _ in range(2)]
    hn = [arena.f32(CT, D) for _ in range(2)]
    ht = [arena.f32(CW) for _ in range(2)]
    gate = arena.f32(BLOCKS, CW)
    u = [arena.f32(BLOCKS, CW) for _ in range(2)]
    xb = [arena.f32(CT, D) for _ in range(2)]
    outs = [arena.f32(CT, D) for _ in range(2)]
    power = arena.f32(CT)
    s = {n: sem("f_" + n) for n in "w power stat chain var std hn t ht a gate u y xb out".split()}
    s_h = [sem(f"f_h{i}") for i in range(2)]
    s_x = [sem(f"f_x{i}") for i in range(2)]
    s_o = [sem(f"f_o{i}") for i in range(2)]
    w = NormBuffers(nc, arena, s["stat"])
    w.invert = None
    LOADS = 7

    with nc.Block() as block:

        @block.sync
        def _(sp):
            def load_shifted(b, z):
                if later(b):
                    sp.wait_ge(s["hn"], CT * (2 * b + z - 1))
                row = b * (N + 1) + CW * z
                for r, lo, hi in ((row + 1, 0, D // 2), (row, D // 2, D)):
                    sp.dma_start(hs[z][:, :, lo:hi], mid[bass.ds(r, CW), lo:hi].rearrange("(t p) d -> p t d", p=P))\
                        .then_inc(s_h[z], 16)

            def load(b, z):
                if later(b):
                    sp.wait_ge(s["xb"], 2 * b + z - 1)
                sp.dma_start(xs[z], mid[bass.ds(b * (N + 1) + CW * z + 1, CW), :].rearrange("(t p) d -> p t d", p=P))\
                    .then_inc(s_x[z], 16)

            def store(b, z):
                sp.wait_ge(s["out"], 2 * b + z + 1)
                sp.dma_start(stream[bass.ds(layer + 1, 1), bass.ds(b * (N + 1) + CW * z + 1, CW), :].rearrange(
                    "a (t p) d -> p (a t) d", p=P), outs[z]).then_inc(s_o[z], 16)

            chunk_turns(sp, ((4, load_shifted), (2, load), (0, store)))
            for z in range(2):
                sp.wait_ge(s_o[z], 16 * B)

        @block.gpsimd
        def _(pool):
            def root(b, z):
                n = 2 * b + z
                pool.wait_ge(s["var"], n + 1)
                pool.wait_ge(s["hn"], CT * n)
                nc.gpsimd.tensor_tensor(w.rstd, w.vareps, power, ALU.pow).then_inc(s["std"], 1)

            def add_bias(b, z):
                pool.wait_ge(s_x[z], 16 * (b + 1))
                if later(b):
                    pool.wait_ge(s["out"], 2 * b + z - 1)
                nc.gpsimd.tensor_tensor(xb[z], xs[z], b2_sb.unsqueeze(1).broadcast_to([P, CT, D]), ALU.add)\
                    .then_inc(s["xb"], 1)

            nc.gpsimd.memset(power, -0.5).then_inc(s["power"], 1)
            pool.wait_ge(s["power"], 1)
            pool.wait_ge(s["w"], 16 * LOADS)
            chunk_turns(pool, ((1, add_bias), (3, root)))

        @block.tensor
        def _(pe):
            def turn_stream(b, z):
                n = 2 * b + z
                pe.wait_ge(s["hn"], CT * (n + 1))
                pe.wait_ge(s["ht"], n)
                for t in range(CT):
                    last = nc.tensor.transpose(bank[0][:, P * t:P * (t + 1)], hn[z][:, t, :], identf)
                last.then_inc(s["t"], 1)

            def hidden(b, z):
                n = 2 * b + z
                pe.wait_ge(s["ht"], n + 1)
                for k in range(BLOCKS):
                    for half in (1, 0):
                        if half == 1:
                            pe.wait_ge(s["gate"], BLOCKS * n)
                        else:
                            pe.wait_ge(s["u"], BLOCKS * n)
                        nc.tensor.matmul(bank[1 + 2 * k + half][0:size[k], :],
                                         w1_sb[:, half, HB * k:HB * k + size[k]], ht[z], start=True, stop=True)\
                            .then_inc(s["a"], 1)

            def output(b, z):
                n = 2 * b + z
                pe.wait_ge(s["u"], BLOCKS * (n + 1))
                pe.wait_ge(s["out"], n)
                for t in range(CT):
                    for k in range(BLOCKS):
                        last = nc.tensor.matmul(bank[7][:, P * t:P * (t + 1)], u[z][0:size[k], k, P * t:P * (t + 1)],
                                                w2_sb[0:size[k], k, :], start=(k == 0), stop=(k == BLOCKS - 1))
                last.then_inc(s["y"], 1)

            pe.wait_ge(s["w"], 16 * LOADS)
            chunk_turns(pe, ((1, hidden), (2, turn_stream), (0, output)))

        @block.scalar
        def _(act):
            def turned(b, z):
                n = 2 * b + z
                act.wait_ge(s["t"], n + 1)
                if later(b):
                    act.wait_ge(s["a"], 2 * BLOCKS * (n - 1))
                nc.scalar.activation(ht[z], bank[0], ACT.Identity, bias=ln_sb[:, 1:2], scale=ln_sb[:, 0:1])\
                    .then_inc(s["ht"], 1)

            def gates(b, z):
                n = 2 * b + z
                for k in range(BLOCKS):
                    act.wait_ge(s["a"], 2 * BLOCKS * n + 2 * k + 1)
                    act.wait_ge(s["u"], BLOCKS * n)
                    r = size[k]
                    nc.scalar.activation(gate[0:r, k, :], bank[2 + 2 * k][0:r, :], ACT.Gelu, bias=b1_sb[0:r, 1, k:k + 1])\
                        .then_inc(s["gate"], 1)

            act.dma_start(w1_sb, w1[bass.ds(layer, 1), :, :].rearrange("a p (w n) -> (a p) w n", w=2)).then_inc(s["w"], 16)
            for k in range(BLOCKS):
                act.dma_start(w2_sb[0:size[k], k, :], w2[bass.ds(layer, 1), HB * k:HB * k + size[k], :].rearrange(
                    "a r n -> (a r) n")).then_inc(s["w"], 16)
            act.dma_start(b1_sb[0:HB], b1[bass.ds(layer, 1), :, :, :].rearrange("a r w k -> (a r) w k")).then_inc(s["w"], 16)
            act.dma_start(b2_sb, b2[bass.ds(layer, 1), :, :].rearrange("a p n -> (a p) n")).then_inc(s["w"], 16)
            act.dma_start(ln_sb, ln[bass.ds(layer, 1), :, :].rearrange("a p n -> (a p) n")).then_inc(s["w"], 16)
            act.wait_ge(s["w"], 16 * LOADS)
            chunk_turns(act, ((1, gates), (2, turned)))

        @block.vector
        def _(dve):
            chain = Chain(dve, s["chain"])
            STEPS = LN_STEPS - 1

            def norm(b, z):
                n = 2 * b + z
                dve.wait_ge(s_h[z], 32 * (b + 1))
                w.stat_count = lambda: (CT - 1) * (n + 1)
                chain.base, chain.n = n * STEPS, 0

                def root():
                    dve.wait_ge(s["std"], n + 1)
                    if later(b):
                        dve.wait_ge(s["t"], n - 1)
                layernorm(nc, chain, hs[z], hn[z], w, root, s["var"], s["hn"])

            def post(b, z):
                n = 2 * b + z
                for k in range(BLOCKS):
                    r = size[k]
                    dve.wait_ge(s["gate"], BLOCKS * n + k + 1)
                    dve.wait_ge(s["a"], 2 * BLOCKS * n + 2 * k + 2)
                    if later(b):
                        dve.wait_ge(s["y"], n - 1)
                    nc.vector.scalar_tensor_tensor(u[z][0:r, k, :], bank[1 + 2 * k][0:r, :], b1_sb[0:r, 0, k:k + 1],
                                                   gate[0:r, k, :], ALU.add, ALU.mult).then_inc(s["u"], 1)

            def finish(b, z):
                n = 2 * b + z
                dve.wait_ge(s["y"], n + 1)
                dve.wait_ge(s["xb"], n + 1)
                dve.wait_ge(s_o[z], 16 * b)
                nc.vector.tensor_tensor(outs[z], bank[7].rearrange("p (t d) -> p t d", t=CT), xb[z], ALU.add)\
                    .then_inc(s["out"], 1)

            dve.wait_ge(s["w"], 16 * LOADS)
            chunk_turns(dve, ((1, post), (0, finish), (3, norm)))
    arena.at = mark



def middle_phase(nc, sem, arena, bank, identf, O, w_out, b_out, x, stream, wq, wkd, wku, wvu, wsw, bsw,
                 x1_out, xn_out, qk_parts, v_rows, logits):
    mark = arena.at
    E = 2 * D
    LR = 64
    w_out_sb = arena.f32(D)
    b_out_sb = arena.f32(D)
    wq_sb = arena.f32(2, D)
    wkd_sb = arena.f32(LR)
    wku_sb, wvu_sb = arena.f32(2, D), arena.f32(E)
    wsw_sb, bsw_sb = arena.f32(8), arena.f32(8)
    xs = [arena.f32(CT, D) for _ in range(2)]
    gs = [arena.f32(CT, D) for _ in range(2)]
    oc = arena.f32(CT, D)
    ot, sg = arena.f32(CW), arena.f32(CT, D)
    sp1, sp2 = arena.f32(CT, D), arena.f32(CT, D)
    x1 = [arena.f32(CT, D) for _ in range(2)]
    xn = [arena.f32(CT, D) for _ in range(2)]
    xt = arena.f32(CW)
    lat = arena.f32(CW)
    rest = [arena.f32(2, CW) for _ in range(2)]
    parts = [arena.bf16(2, 2, 3, CW) for _ in range(2)]
    vrow = arena.f32(CT, 8, 64)
    s = {n: sem("m_" + n) for n in ("w stat chain var std clear oc ot0 ot so sg s1 s2 x1 xn t xt q lat0 lat k v0 v "
                                    "lg lgo p1 r1 p2 p3 fill").split()}
    s_x = [sem(f"m_load{i}") for i in range(2)]
    s_o1 = [sem(f"m_o1{i}") for i in range(2)]
    s_oq = [[sem(f"m_o{name}{i}") for i in range(2)] for name in "qk"]
    s_ov = sem("m_ov")
    w = NormBuffers(nc, arena, s["stat"])
    LOADS = 8

    with nc.Block() as block:

        @block.sync
        def _(sp):
            def load(b, z):
                sp.dma_start(xs[z], x[bass.ds(b, 1), CW * z:CW * (z + 1), :].rearrange("a (t p) d -> p (a t) d", p=P))\
                    .then_inc(s_x[z], 16)
                sp.dma_start(gs[z], stream[2, bass.ds(b * (N + 1) + 1 + CW * z, CW), :].rearrange(
                    "(t p) d -> p t d", p=P)).then_inc(s_x[z], 16)

            def load_later(b, z):
                if not later(b):
                    return
                sp.wait_ge(s["x1"], 2 * b + z - 1)
                load(b, z)

            def store_x(b, z):
                n = 2 * b + z
                for sig, src, dst in ((s["x1"], x1, x1_out), (s["xn"], xn, xn_out)):
                    sp.wait_ge(sig, (CT if src is xn else 1) * (n + 1))
                    sp.dma_start(dst[bass.ds(n * CT, CT), :, :].rearrange("t p d -> p t d"), src[z])\
                        .then_inc(s_o1[z], 16)

            def store_parts(which, b, z):
                n = 2 * b + z
                sp.wait_ge(s["p2"], 2 * n + which + 1)
                sp.wait_ge(s["p3"], 2 * n + which + 1)
                for blk in range(2):
                    for half in range(2):
                        sp.dma_start(
                            qk_parts[bass.ds(4 * b + 2 * blk + half, 1), 3 * which:3 * which + 3, :,
                                     CW * z:CW * (z + 1)].rearrange("a n r t -> (a r) n t"),
                            parts[z][64 * half:64 * (half + 1), which, blk, :, :]).then_inc(s_oq[which][z], 16)

            def store_v(b, z):
                sp.wait_ge(s["v"], 2 * (2 * b + z + 1))
                for pair in range(4):
                    sp.dma_start(v_rows[bass.ds(4 * b + pair, 1), :, CT * z:CT * (z + 1), :].rearrange(
                        "a p t m -> (a p) t m"),
                        vrow[:, :, 2 * pair:2 * pair + 2, :].rearrange("p t h m -> p t (h m)")).then_inc(s_ov, 16)

            load(0, 0)
            load(0, 1)
            chunk_turns(sp, ((3, load_later), (0, lambda b, z: store_parts(1, b, z)), (2, store_x),
                             (1, lambda b, z: store_parts(0, b, z)), (1, store_v)))
            for z in range(2):
                sp.wait_ge(s_o1[z], 32 * B)
                for which in range(2):
                    sp.wait_ge(s_oq[which][z], 16 * 4 * B)
            sp.wait_ge(s_ov, 16 * 4 * CHUNKS)

        @block.gpsimd
        def _(pool):
            n = 0
            for piece, value in ((vrow, 0.0), (vrow[:, :, :, 32:33], 1.0), (wku_sb, 0.0), (wvu_sb, 0.0), (lat, 0.0)):
                nc.gpsimd.memset(piece, value).then_inc(s["clear"], 1)
                n += 1
                pool.wait_ge(s["clear"], n)
            flat = O.rearrange("p u t d -> p (u t d)")
            with pool.Fori(0, B) as b:
                for z in range(2):
                    n = 2 * b + z
                    pool.wait_ge(s["ot0"], n)
                    for g in range(4):
                        src = flat[:, bass.ds(b * (4 * TB * UR) + g * TB * UR + z * CT * UR, CT * UR)]
                        ins = nc.gpsimd.tensor_copy(oc[:, :, UR * g:UR * (g + 1)],
                                                    src.rearrange("p (t d) -> p t d", t=CT))
                        ins.then_inc(s["oc"], 1)

        @block.tensor
        def _(pe):
            def turn_attention(b, z):
                n = 2 * b + z
                pe.wait_ge(s["oc"], 4 * (n + 1))
                if later(n):
                    pe.wait_ge(s["lgo"], n - 1)
                for t in range(CT):
                    last = nc.tensor.transpose(bank[0][:, P * t:P * (t + 1)], oc[:, t, :], identf)
                last.then_inc(s["ot0"], 1)

            def project_attention(b, z):
                n = 2 * b + z
                pe.wait_ge(s["ot"], n + 1)
                pe.wait_ge(s["s1"], n)
                for t in range(CT):
                    last = nc.tensor.matmul(bank[1][:, P * t:P * (t + 1)], ot[:, P * t:P * (t + 1)], w_out_sb,
                                            start=True, stop=True)
                last.then_inc(s["so"], 1)

            def turn_stream(b, z):
                n = 2 * b + z
                pe.wait_ge(s["xn"], CT * (n + 1))
                pe.wait_ge(s["lat"], n)
                for t in range(CT):
                    last = nc.tensor.transpose(bank[2][:, P * t:P * (t + 1)], xn[z][:, t, :], identf)
                last.then_inc(s["t"], 1)

            def queries(b, z):
                n = 2 * b + z
                pe.wait_ge(s["xt"], n + 1)
                pe.wait_ge(s["r1"], 2 * n)
                pe.wait_ge(s["p1"], 2 * n)
                for blk in range(2):
                    last = nc.tensor.matmul(bank[3 + blk], wq_sb[:, blk, :], xt, start=True, stop=True)
                last.then_inc(s["q"], 1)
                nc.tensor.matmul(bank[2][0:LR, :], wkd_sb, xt, start=True, stop=True).then_inc(s["lat0"], 1)

            def router(b, z):
                n = 2 * b + z
                pe.wait_ge(s["ot"], min(n + 2, CHUNKS) if isinstance(n, int) else n + 2)
                for t in range(CT):
                    last = nc.tensor.matmul(bank[0][:, 8 * t:8 * (t + 1)], xt[:, P * t:P * (t + 1)], wsw_sb,
                                            start=True, stop=True)
                last.then_inc(s["lg"], 1)

            def keys_values(b, z):
                n = 2 * b + z
                pe.wait_ge(s["lat"], n + 1)
                for blk in range(2):
                    last = nc.tensor.matmul(bank[5 + blk], wku_sb[:, blk, :], lat, start=True, stop=True)
                last.then_inc(s["k"], 1)
                for g in range(2):
                    pe.wait_ge(s["v"], 2 * n + g)
                    for t in range(2):
                        tt = 2 * g + t
                        last = nc.tensor.matmul(bank[7][:, E * t:E * (t + 1)], lat[:, P * tt:P * (tt + 1)], wvu_sb,
                                                start=True, stop=True)
                    last.then_inc(s["v0"], 1)

            pe.wait_ge(s["w"], 16 * LOADS)
            pe.wait_ge(s["clear"], 5)
            chunk_turns(pe, ((1, turn_stream), (2, turn_attention), (1, queries), (2, project_attention), (1, router),
                             (1, keys_values)))

        @block.scalar
        def _(act):
            for dst, src in ((w_out_sb, w_out), (b_out_sb, b_out), (wq_sb, wq.rearrange("p (c n) -> p c n", c=2)),
                             (wkd_sb, wkd), (wsw_sb, wsw), (bsw_sb, bsw)):
                act.dma_start(dst, src).then_inc(s["w"], 16)
            act.wait_ge(s["clear"], 5)
            act.dma_start(wku_sb[0:LR], wku.rearrange("p (c n) -> p c n", c=2)).then_inc(s["w"], 16)
            act.dma_start(wvu_sb[0:LR], wvu).then_inc(s["w"], 16)

            def gate(b, z):
                act.wait_ge(s_x[z], 32 * (b + 1))
                act.wait_ge(s["s2"], 2 * b + z)
                nc.scalar.activation(sg, gs[z], ACT.Silu).then_inc(s["sg"], 1)

            def attention_copy(b, z):
                n = 2 * b + z
                act.wait_ge(s["ot0"], n + 1)
                act.wait_ge(s["so"], n)
                nc.scalar.activation(ot, bank[0], ACT.Copy).then_inc(s["ot"], 1)

            def root(b, z):
                act.wait_ge(s["var"], 2 * b + z + 1)
                nc.scalar.activation(w.std, w.vareps, ACT.Sqrt).then_inc(s["std"], 1)

            def stream_copy(b, z):
                n = 2 * b + z
                act.wait_ge(s["t"], n + 1)
                act.wait_ge(s["lg"], n)
                act.wait_ge(s["lat0"], n)
                nc.scalar.activation(xt, bank[2], ACT.Copy).then_inc(s["xt"], 1)

            def latent_copy(b, z):
                n = 2 * b + z
                act.wait_ge(s["lat0"], n + 1)
                act.wait_ge(s["v0"], 2 * n)
                nc.scalar.activation(lat[0:LR], bank[2][0:LR, :], ACT.Copy).then_inc(s["lat"], 1)

            def first_part(which, b, z):
                act.wait_ge(s["qk"[which]], 2 * b + z + 1)
                act.wait_ge(s_oq[which][z], 16 * 4 * b)
                src = bank.run(3 + 2 * which, 2).rearrange("p (c t) -> p c t", c=2)
                nc.scalar.activation(parts[z][:, which, :, 0, :], src, ACT.Copy).then_inc(s["p1"], 1)

            def second_part(which, b, z):
                act.wait_ge(s["r1"], 2 * (2 * b + z) + which + 1)
                nc.scalar.activation(parts[z][:, which, :, 1, :], rest[which], ACT.Copy).then_inc(s["p2"], 1)

            def values_copy(b, z):
                n = 2 * b + z
                act.wait_ge(s_ov, 16 * 4 * n)
                for g in range(2):
                    act.wait_ge(s["v0"], 2 * n + g + 1)
                    nc.scalar.activation(vrow[:, 2 * g:2 * g + 2, :, 0:32],
                                         bank[7].rearrange("p (t h d) -> p t h d", t=2, h=8), ACT.Copy)\
                        .then_inc(s["v"], 1)

            chunk_turns(act, ((0, lambda b, z: second_part(1, b, z)), (1, stream_copy), (2, gate), (2, attention_copy),
                              (1, lambda b, z: first_part(0, b, z)), (1, latent_copy), (2, root),
                              (1, lambda b, z: first_part(1, b, z)), (1, lambda b, z: second_part(0, b, z)),
                              (1, values_copy)))

        @block.vector
        def _(dve):
            chain = Chain(dve, s["chain"])

            def add_attention(b, z):
                n = 2 * b + z
                dve.wait_ge(s["so"], n + 1)
                dve.wait_ge(s["s2"], n)
                nc.vector.tensor_tensor(sp1, bank[1].rearrange("p (t d) -> p t d", t=CT),
                                        b_out_sb.unsqueeze(1).broadcast_to([P, CT, D]), ALU.add).then_inc(s["s1"], 1)
                dve.wait_ge(s["s1"], n + 1)
                dve.wait_ge(s["sg"], n + 1)
                dve.wait_ge(s["x1"], n)
                nc.vector.tensor_tensor(sp2, sp1, sg, ALU.mult).then_inc(s["s2"], 1)
                dve.wait_ge(s["s2"], n + 1)
                dve.wait_ge(s_o1[z], 32 * b)
                dve.wait_ge(s_x[z], 32 * (b + 1))
                nc.vector.tensor_tensor(x1[z], xs[z], sp2, ALU.add).then_inc(s["x1"], 1)
                dve.wait_ge(s["x1"], n + 1)
                if later(b):
                    dve.wait_ge(s["t"], n - 1)
                w.stat_count = lambda: (CT - 1) * (n + 1)
                chain.base, chain.n = n * LN_STEPS, 0
                layernorm(nc, chain, x1[z], xn[z], w, lambda: dve.wait_ge(s["std"], n + 1), s["var"], s["xn"])

            def router(b, z):
                n = 2 * b + z
                dve.wait_ge(s["lg"], n + 1)
                lg = logits.rearrange("p t e -> p (t e)")[:, bass.ds(n * (8 * CT), 8 * CT)]
                nc.vector.tensor_tensor(lg.rearrange("p (t e) -> p t e", e=8),
                                        bank[0][:, 0:8 * CT].rearrange("p (t e) -> p t e", e=8),
                                        bsw_sb.unsqueeze(1).broadcast_to([P, CT, 8]), ALU.add).then_inc(s["lgo"], 1)

            def remainder(which, b, z):
                m = 2 * (2 * b + z) + which
                src = bank.run(3 + 2 * which, 2).rearrange("p (c t) -> p c t", c=2)
                dve.wait_ge(s["p1"], m + 1)
                if later(m, 1):
                    dve.wait_ge(s["p2"], m - 1)
                    dve.wait_ge(s["p3"], m - 1)
                nc.vector.tensor_tensor(rest[which], src, parts[z][:, which, :, 0, :], ALU.subtract).then_inc(s["r1"], 1)

            def third_part(which, b, z):
                m = 2 * (2 * b + z) + which
                dve.wait_ge(s["r1"], m + 1)
                dve.wait_ge(s["p2"], m + 1)
                nc.vector.tensor_tensor(parts[z][:, which, :, 2, :], rest[which], parts[z][:, which, :, 1, :],
                                        ALU.subtract).then_inc(s["p3"], 1)

            dve.wait_ge(s["w"], 16 * LOADS)
            chunk_turns(dve, ((1, lambda b, z: remainder(0, b, z)), (0, lambda b, z: third_part(1, b, z)),
                              (2, add_attention), (1, lambda b, z: third_part(0, b, z)), (1, router),
                              (1, lambda b, z: remainder(1, b, z))))
    arena.at = mark



EXPERTS, FF, CAP = 8, 512, B * N // 8


def experts_phase(nc, sem, arena, bank, identf, logits, token, iota8, first_k, ones, xn_dram, w1, b1, w2, b2,
                  slots, answers, xs, fetch, kept):
    C = float(np.sqrt(2.0) / 1.41421)
    TE = TILES * EXPERTS
    mark = arena.at
    zero = arena.f32(8 * D)
    shape = (TILES, EXPERTS)
    top, den, pmax, ipmax, factor = (arena.f32(TILES) for _ in range(5))
    diff, ex, is_top, cand, onehot, counts, before, ranks, picked = (arena.f32(*shape) for _ in range(9))
    scan = [arena.f32(*shape) for _ in range(2)]
    route, pos, keep, target, home, spill = (arena.f32(TILES) for _ in range(6))
    put = arena.take(TILES).bitcast(U32)
    keep_u = arena.take(TILES).bitcast(U32)
    inner = arena.at

    s = {n: sem("x_" + n) for n in "x zero z0 chain count scat t0 t h g y eo ld kept exp b1".split()}
    s_b, s_w, s_v = ([sem(f"x_{name}{i}") for i in range(2)] for name in ("tokens", "hidden", "output"))
    s_e = [sem(f"x_e{i}") for i in range(2)]

    with nc.Block() as block:

        @block.sync
        def _(sp):
            sp.dma_start(xs, xn_dram.rearrange("t p d -> p t d")).then_inc(s["x"], 16)
            sp.wait_ge(s["z0"], 1)
            for i in range(4):
                sp.dma_start(slots[1024 * i:1024 * (i + 1), :].rearrange("(p r) d -> p (r d)", p=P), zero)\
                    .then_inc(s["zero"], 16)
            sp.wait_ge(s["zero"], 64)

        @block.tensor
        def _(pe):
            pe.wait_ge(s["chain"], STEP_ONEHOT)
            flat = onehot.rearrange("p t e -> p (t e)")
            nc.tensor.matmul(bank[0][:, 0:TE], first_k, flat, start=True, stop=True).then_inc(s["count"], 1)
            nc.tensor.matmul(bank[1][:, 0:TE], ones, flat, start=True, stop=True).then_inc(s["count"], 1)

        @block.scalar
        def _(act):
            act.wait_ge(s["chain"], 2)
            nc.scalar.activation(ex, diff, ACT.Exp).then_inc(s["exp"], 1)

        @block.gpsimd
        def _(pool):
            nc.gpsimd.memset(zero, 0.0).then_inc(s["z0"], 1)
            pool.wait_ge(s["x"], 16)
            pool.wait_ge(s["zero"], 64)
            pool.wait_ge(s["ld"], 2)
            for t in range(TILES):
                nc.gpsimd.indirect_dma_start(slots, bass.IndirectOffsetOnAxis(ap=put[:, t:t + 1], axis=0),
                                             xs[:, t, :], None).then_inc(s["scat"], 16)
            pool.wait_ge(s["scat"], 16 * TILES)

        @block.vector
        def _(dve):
            chain = Chain(dve, s["chain"])
            over = lambda a: a.unsqueeze(2).broadcast_to([P, TILES, EXPERTS])
            row = lambda a: a.unsqueeze(1).broadcast_to([P, TILES, EXPERTS])
            v = nc.vector
            chain.step(v.tensor_reduce(top, logits, AX.X, ALU.max))
            chain.step(v.tensor_tensor(diff, logits, over(top), ALU.subtract))
            chain.step(v.tensor_tensor(is_top, logits, over(top), ALU.is_equal))
            chain.step(v.tensor_scalar(cand, is_top, -100.0, 100.0, ALU.mult, ALU.add))
            chain.step(v.tensor_tensor(cand, cand, row(iota8), ALU.add))
            chain.step(v.tensor_reduce(route, cand, AX.X, ALU.min))
            chain.step(v.tensor_tensor(onehot, over(route), row(iota8), ALU.is_equal))
            assert chain.n == STEP_ONEHOT
            dve.wait_ge(s["exp"], 1)
            chain.step(v.tensor_reduce(den, ex, AX.X, ALU.add))
            chain.step(v.reciprocal(pmax, den))
            chain.step(v.reciprocal(ipmax, pmax))
            chain.step(v.tensor_tensor(factor, pmax, ipmax, ALU.mult))
            dve.wait_ge(s["x"], 16)
            v.tensor_tensor(xs, xs, factor.unsqueeze(2).broadcast_to([P, TILES, D]), ALU.mult).then_inc(s["ld"], 1)
            dve.wait_ge(s["count"], 2)
            chain.step(v.tensor_copy(ranks, bank[0][:, 0:TE].rearrange("p (t e) -> p t e", e=EXPERTS)))
            chain.step(v.tensor_copy(counts, bank[1][:, 0:TE].rearrange("p (t e) -> p t e", e=EXPERTS)))
            now, k = counts, 1
            i = 0
            while k < TILES:
                nxt = scan[i % 2]
                chain.step(v.tensor_copy(nxt[:, 0:k, :], now[:, 0:k, :]))
                chain.step(v.tensor_tensor(nxt[:, k:, :], now[:, k:, :], now[:, :TILES - k, :], ALU.add))
                now, k, i = nxt, 2 * k, i + 1
            chain.step(v.tensor_tensor(before, now, counts, ALU.subtract))
            chain.step(v.tensor_tensor(ranks, ranks, before, ALU.add))
            chain.step(v.tensor_tensor(picked, ranks, onehot, ALU.mult))
            chain.step(v.tensor_reduce(pos, picked, AX.X, ALU.add))
            chain.step(v.tensor_scalar(pos, pos, -1.0, None, ALU.add))
            chain.step(v.tensor_scalar(keep, pos, float(CAP), None, ALU.is_lt))
            chain.step(v.tensor_copy(keep_u, keep))
            chain.step(v.scalar_tensor_tensor(home, route, float(CAP), pos, ALU.mult, ALU.add))
            chain.step(v.tensor_scalar(spill, token, float(EXPERTS * CAP), None, ALU.add))
            chain.step(v.tensor_tensor(home, home, spill, ALU.subtract))
            chain.step(v.tensor_tensor(home, home, keep, ALU.mult))
            chain.step(v.tensor_tensor(home, home, spill, ALU.add))
            chain.step(v.tensor_copy(put, home))
            chain.step(v.tensor_scalar(pos, pos, float(CAP - 1), None, ALU.min))
            chain.step(v.scalar_tensor_tensor(target, route, float(CAP), pos, ALU.mult, ALU.add))
            v.tensor_copy(fetch, target).then_inc(s["ld"], 1)
            v.tensor_copy(kept, keep_u.unsqueeze(2).broadcast_to([P, TILES, D])).then_inc(s["kept"], 1)

    assert EXPERTS == CHUNKS and CAP == CW
    RB = FF // P
    arena.at = inner
    w1_sb = [arena.f32(FF) for _ in range(2)]
    w2_sb = [arena.f32(RB, D) for _ in range(2)]
    b1_sb = [arena.f32(RB) for _ in range(2)]
    b1c = [arena.f32(RB) for _ in range(2)]
    b2_sb = [arena.f32(D) for _ in range(2)]
    buf = [arena.f32(CT, D) for _ in range(2)]
    buft = [arena.f32(CW) for _ in range(2)]
    hid = [arena.f32(RB, CW) for _ in range(2)]
    eo = [arena.f32(CT, D) for _ in range(2)]
    with nc.Block() as block:

        @block.sync
        def _(sp):
            def one(t, e):
                return t[bass.ds(e, 1)].rearrange("a p n -> (a p) n")

            def load_tokens(i, z):
                e = 2 * i + z
                if later(i):
                    sp.wait_ge(s["t0"], e - 1)
                sp.dma_start(buf[z], slots[bass.ds(e * CAP, CAP), :].rearrange("(t p) d -> p t d", p=P))\
                    .then_inc(s_b[z], 16)

            def load_hidden(i, z):
                e = 2 * i + z
                if later(i):
                    sp.wait_ge(s["h"], RB * (e - 1))
                    sp.wait_ge(s["b1"], e - 1)
                sp.dma_start(w1_sb[z], one(w1, e)).then_inc(s_w[z], 16)
                sp.dma_start(b1_sb[z], one(b1, e)).then_inc(s_w[z], 16)

            def load_output(i, z):
                e = 2 * i + z
                if later(i):
                    sp.wait_ge(s["eo"], e - 1)
                sp.dma_start(w2_sb[z], one(w2, e).rearrange("p (c d) -> p c d", c=RB)).then_inc(s_v[z], 16)
                sp.dma_start(b2_sb[z], one(b2, e)).then_inc(s_v[z], 16)

            def store(i, z):
                e = 2 * i + z
                sp.wait_ge(s["eo"], e + 1)
                sp.dma_start(answers[bass.ds(e * CAP, CAP), :].rearrange("(t p) d -> p t d", p=P), eo[z])\
                    .then_inc(s_e[z], 16)

            chunk_turns(sp, ((4, load_tokens), (3, load_hidden), (0, store), (2, load_output)))
            for z in range(2):
                sp.wait_ge(s_e[z], 16 * EXPERTS // 2)

        @block.tensor
        def _(pe):
            def turn_tokens(i, z):
                e = 2 * i + z
                pe.wait_ge(s_b[z], 16 * (i + 1))
                pe.wait_ge(s["t"], e)
                for t in range(CT):
                    last = nc.tensor.transpose(bank[0][:, P * t:P * (t + 1)], buf[z][:, t, :], identf)
                last.then_inc(s["t0"], 1)

            def hidden(i, z):
                e = 2 * i + z
                pe.wait_ge(s_w[z], 32 * (i + 1))
                pe.wait_ge(s["t"], e + 1)
                pe.wait_ge(s["g"], RB * e)
                for r in range(RB):
                    nc.tensor.matmul(bank[1 + r], w1_sb[z][:, P * r:P * (r + 1)], buft[z], start=True, stop=True)\
                        .then_inc(s["h"], 1)

            def output(i, z):
                e = 2 * i + z
                pe.wait_ge(s_v[z], 32 * (i + 1))
                pe.wait_ge(s["g"], RB * (e + 1))
                pe.wait_ge(s["eo"], e)
                for t in range(CT):
                    for r in range(RB):
                        last = nc.tensor.matmul(bank[5][:, P * t:P * (t + 1)], hid[z][:, r, P * t:P * (t + 1)],
                                                w2_sb[z][:, r, :], start=(r == 0), stop=(r == RB - 1))
                last.then_inc(s["y"], 1)

            chunk_turns(pe, ((1, hidden), (2, turn_tokens), (0, output)))

        @block.scalar
        def _(act):
            def turned(i, z):
                e = 2 * i + z
                act.wait_ge(s["t0"], e + 1)
                if later(i):
                    act.wait_ge(s["h"], RB * (e - 1))
                nc.scalar.activation(buft[z], bank[0], ACT.Copy).then_inc(s["t"], 1)

            def gelus(i, z):
                e = 2 * i + z
                act.wait_ge(s["b1"], e + 1)
                if later(i):
                    act.wait_ge(s["y"], e - 1)
                for r in range(RB):
                    act.wait_ge(s["h"], RB * e + r + 1)
                    nc.scalar.activation(hid[z][:, r, :], bank[1 + r], ACT.Gelu, bias=b1c[z][:, r:r + 1], scale=C)\
                        .then_inc(s["g"], 1)

            chunk_turns(act, ((1, gelus), (2, turned)))

        @block.vector
        def _(dve):
            def bias(i, z):
                e = 2 * i + z
                dve.wait_ge(s_w[z], 32 * (i + 1))
                if later(i):
                    dve.wait_ge(s["g"], RB * (e - 1))
                nc.vector.tensor_scalar(b1c[z], b1_sb[z], C, None, ALU.mult).then_inc(s["b1"], 1)

            def finish(i, z):
                e = 2 * i + z
                dve.wait_ge(s["y"], e + 1)
                dve.wait_ge(s_e[z], 16 * i)
                nc.vector.scalar_tensor_tensor(eo[z], bank[5].rearrange("p (t d) -> p t d", t=CT), 1.0 / C,
                                               b2_sb[z].unsqueeze(1).broadcast_to([P, CT, D]), ALU.mult, ALU.add)\
                    .then_inc(s["eo"], 1)

            chunk_turns(dve, ((1, bias), (0, finish)))

    arena.at = mark


def gather_answers(nc, pool, answers, fetch, got, s_gather):
    for t in range(TILES):
        nc.gpsimd.indirect_dma_start(got[:, t, :], None, answers,
                                     bass.IndirectOffsetOnAxis(ap=fetch[:, t:t + 1], axis=0)).then_inc(s_gather, 16)
    pool.wait_ge(s_gather, 16 * TILES)


STEP_ONEHOT = 7



def final_phase(nc, sem, arena, bank, identf, O, wo, x1, xs, kept, got, out):
    mark = arena.at
    wo_sb = arena.f32(2, D)
    gate = arena.f32(TILES, D)
    x1s = [arena.f32(CT, D) for _ in range(2)]
    oc = [arena.f32(CT, 2, D) for _ in range(2)]
    ot = [arena.f32(2, CW) for _ in range(2)]
    m = arena.f32(CT, D)
    outs = [arena.f32(CT, D) for _ in range(2)]
    s = {n: sem("z_" + n) for n in "w pick gate oc t ot y m out".split()}
    s_x = [sem(f"z_x{i}") for i in range(2)]
    s_o = [sem(f"z_o{i}") for i in range(2)]

    with nc.Block() as block:

        @block.sync
        def _(sp):
            def load(b, z):
                n = 2 * b + z
                if later(b):
                    sp.wait_ge(s["out"], n - 1)
                sp.dma_start(x1s[z], x1[bass.ds(n * CT, CT), :, :].rearrange("t p d -> p t d")).then_inc(s_x[z], 16)

            def store(b, z):
                sp.wait_ge(s["out"], 2 * b + z + 1)
                sp.dma_start(out[bass.ds(b, 1), CW * z:CW * (z + 1), :].rearrange("a (t p) d -> p (a t) d", p=P),
                             outs[z]).then_inc(s_o[z], 16)

            sp.dma_start(wo_sb, wo.rearrange("(c p) n -> p c n", p=P)).then_inc(s["w"], 16)
            chunk_turns(sp, ((0, store), (2, load)))
            for z in range(2):
                sp.wait_ge(s_o[z], 16 * B)

        @block.gpsimd
        def _(pool):
            flat = O.rearrange("p u t d -> p (u t d)")
            W = 2 * UR

            def collect(b, z):
                if later(b):
                    pool.wait_ge(s["t"], 2 * (2 * b + z - 1))
                for g in range(4):
                    src = flat[:, bass.ds(b * (4 * TB * W) + g * TB * W + z * CT * W, CT * W)]
                    nc.gpsimd.tensor_copy(oc[z].rearrange("p t c d -> p t (c d)")[:, :, W * g:W * (g + 1)],
                                          src.rearrange("p (t d) -> p t d", t=CT)).then_inc(s["oc"], 1)

            chunk_turns(pool, ((3, collect),))

        @block.tensor
        def _(pe):
            def turn_attention(b, z):
                n = 2 * b + z
                pe.wait_ge(s["oc"], 4 * (n + 1))
                for c in range(2):
                    pe.wait_ge(s["ot"], 2 * n)
                    for t in range(CT):
                        last = nc.tensor.transpose(bank[c][:, P * t:P * (t + 1)], oc[z][:, t, c, :], identf)
                    last.then_inc(s["t"], 1)

            def project(b, z):
                n = 2 * b + z
                pe.wait_ge(s["ot"], 2 * n + 2)
                if later(b):
                    pe.wait_ge(s["m"], n - 1)
                for t in range(CT):
                    for c in range(2):
                        last = nc.tensor.matmul(bank[2 + z][:, P * t:P * (t + 1)], ot[z][:, c, P * t:P * (t + 1)],
                                                wo_sb[:, c, :], start=(c == 0), stop=(c == 1))
                last.then_inc(s["y"], 1)

            pe.wait_ge(s["w"], 16)
            chunk_turns(pe, ((2, turn_attention), (1, project)))

        @block.scalar
        def _(act):
            def attention_copy(b, z):
                n = 2 * b + z
                for c in range(2):
                    act.wait_ge(s["t"], 2 * n + c + 1)
                    if later(b):
                        act.wait_ge(s["y"], n - 1)
                    nc.scalar.activation(ot[z][:, c, :], bank[c], ACT.Copy).then_inc(s["ot"], 1)

            act.wait_ge(s["pick"], 1)
            nc.scalar.activation(gate, xs, ACT.Silu).then_inc(s["gate"], 1)
            chunk_turns(act, ((2, attention_copy),))

        @block.vector
        def _(dve):
            flat = gate.rearrange("p t d -> p (t d)")

            def finish(b, z):
                n = 2 * b + z
                dve.wait_ge(s["y"], n + 1)
                dve.wait_ge(s["out"], n)
                nc.vector.tensor_tensor(m.rearrange("p t d -> p (t d)"), bank[2 + z],
                                        flat[:, bass.ds(n * CW, CW)], ALU.mult).then_inc(s["m"], 1)
                dve.wait_ge(s["m"], n + 1)
                dve.wait_ge(s_x[z], 16 * (b + 1))
                dve.wait_ge(s_o[z], 16 * b)
                nc.vector.tensor_tensor(outs[z], m, x1s[z], ALU.add).then_inc(s["out"], 1)

            nc.vector.copy_predicated(xs, kept, got).then_inc(s["pick"], 1)
            dve.wait_ge(s["gate"], 1)
            chunk_turns(dve, ((0, finish),))
    arena.at = mark



ARENA = 49000


def build(nc, t, out, stop=99):
    with ExitStack() as ctx:
        arena = Arena(ctx.enter_context(nc.sbuf_tensor("arena", [P, ARENA], F32)), ARENA)
        bank = Banks(ctx.enter_context(nc.psum_tensor("banks", [P, 8 * CW], F32)))

        def sem(name):
            return ctx.enter_context(nc.semaphore(name))

        def phase(run, *args):
            own = []

            def own_sem(name):
                own.append(nc.alloc_semaphore(name=name))
                return own[-1]

            run(nc, own_sem, arena, bank, *args)
            nc.all_engine_barrier()
            nc.clear_and_free_semaphores(own)
            nc.all_engine_barrier()

        def scratch(name, shape, dt=F32):
            return nc.dram_tensor(name, shape, dt).ap()

        identf, identb = arena.f32(P), arena.bf16(P)
        wide = arena.f32(2 * TILES * D)
        logits = arena.f32(TILES, EXPERTS)

        R = B * (N + 1)
        stream = scratch("stream", (3, R, D))
        mid = scratch("mid", (R, D))
        qk0, v0 = scratch("qk0", (UNITS, 6, UR, N), BF16), scratch("v0", (UNITS, P, TB, P))
        qk1, v1 = scratch("qk1", (UNITS, 6, 2 * UR, N), BF16), scratch("v1", (UNITS, P, TB, P))
        x1, xn1 = scratch("x1", (TILES, P, D)), scratch("xn1", (TILES, P, D))
        slots, answers = scratch("slots", (2 * B * N, D)), scratch("answers", (B * N, D))

        s_start, s_zero, s_rows, s_identb = sem("start"), sem("zero"), sem("zero_rows"), sem("identb")
        zero = arena.f32(D)
        with nc.Block() as block:
            @block.sync
            def _(sp):
                sp.dma_start(identf, t["identf"]).then_inc(s_start, 16)
                sp.wait_ge(s_start, 16)
                sp.wait_ge(s_zero, 1)
                for dst in (mid, stream[1], stream[2]):
                    sp.dma_start(dst[0:3 * (N + 1) + 1:N + 1, :], zero[0:B, :]).then_inc(s_rows, 16)
                sp.wait_ge(s_rows, 48)

            @block.vector
            def _(dve):
                dve.wait_ge(s_start, 16)
                nc.vector.tensor_copy(identb, identf).then_inc(s_identb, 1)
                dve.wait_ge(s_identb, 1)

            @block.gpsimd
            def _(pool):
                nc.gpsimd.memset(zero, 0.0).then_inc(s_zero, 1)

        O0 = wide[:, 0:TILES * D].rearrange("p (u t d) -> p u t d", u=UNITS, t=TB)
        O1 = wide.rearrange("p (u t d) -> p u t d", u=UNITS, t=TB)
        phase(enter_phase, identf, t["L0_attn_x"], [t[n] for n in ("wq", "wk", "wqs", "wks", "wv")],
                    (t["rope_cos"], t["rope_sin"]), stream[0], qk0, v0)
        if stop > 1:
            phase(attention_phase, identb, identf, "A", 4, 8, qk0, v0, O0)
        if stop > 2:
            with nc.Fori(0, 2) as layer:
                phase(local_attention, identf, identb, layer, stream, mid, t["wqkv"], t["qk_scales"], t["wo"],
                                t["xpos"], t["masks"])
                phase(feed_forward, identf, layer, mid, stream, t["ln_gb"], t["w1"], t["b1"], t["w2"],
                             t["b2"])
        if stop > 3:
            phase(middle_phase, identf, O0, t["w_out"], t["b_out"], t["L0_attn_x"], stream, t["l1_wq"],
                         t["l1_wkd"], t["l1_wku"], t["l1_wvu"], t["l1_wsw"], t["l1_bsw"], x1, xn1, qk1, v1, logits)
        if stop > 4:
            iota8, token = arena.f32(EXPERTS), arena.f32(TILES)
            first_k, ones = arena.f32(P), arena.f32(P)
            xn1_sb, got = arena.f32(TILES, D), arena.f32(TILES, D)
            kept = arena.take(TILES * D).bitcast(U32).rearrange("p (t d) -> p t d", d=D)
            fetch = arena.take(TILES).bitcast(U32)
            s_cst, s_gather = sem("consts"), sem("gather")
            with nc.Block() as block:
                @block.sync
                def _(sp):
                    for dst, name in ((iota8, "iota8"), (token, "token"), (first_k, "first_k"), (ones, "ones")):
                        sp.dma_start(dst, t[name]).then_inc(s_cst, 16)
                    sp.wait_ge(s_cst, 64)
            phase(experts_phase, identf, logits, token, iota8, first_k, ones, xn1, t["l1_w1"],
                          t["l1_b1"], t["l1_w2"], t["l1_b2"], slots, answers, xn1_sb, fetch, kept)
        if stop > 5:
            phase(attention_phase, identb, identf, "B", 2, 32, qk1, v1, O1,
                  lambda pool: gather_answers(nc, pool, answers, fetch, got, s_gather))
            phase(final_phase, identf, O1, t["l1_wo"], x1, xn1_sb, kept, got, out)



def layouts(a):
    import numpy as _np
    c = _np.ascontiguousarray
    rep = lambda v: c(_np.broadcast_to(v, (P,) + v.shape))
    w = a["L0_attn_w_qkv"]
    half = (_np.arange(D) // 8) * 8 + (_np.arange(D) % 8 + 4) % 8
    t = {"L0_attn_x": a["L0_attn_x"]}
    t["wq"], t["wk"], t["wv"] = c(w[0:D].T), c(w[D:2 * D].T), c(w[2 * D:].T)
    t["wqs"], t["wks"] = c(w[0:D][half].T), c(w[D:2 * D][half].T)
    t["w_out"], t["b_out"] = c(a["L0_attn_w_out"].T), rep(a["L0_attn_b_out"])
    t["wqkv"], t["wo"], t["w1"] = a["L0_ffn_wqkv"], a["L0_ffn_wo"], a["L0_ffn_w1"]
    t["w2"] = a["L0_ffn_w2"]
    b1 = _np.zeros((2, 2, BLOCKS * HB), _np.float32)
    b1[:, :, :HID] = a["L0_ffn_b1"].reshape(2, 2, HID)
    t["b1"] = c(b1.reshape(2, 2, BLOCKS, HB).transpose(0, 3, 1, 2))
    t["b2"] = c(_np.broadcast_to(a["L0_ffn_b2"][:, None, :], (2, P, D)))
    t["ln_gb"] = c(_np.stack([a["L0_ffn_ln_g"], a["L0_ffn_ln_b"]], axis=-1))
    qk = _np.stack([a["L0_ffn_q_scale"], a["L0_ffn_k_scale"]], axis=1)
    swapped = _np.concatenate([qk[..., DH // 2:], qk[..., :DH // 2]], axis=-1)
    t["qk_scales"] = c(_np.broadcast_to(_np.stack([qk, swapped], axis=1)[:, None], (2, P, 2, 2, DH)))
    t["l1_wq"], t["l1_wkd"] = c(a["L1_attn_Wq"].T), c(a["L1_attn_Wkv_down"].T)
    t["l1_wku"], t["l1_wvu"] = c(a["L1_attn_Wk_up"].T), c(a["L1_attn_Wv_up"].T)
    t["l1_wo"] = c(a["L1_attn_Wo"].T)
    t["l1_wsw"], t["l1_bsw"] = a["L1_ffn_W_sw"], rep(a["L1_ffn_b_sw"])
    t["l1_w1"] = a["L1_ffn_W1"]
    t["l1_b1"] = c(a["L1_ffn_b1"].reshape(EXPERTS, FF // P, P).transpose(0, 2, 1))
    t["l1_w2"] = c(a["L1_ffn_W2"].reshape(EXPERTS, FF // P, P, D).transpose(0, 2, 1, 3).reshape(EXPERTS, P, -1))
    t["l1_b2"] = c(_np.broadcast_to(a["L1_ffn_b2"][:, None, :], (EXPERTS, P, D)))
    return t


def tables():
    import numpy as _np
    f = _np.float32
    c = _np.ascontiguousarray
    t = {}
    inv = f(1.0) / f(10000.0) ** (_np.arange(0, 8, 2, dtype=f) / f(8))
    ang = _np.arange(N, dtype=f)[:, None] * inv[None, :]
    cos, sin = _np.cos(ang).T, _np.sin(ang).T
    t["rope_cos"] = c(_np.tile(_np.concatenate([cos, cos]), (16, 1)).astype(f))
    t["rope_sin"] = c(_np.tile(_np.concatenate([-sin, sin]), (16, 1)).astype(f))
    idx = _np.arange(0, DH, 2, dtype=f)
    inv = f(1.0) / f(10000.0) ** (idx / f(DH))
    pos = _np.arange(N, dtype=f)
    ang = pos[:, None] * inv[None, :]
    base = (idx + f(0.4 * DH)) / f(1.4 * DH)
    scale = base[None, :] ** ((pos - f(N // 2)) / f(WINDOW // 2))[:, None]
    cos, sin = _np.cos(ang), _np.sin(ang)
    both = []
    for q in (True, False):
        m = scale if q else f(1.0) / scale
        both.append((_np.concatenate([cos * m, cos * m], -1), _np.concatenate([-sin * m, sin * m], -1)))
    xpos = _np.stack([_np.stack([b[x] for b in both], 1) for x in range(2)])
    t["xpos"] = c(xpos.reshape(2, TB, P, 2, DH).transpose(2, 0, 1, 3, 4).astype(f))
    k, p = _np.arange(SPAN)[None, :], _np.arange(P)[:, None]
    seen = (k >= p) & (k <= p + WINDOW)
    inside = _np.where(seen, f(0), f(NEG))
    first = _np.where(seen & (k >= WINDOW), f(0), f(NEG))
    t["masks"] = c(_np.stack([_np.tile(first, 2), _np.tile(inside, 2)], 1).astype(f))
    t["identf"] = _np.eye(P, dtype=f)
    t["iota8"] = c(_np.tile(_np.arange(EXPERTS, dtype=f), (P, 1)))
    t["token"] = c((_np.arange(TILES)[None, :] * P + _np.arange(P)[:, None]).astype(f))
    t["first_k"] = _np.triu(_np.ones((P, P), f))
    t["ones"] = _np.ones((P, P), f)
    return t


def kernel(**inputs):
    import numpy as _np
    import concourse.bacc as _bacc
    from concourse import mybir as _mybir
    from concourse.bass_utils import run_bass_kernel_spmd as _run

    nc = _bacc.Bacc("TRN2", target_bir_lowering=False, num_devices=1)
    arrays, aps = {}, {}
    for name, a in {**layouts({k: _np.asarray(v) for k, v in inputs.items()}), **tables()}.items():
        a = _np.ascontiguousarray(a)
        arrays[f"in_{name}"] = a
        aps[name] = nc.dram_tensor(f"in_{name}", a.shape, _mybir.dt.from_np(a.dtype), kind="ExternalInput").ap()
    out = nc.dram_tensor("out_0_dram", (B, N, D), _mybir.dt.float32, kind="ExternalOutput").ap()
    build(nc, aps, out)
    r = _run(nc, [arrays], core_ids=[0])
    return r.results[0]["out_0_dram"]
```
